# Optimizing a Trainium2 kernel written in Bass

```python
import numpy as np
import jax
import jax.numpy as jnp

def _softmax(x, axis=-1):
    return jax.nn.softmax(x, axis=axis)

def _gelu(x):
    return jax.nn.gelu(x, approximate=True)

def _silu(x):
    return jax.nn.silu(x)

def _sigmoid(x):
    return jax.nn.sigmoid(x)

def _layernorm(x, axis=-1, eps=1e-05):
    m = jnp.mean(x, axis=axis, keepdims=True)
    v = jnp.var(x, axis=axis, keepdims=True)
    return (x - m) / jnp.sqrt(v + eps)

def _scatter_add(tgt, idx, src, axis=0):
    return tgt.at[idx].add(src)

def _segment_sum(src, seg, n):
    return jax.ops.segment_sum(src, seg, n)
kernel_name = 'mk_flamingo_gated_d4_seqx_r8_97fbf6'

def setup_inputs(seed: int=0):
    np.random.seed(seed)
    _w = jnp.asarray

    def _rec_inputs():
        import jax
        import jax.numpy as jnp
        _rk = jax.random.key(seed)
        x = -0.0002928 + 1 * jax.random.normal(jax.random.fold_in(_rk, 1), (2, 512, 128), jnp.float32)
        _lenS = 512 - jax.random.randint(jax.random.fold_in(_rk, 7), (2,), 0, max(1, 512 // 4) + 1, jnp.int32)
        _lenS2 = 77 - jax.random.randint(jax.random.fold_in(_rk, 8), (2,), 0, max(1, 77 // 4) + 1, jnp.int32)
        _ctx_1024P = jax.random.normal(jax.random.fold_in(_rk, 11), (2, 16, 128), jnp.float32)
        _ctx_1024c = jax.random.dirichlet(jax.random.fold_in(_rk, 511), 0.3 * jnp.ones((16,), jnp.float32), (2, 77))
        _ctx_1024t = jnp.einsum('bsk,bkd->bsd', _ctx_1024c, _ctx_1024P)
        _ctx_1024t = _ctx_1024t * jax.lax.rsqrt(jnp.mean(jnp.square(_ctx_1024t)) + 1e-12) * 0.953939
        ctx_1024 = -1.39393e-06 + 0.999914 * (_ctx_1024t + 0.3 * jax.random.normal(jax.random.fold_in(_rk, 611), (2, 77, 128), jnp.float32))
        _validS = jnp.arange(512)[None, :] < _lenS[:, None]
        _validS2 = jnp.arange(77)[None, :] < _lenS2[:, None]
        _causal = jnp.tril(jnp.ones((512, 512), dtype=bool))
        mask_1x1xSxS2_bk1 = jnp.broadcast_to(_validS2[0:1, None, None, :], (1, 1, 512, 77))
        mask_BxSx1_ik1 = jnp.where(jnp.ones((2, 512, 1), dtype=bool), 1, 0).astype(jnp.int32)
        _g = jax.random.normal(jax.random.fold_in(_rk, 9001), (2, 4), jnp.float32)
        _g = jnp.sign(_g) * jnp.maximum(jnp.abs(_g), 1.0) + (_g == 0) * 1.0
        g_xattn = _g[0]
        g_ffn = _g[1]
        return (x, ctx_1024, mask_1x1xSxS2_bk1, mask_BxSx1_ik1, g_xattn, g_ffn)
    x, ctx_1024, mask_1x1xSxS2_bk1, mask_BxSx1_ik1, g_xattn, g_ffn = _rec_inputs()

    def _L0_xattn_setup():
        import jax, jax.numpy as jnp
        import numpy as np
        import math
        DIM = 128
        H = 16
        HD = DIM // H // 2
        DEPTH = 4
        LAMBDA_INIT = 0.8 - 0.6 * math.exp(-0.3 * DEPTH)
        SCALE = HD ** (-0.5)
        EPS = 1e-05

        def _sdpa(q, k, v):
            scores = jnp.einsum('bhqd,bhkd->bhqk', q * SCALE, k)
            p = jax.nn.softmax(scores, axis=-1)
            return jnp.einsum('bhqk,bhkd->bhqd', p, v)
        key = jax.random.key(seed)
        ks = jax.random.split(key, 12)
        B, Nq, Nk = (2, 256, 256)
        s = DIM ** (-0.5)
        return {'query': jax.random.normal(ks[0], (B, Nq, DIM), jnp.float32), 'key_': jax.random.normal(ks[1], (B, Nk, DIM), jnp.float32), 'value': jax.random.normal(ks[2], (B, Nk, DIM), jnp.float32), 'Wq': jax.random.normal(ks[3], (DIM, DIM), jnp.float32) * s, 'Wk': jax.random.normal(ks[4], (DIM, DIM), jnp.float32) * s, 'Wv': jax.random.normal(ks[5], (DIM, DIM), jnp.float32) * s, 'Wp': jax.random.normal(ks[6], (DIM, DIM), jnp.float32) * s, 'bp': jnp.zeros((DIM,), jnp.float32), 'lq1': jax.random.normal(ks[7], (HD,), jnp.float32) * 0.1, 'lk1': jax.random.normal(ks[8], (HD,), jnp.float32) * 0.1, 'lq2': jax.random.normal(ks[9], (HD,), jnp.float32) * 0.1, 'lk2': jax.random.normal(ks[10], (HD,), jnp.float32) * 0.1, 'subln_w': jnp.ones((2 * HD,), jnp.float32)}
    _L0_xattn_all = _L0_xattn_setup()
    _L0_xattn_in = {k: v for k, v in _L0_xattn_all.items() if k in ('Wq', 'Wk', 'Wv', 'Wp', 'bp', 'lq1', 'lk1', 'lq2', 'lk2', 'subln_w')}
    del _L0_xattn_all

    def _L0_ffn_setup():
        import jax, jax.numpy as jnp
        import numpy as np
        NUM_EXPERTS = 8
        CAPACITY_FACTOR = 1.0
        key = jax.random.key(seed)
        k1, k2, k3, k4 = jax.random.split(key, 4)
        B, S, D, E, F = (8, 256, 128, NUM_EXPERTS, 512)
        x = jax.random.normal(k1, (B, S, D), dtype=jnp.float32)
        router_w = jax.random.normal(k2, (D, E), dtype=jnp.float32) * D ** (-0.5)
        w1 = jax.random.normal(k3, (E, D, F), dtype=jnp.float32) * D ** (-0.5)
        w2 = jax.random.normal(k4, (E, F, D), dtype=jnp.float32) * F ** (-0.5)
        return {'x': x, 'router_w': router_w, 'w1': w1, 'w2': w2}
    _L0_ffn_all = _L0_ffn_setup()
    _L0_ffn_in = {k: v for k, v in _L0_ffn_all.items() if k in ('router_w', 'w1', 'w2')}
    del _L0_ffn_all

    def _L1_xattn_setup():
        import jax, jax.numpy as jnp
        import numpy as np
        B, T, E, H = (4, 1024, 128, 16)
        D = E // H
        SCALE = 1.0 / np.sqrt(D).astype(np.float32)
        EPS_FM = 1e-06
        EPS_Z = 1e-08

        def _heads(x):
            b, t, _ = x.shape
            return x.reshape(b, t, H, D).transpose(0, 2, 1, 3)

        def _feature_map(x):
            return jax.nn.relu(x) + EPS_FM
        key = jax.random.key(seed)
        ks = jax.random.split(key, 11)
        s = 1.0 / np.sqrt(E).astype(np.float32)
        return {'query': jax.random.normal(ks[0], (B, T, E), jnp.float32), 'key': jax.random.normal(ks[1], (B, T, E), jnp.float32), 'value': jax.random.normal(ks[2], (B, T, E), jnp.float32), 'Wq': jax.random.normal(ks[3], (E, E), jnp.float32) * s, 'bq': jax.random.normal(ks[4], (E,), jnp.float32) * 0.01, 'Wk': jax.random.normal(ks[5], (E, E), jnp.float32) * s, 'bk': jax.random.normal(ks[6], (E,), jnp.float32) * 0.01, 'Wv': jax.random.normal(ks[7], (E, E), jnp.float32) * s, 'bv': jax.random.normal(ks[8], (E,), jnp.float32) * 0.01, 'Wo': jax.random.normal(ks[9], (E, E), jnp.float32) * s, 'bo': jax.random.normal(ks[10], (E,), jnp.float32) * 0.01}
    _L1_xattn_all = _L1_xattn_setup()
    _L1_xattn_in = {k: v for k, v in _L1_xattn_all.items() if k in ('Wq', 'bq', 'Wk', 'bk', 'Wv', 'bv', 'Wo', 'bo')}
    del _L1_xattn_all

    def _L1_ffn_setup():
        import jax, jax.numpy as jnp
        import numpy as np
        DIM = 128

        def _reference_tuple_inner(x, W_r, W_k, W_v, mu_r, mu_k):
            B, T, C = x.shape
            x_prev = jnp.concatenate([jnp.zeros((B, 1, C), x.dtype), x[:, :-1, :]], axis=1)
            xr = mu_r * x + (1.0 - mu_r) * x_prev
            xk = mu_k * x + (1.0 - mu_k) * x_prev
            r = jax.nn.sigmoid(jnp.einsum('btc,dc->btd', xr, W_r))
            k = jnp.einsum('btc,dc->btd', xk, W_k)
            k_act = jnp.square(jax.nn.relu(k))
            out = r * jnp.einsum('btc,dc->btd', k_act, W_v)
            new_state = x[:, -1, :]
            return (out, new_state)
        key = jax.random.key(seed)
        ks = jax.random.split(key, 6)
        B, T, C = (8, 256, DIM)
        x = jax.random.normal(ks[0], (B, T, C), dtype=jnp.float32)
        s = 1.0 / np.sqrt(C)
        W_r = jax.random.uniform(ks[1], (C, C), jnp.float32, -s, s)
        W_k = jax.random.uniform(ks[2], (C, C), jnp.float32, -s, s)
        W_v = jax.random.uniform(ks[3], (C, C), jnp.float32, -s, s)
        mu_r = jax.random.uniform(ks[4], (C,), jnp.float32)
        mu_k = jax.random.uniform(ks[5], (C,), jnp.float32)
        return {'x': x, 'W_r': W_r, 'W_k': W_k, 'W_v': W_v, 'mu_r': mu_r, 'mu_k': mu_k}
    _L1_ffn_all = _L1_ffn_setup()
    _L1_ffn_in = {k: v for k, v in _L1_ffn_all.items() if k in ('W_r', 'W_k', 'W_v', 'mu_r', 'mu_k')}
    del _L1_ffn_all

    def _L2_xattn_setup():
        import jax, jax.numpy as jnp
        import numpy as np
        B, S, D, H = (2, 256, 128, 16)
        DH = D // H

        def _split(x):
            return x.reshape(x.shape[0], -1, H, DH).transpose(0, 2, 1, 3)
        key = jax.random.key(seed)
        ks = jax.random.split(key, 12)
        s = 1.0 / np.sqrt(D)
        inp = {'q': jax.random.normal(ks[0], (B, S, D), jnp.float32), 'k': jax.random.normal(ks[1], (B, S, D), jnp.float32), 'v': jax.random.normal(ks[2], (B, S, D), jnp.float32), 'mask': jnp.triu(jnp.ones((S, S), dtype=bool), k=1)[None, None], 'Wq': jax.random.normal(ks[3], (D, D), jnp.float32) * s, 'bq': jax.random.normal(ks[4], (D,), jnp.float32) * s, 'Wk': jax.random.normal(ks[5], (D, D), jnp.float32) * s, 'bk': jax.random.normal(ks[6], (D,), jnp.float32) * s, 'Wv': jax.random.normal(ks[7], (D, D), jnp.float32) * s, 'bv': jax.random.normal(ks[8], (D,), jnp.float32) * s, 'Wo': jax.random.normal(ks[9], (D, D), jnp.float32) * s, 'bo': jax.random.normal(ks[10], (D,), jnp.float32) * s}
        return inp
    _L2_xattn_all = _L2_xattn_setup()
    _L2_xattn_in = {k: v for k, v in _L2_xattn_all.items() if k in ('Wq', 'bq', 'Wk', 'bk', 'Wv', 'bv', 'Wo', 'bo')}
    del _L2_xattn_all

    def _L2_ffn_setup():
        import jax, jax.numpy as jnp
        import numpy as np
        D_MODEL = 128
        H_SHARED = 256
        H_ROUTED = 128
        N_EXPERTS = 8
        TOP_K = 2
        key = jax.random.key(seed)
        ks = jax.random.split(key, 8)
        B, T = (2, 256)
        sc_d = 1.0 / np.sqrt(D_MODEL)
        sc_hs = 1.0 / np.sqrt(H_SHARED)
        sc_hr = 1.0 / np.sqrt(H_ROUTED)
        return {'x': jax.random.normal(ks[0], (B, T, D_MODEL), dtype=jnp.float32), 'router_w': jax.random.normal(ks[1], (N_EXPERTS, D_MODEL), dtype=jnp.float32) * sc_d, 'router_bias': jnp.zeros((N_EXPERTS,), dtype=jnp.float32), 'sw1': jax.random.normal(ks[2], (D_MODEL, H_SHARED), dtype=jnp.float32) * sc_d, 'sw3': jax.random.normal(ks[3], (D_MODEL, H_SHARED), dtype=jnp.float32) * sc_d, 'sw2': jax.random.normal(ks[4], (H_SHARED, D_MODEL), dtype=jnp.float32) * sc_hs, 'ew1': jax.random.normal(ks[5], (N_EXPERTS, D_MODEL, H_ROUTED), dtype=jnp.float32) * sc_d, 'ew2': jax.random.normal(ks[6], (N_EXPERTS, H_ROUTED, D_MODEL), dtype=jnp.float32) * sc_hr}
    _L2_ffn_all = _L2_ffn_setup()
    _L2_ffn_in = {k: v for k, v in _L2_ffn_all.items() if k in ('router_w', 'router_bias', 'sw1', 'sw3', 'sw2', 'ew1', 'ew2')}
    del _L2_ffn_all

    def _L3_xattn_setup():
        import jax, jax.numpy as jnp
        import numpy as np
        DIM = 128
        H = 8
        HD = DIM // H
        SCALE = DIM ** (-0.5)
        key = jax.random.key(seed)
        ks = jax.random.split(key, 12)
        B, T, S = (8, 256, 64)
        x = jax.random.normal(ks[0], (B, T, DIM), jnp.float32)
        keys = jax.random.normal(ks[1], (B, S, DIM), jnp.float32)
        values = jax.random.normal(ks[2], (B, S, DIM), jnp.float32)
        mask_t = jax.random.randint(ks[3], (B, T, 1), 0, 2).astype(jnp.int32)
        w = DIM ** (-0.5)
        Wq = jax.random.normal(ks[4], (DIM, DIM), jnp.float32) * w
        bq = jax.random.normal(ks[5], (DIM,), jnp.float32) * 0.01
        Wk = jax.random.normal(ks[6], (DIM, DIM), jnp.float32) * w
        bk = jax.random.normal(ks[7], (DIM,), jnp.float32) * 0.01
        Wv = jax.random.normal(ks[8], (DIM, DIM), jnp.float32) * w
        bv = jax.random.normal(ks[9], (DIM,), jnp.float32) * 0.01
        Wo = jax.random.normal(ks[10], (DIM, DIM), jnp.float32) * w
        bo = jax.random.normal(ks[11], (DIM,), jnp.float32) * 0.01
        return {'x': x, 'keys': keys, 'values': values, 'mask_t': mask_t, 'Wq': Wq, 'bq': bq, 'Wk': Wk, 'bk': bk, 'Wv': Wv, 'bv': bv, 'Wo': Wo, 'bo': bo}
    _L3_xattn_all = _L3_xattn_setup()
    _L3_xattn_in = {k: v for k, v in _L3_xattn_all.items() if k in ('Wq', 'bq', 'Wk', 'bk', 'Wv', 'bv', 'Wo', 'bo')}
    del _L3_xattn_all

    def _L3_ffn_setup():
        import jax, jax.numpy as jnp
        import numpy as np
        H, HP, NH_M, NH_D = (128, 64, 8, 8)
        B, T = (2, 256)
        SPARSITY = 8
        N_ROT = 32
        BASE = 10000.0

        def _rope(x, pos, n_rot, base):
            half = n_rot // 2
            inv = base ** (-jnp.arange(half, dtype=x.dtype) / half)
            ang = pos[..., None] * inv
            cos, sin = (jnp.cos(ang), jnp.sin(ang))
            x1, x2 = (x[..., :half], x[..., half:n_rot])
            rot = jnp.concatenate([x1 * cos - x2 * sin, x1 * sin + x2 * cos], axis=-1)
            return jnp.concatenate([rot, x[..., n_rot:]], axis=-1)

        def _mosa_branch(X, router_w, wqkv, wo):
            b, t, _ = X.shape
            k = t // SPARSITY
            scores = jnp.einsum('bth,hn->bnt', X, router_w)
            _, idx = jax.lax.top_k(scores, k)
            idx = jnp.sort(idx, axis=-1)
            gates = jax.nn.sigmoid(jnp.take_along_axis(scores, idx, axis=-1))
            Xg = jnp.take_along_axis(X[:, None], idx[..., None], axis=2)
            qkv = jnp.einsum('bnkh,hnd->bnkd', Xg, wqkv)
            Q, K, V = jnp.split(qkv, 3, axis=-1)
            pos = idx.astype(X.dtype)
            Q = _rope(Q, pos, N_ROT, BASE)
            K = _rope(K, pos, N_ROT, BASE)
            att = jnp.einsum('bnqd,bnkd->bnqk', Q, K) / jnp.sqrt(jnp.asarray(HP, X.dtype))
            causal = idx[..., :, None] >= idx[..., None, :]
            att = jnp.where(causal, att, -jnp.inf)
            AV = jnp.einsum('bnqk,bnkd->bnqd', jax.nn.softmax(att, axis=-1), V)
            AV = AV * gates[..., None]
            out = jnp.zeros((b, NH_M, t, HP), X.dtype)
            bi = jnp.arange(b)[:, None, None]
            hi = jnp.arange(NH_M)[None, :, None]
            out = out.at[bi, hi, idx].set(AV)
            out = out.transpose(0, 2, 1, 3).reshape(b, t, NH_M * HP)
            return out @ wo

        def _dense_branch(X, wqkv, wo):
            b, t, _ = X.shape
            qkv = jnp.einsum('bth,hnd->bntd', X, wqkv)
            Q, K, V = jnp.split(qkv, 3, axis=-1)
            pos = jnp.arange(t, dtype=X.dtype)
            Q = _rope(Q, pos, N_ROT, BASE)
            K = _rope(K, pos, N_ROT, BASE)
            att = jnp.einsum('bnqd,bnkd->bnqk', Q, K) / jnp.sqrt(jnp.asarray(HP, X.dtype))
            causal = jnp.tril(jnp.ones((t, t), bool))
            att = jnp.where(causal, att, -jnp.inf)
            AV = jnp.einsum('bnqk,bnkd->bnqd', jax.nn.softmax(att, axis=-1), V)
            return AV.transpose(0, 2, 1, 3).reshape(b, t, NH_D * HP) @ wo
        key = jax.random.key(seed)
        ks = jax.random.split(key, 6)
        s = 0.02
        return {'X': jax.random.normal(ks[0], (B, T, H), jnp.float32), 'mosa_router_w': jax.random.normal(ks[1], (H, NH_M), jnp.float32) * s, 'mosa_wqkv': jax.random.normal(ks[2], (H, NH_M, 3 * HP), jnp.float32) * s, 'mosa_wo': jax.random.normal(ks[3], (NH_M * HP, H), jnp.float32) * s, 'dense_wqkv': jax.random.normal(ks[4], (H, NH_D, 3 * HP), jnp.float32) * s, 'dense_wo': jax.random.normal(ks[5], (NH_D * HP, H), jnp.float32) * s}
    _L3_ffn_all = _L3_ffn_setup()
    _L3_ffn_in = {k: v for k, v in _L3_ffn_all.items() if k in ('mosa_router_w', 'mosa_wqkv', 'mosa_wo', 'dense_wqkv', 'dense_wo')}
    del _L3_ffn_all
    return {'x': x, 'ctx_1024': ctx_1024, 'mask_1x1xSxS2_bk1': mask_1x1xSxS2_bk1, 'mask_BxSx1_ik1': mask_BxSx1_ik1, 'g_xattn': g_xattn, 'g_ffn': g_ffn, 'L0_xattn_Wq': _L0_xattn_in['Wq'], 'L0_xattn_Wk': _L0_xattn_in['Wk'], 'L0_xattn_Wv': _L0_xattn_in['Wv'], 'L0_xattn_Wp': _L0_xattn_in['Wp'], 'L0_xattn_bp': _L0_xattn_in['bp'], 'L0_xattn_lq1': _L0_xattn_in['lq1'], 'L0_xattn_lk1': _L0_xattn_in['lk1'], 'L0_xattn_lq2': _L0_xattn_in['lq2'], 'L0_xattn_lk2': _L0_xattn_in['lk2'], 'L0_xattn_subln_w': _L0_xattn_in['subln_w'], 'L0_ffn_router_w': _L0_ffn_in['router_w'], 'L0_ffn_w1': _L0_ffn_in['w1'], 'L0_ffn_w2': _L0_ffn_in['w2'], 'L1_xattn_Wq': _L1_xattn_in['Wq'], 'L1_xattn_bq': _L1_xattn_in['bq'], 'L1_xattn_Wk': _L1_xattn_in['Wk'], 'L1_xattn_bk': _L1_xattn_in['bk'], 'L1_xattn_Wv': _L1_xattn_in['Wv'], 'L1_xattn_bv': _L1_xattn_in['bv'], 'L1_xattn_Wo': _L1_xattn_in['Wo'], 'L1_xattn_bo': _L1_xattn_in['bo'], 'L1_ffn_W_r': _L1_ffn_in['W_r'], 'L1_ffn_W_k': _L1_ffn_in['W_k'], 'L1_ffn_W_v': _L1_ffn_in['W_v'], 'L1_ffn_mu_r': _L1_ffn_in['mu_r'], 'L1_ffn_mu_k': _L1_ffn_in['mu_k'], 'L2_xattn_Wq': _L2_xattn_in['Wq'], 'L2_xattn_bq': _L2_xattn_in['bq'], 'L2_xattn_Wk': _L2_xattn_in['Wk'], 'L2_xattn_bk': _L2_xattn_in['bk'], 'L2_xattn_Wv': _L2_xattn_in['Wv'], 'L2_xattn_bv': _L2_xattn_in['bv'], 'L2_xattn_Wo': _L2_xattn_in['Wo'], 'L2_xattn_bo': _L2_xattn_in['bo'], 'L2_ffn_router_w': _L2_ffn_in['router_w'], 'L2_ffn_router_bias': _L2_ffn_in['router_bias'], 'L2_ffn_sw1': _L2_ffn_in['sw1'], 'L2_ffn_sw3': _L2_ffn_in['sw3'], 'L2_ffn_sw2': _L2_ffn_in['sw2'], 'L2_ffn_ew1': _L2_ffn_in['ew1'], 'L2_ffn_ew2': _L2_ffn_in['ew2'], 'L3_xattn_Wq': _L3_xattn_in['Wq'], 'L3_xattn_bq': _L3_xattn_in['bq'], 'L3_xattn_Wk': _L3_xattn_in['Wk'], 'L3_xattn_bk': _L3_xattn_in['bk'], 'L3_xattn_Wv': _L3_xattn_in['Wv'], 'L3_xattn_bv': _L3_xattn_in['bv'], 'L3_xattn_Wo': _L3_xattn_in['Wo'], 'L3_xattn_bo': _L3_xattn_in['bo'], 'L3_ffn_mosa_router_w': _L3_ffn_in['mosa_router_w'], 'L3_ffn_mosa_wqkv': _L3_ffn_in['mosa_wqkv'], 'L3_ffn_mosa_wo': _L3_ffn_in['mosa_wo'], 'L3_ffn_dense_wqkv': _L3_ffn_in['dense_wqkv'], 'L3_ffn_dense_wo': _L3_ffn_in['dense_wo']}

def reference(x, ctx_1024, mask_1x1xSxS2_bk1, mask_BxSx1_ik1, g_xattn, g_ffn, L0_xattn_Wq, L0_xattn_Wk, L0_xattn_Wv, L0_xattn_Wp, L0_xattn_bp, L0_xattn_lq1, L0_xattn_lk1, L0_xattn_lq2, L0_xattn_lk2, L0_xattn_subln_w, L0_ffn_router_w, L0_ffn_w1, L0_ffn_w2, L1_xattn_Wq, L1_xattn_bq, L1_xattn_Wk, L1_xattn_bk, L1_xattn_Wv, L1_xattn_bv, L1_xattn_Wo, L1_xattn_bo, L1_ffn_W_r, L1_ffn_W_k, L1_ffn_W_v, L1_ffn_mu_r, L1_ffn_mu_k, L2_xattn_Wq, L2_xattn_bq, L2_xattn_Wk, L2_xattn_bk, L2_xattn_Wv, L2_xattn_bv, L2_xattn_Wo, L2_xattn_bo, L2_ffn_router_w, L2_ffn_router_bias, L2_ffn_sw1, L2_ffn_sw3, L2_ffn_sw2, L2_ffn_ew1, L2_ffn_ew2, L3_xattn_Wq, L3_xattn_bq, L3_xattn_Wk, L3_xattn_bk, L3_xattn_Wv, L3_xattn_bv, L3_xattn_Wo, L3_xattn_bo, L3_ffn_mosa_router_w, L3_ffn_mosa_wqkv, L3_ffn_mosa_wo, L3_ffn_dense_wqkv, L3_ffn_dense_wo):
    import jax
    import jax.numpy as jnp

    def _L0_xattn_ref(query, key_, value, Wq, Wk, Wv, Wp, bp, lq1, lk1, lq2, lk2, subln_w):
        import jax, jax.numpy as jnp
        import numpy as np
        import math
        DIM = 128
        H = 16
        HD = DIM // H // 2
        DEPTH = 4
        LAMBDA_INIT = 0.8 - 0.6 * math.exp(-0.3 * DEPTH)
        SCALE = HD ** (-0.5)
        EPS = 1e-05

        def _sdpa(q, k, v):
            scores = jnp.einsum('bhqd,bhkd->bhqk', q * SCALE, k)
            p = jax.nn.softmax(scores, axis=-1)
            return jnp.einsum('bhqk,bhkd->bhqd', p, v)
        B, Nq, C = query.shape
        Nk = key_.shape[1]
        q = (query @ Wq.T).reshape(B, Nq, 2 * H, HD).transpose(0, 2, 1, 3)
        k = (key_ @ Wk.T).reshape(B, Nk, 2 * H, HD).transpose(0, 2, 1, 3)
        v = (value @ Wv.T).reshape(B, Nk, H, 2 * HD).transpose(0, 2, 1, 3)
        q1, q2 = (q[:, :H], q[:, H:])
        k1, k2 = (k[:, :H], k[:, H:])
        a1 = _sdpa(q1, k1, v)
        a2 = _sdpa(q2, k2, v)
        lam1 = jnp.exp(jnp.sum(lq1 * lk1))
        lam2 = jnp.exp(jnp.sum(lq2 * lk2))
        lam = lam1 - lam2 + LAMBDA_INIT
        attn = a1 - lam * a2
        attn = attn.transpose(0, 2, 1, 3)
        attn = attn * jax.lax.rsqrt(jnp.mean(attn * attn, axis=-1, keepdims=True) + EPS)
        attn = attn * subln_w
        attn = attn * (1.0 - LAMBDA_INIT)
        attn = attn.reshape(B, Nq, C)
        return attn @ Wp.T + bp

    def _L0_ffn_ref(x, router_w, w1, w2):
        import jax, jax.numpy as jnp
        import numpy as np
        NUM_EXPERTS = 8
        CAPACITY_FACTOR = 1.0
        B, S, D = x.shape
        E = router_w.shape[1]
        T = B * S
        C = int(CAPACITY_FACTOR * T / E)
        x_flat = x.reshape(T, D)
        logits = x_flat @ router_w
        probs = jax.nn.softmax(logits, axis=-1)
        expert_idx = jnp.argmax(probs, axis=-1)
        gate = jnp.take_along_axis(probs, expert_idx[:, None], axis=1)[:, 0]
        onehot = jax.nn.one_hot(expert_idx, E, dtype=jnp.float32)
        pos_all = jnp.cumsum(onehot, axis=0) - 1.0
        pos = jnp.take_along_axis(pos_all, expert_idx[:, None], axis=1)[:, 0]
        pos = pos.astype(jnp.int32)
        keep = (pos < C).astype(x_flat.dtype)
        pos_c = jnp.clip(pos, 0, C - 1)
        expert_in = jnp.zeros((E, C, D), dtype=x_flat.dtype)
        expert_in = expert_in.at[expert_idx, pos_c].add(x_flat * keep[:, None])
        hidden = jax.nn.gelu(jnp.einsum('ecd,edf->ecf', expert_in, w1))
        expert_out = jnp.einsum('ecf,efd->ecd', hidden, w2)
        y = expert_out[expert_idx, pos_c] * (gate * keep)[:, None]
        return y.reshape(B, S, D)

    def _L1_xattn_ref(query, key, value, Wq, bq, Wk, bk, Wv, bv, Wo, bo):
        import jax, jax.numpy as jnp
        import numpy as np
        B, T, E, H = (4, 1024, 128, 16)
        D = E // H
        SCALE = 1.0 / np.sqrt(D).astype(np.float32)
        EPS_FM = 1e-06
        EPS_Z = 1e-08

        def _heads(x):
            b, t, _ = x.shape
            return x.reshape(b, t, H, D).transpose(0, 2, 1, 3)

        def _feature_map(x):
            return jax.nn.relu(x) + EPS_FM
        b, tq, _ = query.shape
        Q = _feature_map(_heads(query @ Wq.T + bq) * SCALE)
        K = _feature_map(_heads(key @ Wk.T + bk) * SCALE)
        V = _heads(value @ Wv.T + bv)
        KV = jnp.einsum('bhnd,bhne->bhde', K, V)
        K_sum = K.sum(axis=2)
        Z = jnp.einsum('bhnd,bhd->bhn', Q, K_sum) + EPS_Z
        out = jnp.einsum('bhnd,bhde->bhne', Q, KV) / Z[..., None]
        out = out.transpose(0, 2, 1, 3).reshape(b, tq, E)
        return out @ Wo.T + bo

    def _L1_ffn_ref(x, W_r, W_k, W_v, mu_r, mu_k):
        import jax, jax.numpy as jnp
        import numpy as np
        DIM = 128

        def _reference_tuple_inner(x, W_r, W_k, W_v, mu_r, mu_k):
            B, T, C = x.shape
            x_prev = jnp.concatenate([jnp.zeros((B, 1, C), x.dtype), x[:, :-1, :]], axis=1)
            xr = mu_r * x + (1.0 - mu_r) * x_prev
            xk = mu_k * x + (1.0 - mu_k) * x_prev
            r = jax.nn.sigmoid(jnp.einsum('btc,dc->btd', xr, W_r))
            k = jnp.einsum('btc,dc->btd', xk, W_k)
            k_act = jnp.square(jax.nn.relu(k))
            out = r * jnp.einsum('btc,dc->btd', k_act, W_v)
            new_state = x[:, -1, :]
            return (out, new_state)
        return _reference_tuple_inner(x, W_r, W_k, W_v, mu_r, mu_k)[0]

    def _L2_xattn_ref(q, k, v, mask, Wq, bq, Wk, bk, Wv, bv, Wo, bo):
        import jax, jax.numpy as jnp
        import numpy as np
        B, S, D, H = (2, 256, 128, 16)
        DH = D // H

        def _split(x):
            return x.reshape(x.shape[0], -1, H, DH).transpose(0, 2, 1, 3)
        qh = _split(q @ Wq.T + bq)
        kh = _split(k @ Wk.T + bk)
        vh = _split(v @ Wv.T + bv)
        scores = jnp.einsum('bhqd,bhkd->bhqk', qh, kh) / jnp.sqrt(jnp.float32(DH))
        scores = jnp.where(mask, -jnp.inf, scores)
        attn = jax.nn.softmax(scores, axis=-1)
        out = jnp.einsum('bhqk,bhkd->bhqd', attn, vh)
        out = out.transpose(0, 2, 1, 3).reshape(q.shape[0], -1, H * DH)
        return out @ Wo.T + bo

    def _L2_ffn_ref(x, router_w, router_bias, sw1, sw3, sw2, ew1, ew2):
        import jax, jax.numpy as jnp
        import numpy as np
        D_MODEL = 128
        H_SHARED = 256
        H_ROUTED = 128
        N_EXPERTS = 8
        TOP_K = 2
        B, T, C = x.shape
        xf = x.reshape(-1, C)
        shared_out = jax.nn.silu(xf @ sw1) * (xf @ sw3) @ sw2
        s = jax.nn.sigmoid((xf @ router_w.T).astype(jnp.float32))
        sel_scores = s + router_bias.astype(jnp.float32)
        _, topk_idx = jax.lax.top_k(sel_scores, TOP_K)
        s_sel = jnp.take_along_axis(s, topk_idx, axis=1)
        denom = s_sel.sum(axis=1, keepdims=True)
        gates = jnp.where(denom > 1e-09, s_sel / (denom + 1e-09), 1.0 / TOP_K).astype(x.dtype)
        one_hot = jax.nn.one_hot(topk_idx, N_EXPERTS, dtype=x.dtype)
        comb = jnp.einsum('nke,nk->ne', one_hot, gates)
        h = jax.nn.gelu(jnp.einsum('nd,edh->neh', xf, ew1), approximate=False)
        y = jnp.einsum('neh,ehd->ned', h, ew2)
        routed_out = jnp.einsum('ned,ne->nd', y, comb)
        return (shared_out + routed_out).reshape(B, T, C)

    def _L3_xattn_ref(x, keys, values, mask_t, Wq, bq, Wk, bk, Wv, bv, Wo, bo):
        import jax, jax.numpy as jnp
        import numpy as np
        DIM = 128
        H = 8
        HD = DIM // H
        SCALE = DIM ** (-0.5)
        B, T, _ = x.shape
        S = keys.shape[1]
        q = (x @ Wq.T + bq).reshape(B, T, H, HD)
        k = jnp.tanh(keys @ Wk.T + bk).reshape(B, S, H, HD)
        v = (values @ Wv.T + bv).reshape(B, S, H, HD)
        scores = jnp.einsum('bthd,bshd->bhts', q, k) * SCALE
        attn = jax.nn.softmax(scores, axis=-1)
        keep = (mask_t != 0)[:, None, :, :]
        attn = jnp.where(keep, attn, 0.0)
        out = jnp.einsum('bhts,bshd->bthd', attn, v).reshape(B, T, DIM)
        out = out @ Wo.T + bo
        out = out * mask_t.astype(out.dtype)
        return out

    def _L3_ffn_ref(X, mosa_router_w, mosa_wqkv, mosa_wo, dense_wqkv, dense_wo):
        import jax, jax.numpy as jnp
        import numpy as np
        H, HP, NH_M, NH_D = (128, 64, 8, 8)
        B, T = (2, 256)
        SPARSITY = 8
        N_ROT = 32
        BASE = 10000.0

        def _rope(x, pos, n_rot, base):
            half = n_rot // 2
            inv = base ** (-jnp.arange(half, dtype=x.dtype) / half)
            ang = pos[..., None] * inv
            cos, sin = (jnp.cos(ang), jnp.sin(ang))
            x1, x2 = (x[..., :half], x[..., half:n_rot])
            rot = jnp.concatenate([x1 * cos - x2 * sin, x1 * sin + x2 * cos], axis=-1)
            return jnp.concatenate([rot, x[..., n_rot:]], axis=-1)

        def _mosa_branch(X, router_w, wqkv, wo):
            b, t, _ = X.shape
            k = t // SPARSITY
            scores = jnp.einsum('bth,hn->bnt', X, router_w)
            _, idx = jax.lax.top_k(scores, k)
            idx = jnp.sort(idx, axis=-1)
            gates = jax.nn.sigmoid(jnp.take_along_axis(scores, idx, axis=-1))
            Xg = jnp.take_along_axis(X[:, None], idx[..., None], axis=2)
            qkv = jnp.einsum('bnkh,hnd->bnkd', Xg, wqkv)
            Q, K, V = jnp.split(qkv, 3, axis=-1)
            pos = idx.astype(X.dtype)
            Q = _rope(Q, pos, N_ROT, BASE)
            K = _rope(K, pos, N_ROT, BASE)
            att = jnp.einsum('bnqd,bnkd->bnqk', Q, K) / jnp.sqrt(jnp.asarray(HP, X.dtype))
            causal = idx[..., :, None] >= idx[..., None, :]
            att = jnp.where(causal, att, -jnp.inf)
            AV = jnp.einsum('bnqk,bnkd->bnqd', jax.nn.softmax(att, axis=-1), V)
            AV = AV * gates[..., None]
            out = jnp.zeros((b, NH_M, t, HP), X.dtype)
            bi = jnp.arange(b)[:, None, None]
            hi = jnp.arange(NH_M)[None, :, None]
            out = out.at[bi, hi, idx].set(AV)
            out = out.transpose(0, 2, 1, 3).reshape(b, t, NH_M * HP)
            return out @ wo

        def _dense_branch(X, wqkv, wo):
            b, t, _ = X.shape
            qkv = jnp.einsum('bth,hnd->bntd', X, wqkv)
            Q, K, V = jnp.split(qkv, 3, axis=-1)
            pos = jnp.arange(t, dtype=X.dtype)
            Q = _rope(Q, pos, N_ROT, BASE)
            K = _rope(K, pos, N_ROT, BASE)
            att = jnp.einsum('bnqd,bnkd->bnqk', Q, K) / jnp.sqrt(jnp.asarray(HP, X.dtype))
            causal = jnp.tril(jnp.ones((t, t), bool))
            att = jnp.where(causal, att, -jnp.inf)
            AV = jnp.einsum('bnqk,bnkd->bnqd', jax.nn.softmax(att, axis=-1), V)
            return AV.transpose(0, 2, 1, 3).reshape(b, t, NH_D * HP) @ wo
        return _mosa_branch(X, mosa_router_w, mosa_wqkv, mosa_wo) + _dense_branch(X, dense_wqkv, dense_wo)
    x = x + jnp.tanh(g_xattn[0]) * _L0_xattn_ref(_layernorm(x, axis=-1), ctx_1024, ctx_1024, L0_xattn_Wq, L0_xattn_Wk, L0_xattn_Wv, L0_xattn_Wp, L0_xattn_bp, L0_xattn_lq1, L0_xattn_lk1, L0_xattn_lq2, L0_xattn_lk2, L0_xattn_subln_w)
    x = x + jnp.tanh(g_ffn[0]) * _L0_ffn_ref(_layernorm(x, axis=-1), L0_ffn_router_w, L0_ffn_w1, L0_ffn_w2)
    x = x + jnp.tanh(g_xattn[1]) * _L1_xattn_ref(_layernorm(x, axis=-1), ctx_1024, ctx_1024, L1_xattn_Wq, L1_xattn_bq, L1_xattn_Wk, L1_xattn_bk, L1_xattn_Wv, L1_xattn_bv, L1_xattn_Wo, L1_xattn_bo)
    x = x + jnp.tanh(g_ffn[1]) * _L1_ffn_ref(_layernorm(x, axis=-1), L1_ffn_W_r, L1_ffn_W_k, L1_ffn_W_v, L1_ffn_mu_r, L1_ffn_mu_k)
    x = x + jnp.tanh(g_xattn[2]) * _L2_xattn_ref(_layernorm(x, axis=-1), ctx_1024, ctx_1024, mask_1x1xSxS2_bk1, L2_xattn_Wq, L2_xattn_bq, L2_xattn_Wk, L2_xattn_bk, L2_xattn_Wv, L2_xattn_bv, L2_xattn_Wo, L2_xattn_bo)
    x = x + jnp.tanh(g_ffn[2]) * _L2_ffn_ref(_layernorm(x, axis=-1), L2_ffn_router_w, L2_ffn_router_bias, L2_ffn_sw1, L2_ffn_sw3, L2_ffn_sw2, L2_ffn_ew1, L2_ffn_ew2)
    x = x + jnp.tanh(g_xattn[3]) * _L3_xattn_ref(_layernorm(x, axis=-1), ctx_1024, ctx_1024, mask_BxSx1_ik1, L3_xattn_Wq, L3_xattn_bq, L3_xattn_Wk, L3_xattn_bk, L3_xattn_Wv, L3_xattn_bv, L3_xattn_Wo, L3_xattn_bo)
    x = x + jnp.tanh(g_ffn[3]) * _L3_ffn_ref(_layernorm(x, axis=-1), L3_ffn_mosa_router_w, L3_ffn_mosa_wqkv, L3_ffn_mosa_wo, L3_ffn_dense_wqkv, L3_ffn_dense_wo)
    return x

_drawn_inputs = setup_inputs


def setup_inputs(seed=0):
    import zlib

    import numpy as np

    out = dict(_drawn_inputs(seed))
    spreads = {'L0_xattn_bp': (0.0, 0.1),
     'L0_xattn_subln_w': (1.0, 0.2),
     'L2_ffn_router_bias': (0.0, 0.1)}
    factors = {'g_ffn': 48.632,
     'L0_xattn_lq2': 3.651,
     'L0_xattn_lk2': 3.651,
     'L1_xattn_bq': 7.729,
     'L1_xattn_bk': 8.0,
     'L1_xattn_bv': 3.537,
     'L1_xattn_bo': 2.977,
     'L1_ffn_mu_r': 4.204,
     'L2_xattn_bk': 200.0,
     'L3_xattn_bq': 64.0,
     'L3_xattn_bk': 64.0,
     'L3_xattn_bv': 8.0,
     'L3_xattn_bo': 8.0,
     'L3_ffn_mosa_router_w': 7.599,
     'L3_ffn_mosa_wqkv': 7.147,
     'L3_ffn_mosa_wo': 7.434}
    for name, (base, spread) in spreads.items():
        noise = np.random.default_rng([zlib.crc32(name.encode()), seed]).standard_normal(out[name].shape)
        drawn = base * np.exp(spread * noise) if base else spread * noise
        out[name] = jnp.asarray(drawn.astype(out[name].dtype))
    for name, factor in factors.items():
        out[name] = (out[name] * factor).astype(out[name].dtype)
    return out
```

```python
from contextlib import ExitStack

import numpy as np
import concourse.bass as bass
from concourse import mybir

F32 = mybir.dt.float32
I32 = mybir.dt.int32
U8 = mybir.dt.uint8
ALU = mybir.AluOpType
ACT = mybir.ActivationFunctionType
AX = mybir.AxisListType

D = 128
B = 2
T = 512
N = B * T
NT = N // 128
TB = T // 128
SK = 77
E = 8
CAP = N // E
F = 512
EPS = 1e-5
BIG = 3.0e38
NEG = -1.0e30
LAMBDA_INIT = 0.8 - 0.6 * float(np.exp(-0.3 * 4))

ATTN = [dict(layer=0, nsub=4, nh=8, qd=32, mrow=32, scale=0.5),
        dict(layer=2, nsub=2, nh=8, qd=64, mrow=64, scale=8 ** -0.5),
        dict(layer=3, nsub=2, nh=4, qd=64, mrow=64, scale=128 ** -0.5)]
for _c in ATTN:
    _c["rows"] = _c["nh"] * SK
    _c["chunks"] = [(c, min(128, _c["rows"] - c)) for c in range(0, _c["rows"], 128)]

NHD = 8
HP = 64
ROT = 32
SEL = T // 8


def signals(c):
    units = B * c["nsub"]
    parts = units * len(c["chunks"])
    first = B if c["layer"] == 0 else 0
    return dict(q_zeroed=1, keys=1, k_placed=1, values=B, v_placed=B, query=B if c["layer"] == 0 else units, q_placed=units,
                k_built=units, scores=units * TB, max_taken=units * TB, max_rows=units, max_placed=units,
                shifted=parts, probs=parts, weighed=parts, p_masked=parts if c["layer"] == 2 else 0, o_taken=units,
                dens=B, recs=B, rec_bcast=B * c["nsub"] // 2, normed=first, att_raw=first, att_sq=first, rms_ms=first, rms_eps=first, rms_r=first,
                rms_wide=first, rms_bcast=first, att_done=B, projected=B, y_placed=B)


POOL_SET = dict(ones=11, iota=12, keep=14, mask3=15, last=22)


def before(a, name):
    return sum(signals(c)[name] for c in ATTN[:a])


def columns(*widths):
    at, out = 0, {}
    for name, w in widths:
        out[name] = (at, at + w)
        at += w
    out["_"] = at
    return out


CONST = columns(("ident", 128), ("center", 128), ("tri", 128), ("ones", 128), ("mean", 1),
                ("head8", 16), ("head8mean", 16), ("block8", 128), ("firstw", 64), ("slot0", 64),
                ("slotid", 8), ("vmask8", 320), ("vmask16", 192), ("vone8", 40), ("vone16", 12),
                ("kmask4", 8), ("kmask8", 8), ("kmask16", 4))
CONST3 = columns(("causal", 128), ("ropec", 512), ("ropes", 512), ("tab", 256), ("iota64", 64))
COLS = columns(("g", 8), ("lq1", 4), ("lk1", 4), ("lq2", 4), ("lk2", 4), ("subln", 1), ("bp", 1),
               ("bo1", 1), ("bo2", 1), ("bo3", 1), ("bq1", 1), ("mur", 1), ("muk", 1),
               ("bq2", 2), ("bk2", 2), ("bq3", 2), ("bk3", 2), ("rbias", 64))
ROWS = columns(("bk1", 128), ("bv1", 128), ("bv2", 128), ("bv3", 128))


def constants():
    c = np.zeros((128, CONST["_"]), np.float32)
    p = np.arange(128)

    def put(name, a):
        lo, hi = CONST[name]
        c[:a.shape[0], lo:hi] = a.reshape(a.shape[0], -1)

    put("ident", np.eye(128))
    put("center", np.eye(128) - 1.0 / D)
    put("tri", p[:, None] <= p[None, :])
    put("ones", np.ones((128, 128)))
    put("mean", np.full((128, 1), 1.0 / D))
    put("head8", p[:, None] // 8 == np.arange(16))
    put("head8mean", (p[:, None] // 8 == np.arange(16)) / 8.0)
    put("block8", p[:, None] // 8 == p[None, :] // 8)
    put("firstw", np.tile(8.0 - np.arange(8), (128, 8)))
    put("slot0", np.tile(CAP * np.arange(8.0), (128, 8)))
    put("slotid", p[:, None] + CAP * np.arange(8.0))
    r8 = p[:, None] + 128 * np.arange(5)
    r16 = p[:, None] + 128 * np.arange(3)
    f = np.arange(64)
    put("vmask8", r8[:, :, None] // SK == f // 8)
    put("vmask16", r16[:, :, None] // SK == f // 16)
    put("vone8", r8[:, :, None] // SK == np.arange(8))
    put("vone16", r16[:, :, None] // SK == np.arange(4))
    put("kmask4", np.arange(32)[:, None] // 4 == np.arange(8))
    put("kmask8", f[:, None] // 8 == np.arange(8))
    put("kmask16", f[:, None] // 16 == np.arange(4))

    d = np.zeros((128, CONST3["_"]), np.float32)

    def put3(name, a):
        lo, hi = CONST3[name]
        d[:a.shape[0], lo:hi] = a.reshape(a.shape[0], -1)

    put3("causal", np.where(p[None, :] > p[:, None], NEG, 0.0))
    half = ROT // 2
    inv = (10000.0 ** (-np.arange(half, dtype=np.float32) / half)).astype(np.float32)
    ang = (np.arange(T, dtype=np.float32)[:, None] * inv).astype(np.float32)
    cos, sin = np.cos(ang), np.sin(ang)
    cos2 = np.concatenate([cos, cos], 1)
    sin2 = np.concatenate([-sin, sin], 1)
    put3("ropec", cos2.T)
    put3("ropes", sin2.T)
    put3("tab", np.concatenate([cos2, sin2], 1).reshape(TB, 128, 64).transpose(1, 0, 2))
    put3("iota64", np.tile(np.arange(64.0), (128, 1)))

    def minus(nh, copies):
        m = np.zeros((nh, copies, nh, SK), np.float32)
        for h in range(nh):
            m[h, :, h] = -1.0
        return m.reshape(nh, -1)

    return {"const": c, "const3": d,
            "minus0": minus(8, 8), "minus1": minus(8, 4), "minus2": minus(4, 4)}


def build(nc, A, out):
    with ExitStack() as ctx:
        sems = {}

        def S(name):
            if name not in sems:
                sems[name] = ctx.enter_context(nc.semaphore(name))
            return sems[name]

        def sb(name, shape, dt=F32):
            return ctx.enter_context(nc.sbuf_tensor(name, shape, dt))

        PS = ctx.enter_context(nc.psum_tensor("PS", [128, 8, 512], F32))

        cst = sb("cst", [128, CONST["_"]])
        cst3 = sb("cst3", [128, CONST3["_"]])
        cols = sb("cols", [128, COLS["_"]])
        rows = sb("rows", [1, ROWS["_"]])
        x = sb("x", [128, N])
        ctxr = sb("ctxr", [128, B, 8 * SK])
        wa0 = sb("wa0", [128, 4, 128])
        wa1 = sb("wa1", [128, 4, 128])
        wa2 = sb("wa2", [128, 4, 128])
        wa3 = sb("wa3", [128, 4, 128])
        wf1 = sb("wf1", [128, 3, 128])
        rw0 = sb("rw0", [128, 24])
        wmoe = sb("wmoe", [128, 2 * E * F])
        w1 = wmoe[:, 0:E * F].rearrange("p (e f) -> p e f", e=E)
        w2 = wmoe[:, E * F:2 * E * F].rearrange("p (e c d) -> p e c d", e=E, c=4)
        sw13 = sb("sw13", [128, 2, 256])
        sw2 = sb("sw2", [128, 2, 128])
        wlate = sb("wlate", [128, 3 * 512 + 512])
        ew1 = wlate[:, 0:1024].rearrange("p (e f) -> p e f", e=E)
        ew2 = wlate[:, 1024:2048].rearrange("p (e f) -> p e f", e=E)
        wd = sb("wd", [128, 3 * 512 + 512])
        wm = wlate
        wod = sb("wod", [128, 4, 128])
        wom = sb("wom", [64, 8, 128])
        maskr = sb("maskr", [128, 5, 512], U8)
        maskq = sb("maskq", [128, TB, SK], U8)
        mask3f = sb("mask3", [128, N])
        mask3 = mask3f[:].bitcast(I32)

        def C(name, p=128):
            lo, hi = CONST[name]
            return cst[0:p, lo:hi]

        def C3(name, p0=0, p=128):
            lo, hi = CONST3[name]
            return cst3[p0:p, lo:hi]

        def V(name, p=128, j=None):
            lo, hi = COLS[name]
            return cols[0:p, lo:hi] if j is None else cols[0:p, lo + j:lo + j + 1]

        def R(name):
            lo, hi = ROWS[name]
            return rows[0:1, lo:hi]

        ident = C("ident")

        sq = sb("sq", [128, B, T])
        xc = sb("xc", [128, B, T])
        veps = sb("veps", [128, B, TB])
        rstd = sb("rstd", [128, B, TB])
        mhalf = sb("mhalf", [128, 64])
        hp = sb("hp", [128, B, T + 1])
        h = [hp[:, b, 1:T + 1] for b in range(B)]
        tg = sb("tg", [128, 8])
        small = sb("small", [128, 16])
        kT = sb("kT", [64, 4, B * SK])
        keys = sb("keys", [128, 8 * 8 * SK])
        half_ = 4 * 8 * SK
        KA = [keys[:, :].rearrange("p (b s k) -> p b s k", b=B, s=4),
              keys[:, 0:half_].rearrange("p (b s k) -> p b s k", b=B, s=2),
              keys[:, half_:half_ + 4 * 4 * SK].rearrange("p (b s k) -> p b s k", b=B, s=2)]
        VD = keys[:, 0:B * TB * NHD * 65].rearrange("p (n h d) -> p n h d", n=NT, h=NHD)
        va8 = sb("va8", [128, B, 2, 5, 72])
        VA = [va8, va8, sb("va16", [128, B, 2, 3, 68])]
        PTB = sb("PTB", [128, 8, T])
        QA = PTB[:].rearrange("p (b s) t -> p b s t", b=B)
        mx = sb("mx", [128, B, 4, TB, 8])
        PT = sb("PT", [128, 4, T])
        OT = sb("OT", [128, B, 2, T])
        G = OT[:].rearrange("p b z t -> p b (z t)")
        qf = OT[:, 0]
        den4 = sb("den4", [32, 4, T])
        den = den4[0:8]
        rec = sb("rec", [128, B, TB, 32])
        att = sb("att", [128, B, T])
        rms = sb("rms", [128, B, 64])
        rmsr = sb("rmsr", [128, B, TB, 16])
        yb = sb("yb", [128, B, T])
        keep = wmoe[:, E * F:E * F + 5 * T].rearrange("p (c t) -> p c t", c=5)
        mbias = sb("mbias", [128, TB, SK])
        sm = wmoe[:, 0:4 * 308].rearrange("p (n k) -> p n k", n=2)
        pool_iota = sb("pool_iota", [128, 1024])
        htok = sb("htok", [128, NT, 128])
        r8t = sb("r8t", [128, 10, 8])
        ein = PT[:, 2:4].rearrange("p a t -> p (a t)")
        hid = PT[:, 0:2]
        eo = sb("eo", [128, 2, 128])
        destb = sq[:].rearrange("p b t -> p (b t)")
        gateb = xc[:].rearrange("p b t -> p (b t)")
        kf = sb("kf", [SK, B, 128])
        vs = sb("vs", [SK, B, 128])
        kvm = sb("kvm", [128, B, 128])
        ksh = sb("ksh", [128, B, 16])
        combT = pool_iota
        rt = sb("rt", [128, 10, 64])
        QK = [wmoe[:, 0:4 * T].rearrange("p (j t) -> p j t", j=4),
              wmoe[:, 4 * T:8 * T].rearrange("p (j t) -> p j t", j=4), PTB[:, 4:8]]
        AVT = wmoe[:, 8 * T:16 * T].rearrange("p (b n t) -> p b n t", b=B, n=4)
        GT = [[sq[:, 0, :], sq[:, 1, :], xc[:, 0, :], xc[:, 1, :]], [PT[:, q, :] for q in range(4)]]
        xg = att[:, 0, :]
        sqk = OT[0:64, 0]
        spv = OT[0:64, 1]
        spp = att[0:64, 1, :]
        spo = yb[0:64, 0, :]
        sdiff = yb[0:64, 1, :]
        sps = sb("sps", [64, 4, 8])
        trig = den4
        spz = rt[:, 0:8, :].rearrange("p (q a) c -> p q (a c)", q=4)
        mxd = sb("mxd", [128, 2, TB])
        recd = sb("recd", [128, B, TB, NHD])
        denr = pool_iota[0:1, :].rearrange("p (r t) -> p r t", r=2)
        wk = yb[0:40, 0, :]
        wide = pool_iota[:, :].rearrange("p (r t) -> p r t", r=2)
        m8 = sb("m8", [40, 8])
        selT = sb("selT", [128, 3, 64])

        block = ctx.enter_context(nc.Block())

        loads = [[("xT", x[:]), ("const", cst[:])],
                 [("wa0", wa0[:]), ("ctx", ctxr[:]), ("cols", cols[:]), ("minus0", keys[32:40, :])],
                 [("rw0", rw0[:]), ("w1", wmoe[:, 0:E * F]), ("w2", wmoe[:, E * F:2 * E * F])],
                 [("rows", rows[:]), ("wa1", wa1[:]), ("wf1", wf1[:])],
                 [("wa2", wa2[:]), ("minus1", keys[64:72, 0:half_]), ("maskr", maskr[:]), ("maskq", maskq[:]),
                  ("mask3", mask3)],
                 [("sw13", sw13[:]), ("sw2", sw2[:]), ("ew1", wlate[:, 0:1024]), ("ew2", wlate[:, 1024:2048])],
                 [("wa3", wa3[:]), ("minus2", keys[64:68, half_:half_ + 16 * SK])],
                 [("const3", cst3[:]), ("wd", wd[:]), ("wod", wod[:]), ("wom", wom[:])],
                 [("wm", wm[:])]]
        lot = {name: n for n, group in enumerate(loads) for name, _ in group}

        @block.sync
        def _(sp):
            for n, group in enumerate(loads):
                if n == lot["wm"]:
                    sp.wait_ge(S("x_ready"), 2 * 6)
                if n == lot["minus1"]:
                    sp.wait_ge(S("x_ready"), 2)
                for name, dst in group:
                    if name == "minus0":
                        sp.wait_ge(S("pool_set"), 1)
                    shape, src = dst.shape, A[name]
                    if len(shape) == 3:
                        src = src.rearrange("p (a b) -> p a b", a=shape[1])
                    elif len(shape) == 4:
                        src = src.rearrange("p (a b c) -> p a b c", a=shape[1], b=shape[2])
                    sp.dma_start(dst, src).then_inc(S(f"loaded_{n}"), 16)
            for b in range(B):
                sp.wait_ge(S("x_ready"), 2 * 8 + b + 1 - 2)
                sp.dma_start(out[:, b * T:(b + 1) * T], x[:, b * T:(b + 1) * T]).then_inc(S("stored"), 16)
            sp.wait_ge(S("stored"), 16 * B)

        def arrived(eng, *names):
            for n in sorted({lot[name] for name in names}):
                eng.wait_ge(S(f"loaded_{n}"), 16 * len(loads[n]))

        class Chain:

            def __init__(self, eng, name):
                self.eng, self.name, self.n = eng, name, 0

            def __call__(self, ins):
                self.n += 1
                ins.then_inc(S(self.name), 1)
                self.eng.wait_ge(S(self.name), self.n)

        xb = [x[:, b * T:(b + 1) * T] for b in range(B)]

        @block.tensor
        def _(pe):
            def mm(o, l, r, start=True, stop=True):
                return nc.tensor.matmul(o, l, r, start=start, stop=stop, skip_group_check=True)

            def layernorm(i):
                for b in range(B):
                    k = 2 * i + b + 1
                    if i == 0:
                        if b == 0:
                            arrived(pe, "xT", "const")
                    else:
                        pe.wait_ge(S("x_ready"), k - 2)
                    mm(PS[:, 2 * b, :], C("center"), xb[b]).then_inc(S("ln_centered"), 1)
                for b in range(B):
                    k = 2 * i + b + 1
                    pe.wait_ge(S("ln_act"), 2 * k - 1)
                    for t in range(TB):
                        last = mm(PS[:, 2 * b + 1, t:t + 1], sq[:, b, t * 128:(t + 1) * 128], C("mean"))
                    last.then_inc(S("ln_var"), 1)
                for b in range(B):
                    k = 2 * i + b + 1
                    pe.wait_ge(S("ln_rstd"), k)
                    for t in range(TB):
                        last = nc.tensor.transpose(PS[:, 2 * b + 1, t * 128:(t + 1) * 128],
                                                   rstd[:, b, t:t + 1].to_broadcast([128, 128]), ident)
                    last.then_inc(S("ln_bcast"), 1)

            def attention(a, i, w, kbias):
                c = ATTN[a]
                nsub, nh, qd, mr = c["nsub"], c["nh"], c["qd"], c["mrow"]
                chunks = c["chunks"]
                s_ = lambda n: S("at_" + n)
                arrived(pe, *(["ctx", "wa0"] if a == 0 else [f"wa{c['layer']}"]))
                for s in range(nsub):
                    last = mm(PS[0:qd, 4 + s // 2, (s % 2) * 154:(s % 2) * 154 + 154], w[:, 1, s * qd:(s + 1) * qd],
                              ctxr[:, :, 0:SK])
                last.then_inc(s_("keys"), 1)
                for b in range(B):
                    if b == 1:
                        pe.wait_ge(s_("v_placed"), before(a, "v_placed") + 1)
                    for j, (c0, m) in enumerate(chunks):
                        o = PS[0:m, 6 + j // 4, (j % 4) * 128:(j % 4) * 128 + 128]
                        last = mm(o, ctxr[:, b, c0:c0 + m], w[:, 2, :], stop=not kbias)
                        if kbias:
                            last = mm(o, C("ones", 1)[:, 0:m], R(kbias), start=False)
                    last.then_inc(s_("values"), 1)
                layernorm(i)
                pe.wait_ge(s_("k_placed"), before(a, "k_placed") + 1)
                for b in range(B):
                    pe.wait_ge(S("ln_h"), 2 * i + b + 1)
                    if a == 0:
                        mm(PS[:, 4 + b, :], w[:, 0, :], h[b]).then_inc(s_("query"), 1)
                    else:
                        if b == 1:
                            pe.wait_ge(s_("v_placed"), before(a, "v_placed") + 2)
                        for s in range(nsub):
                            mm(PS[0:qd, 4 + 2 * b + s, :], w[:, 0, s * qd:(s + 1) * qd], h[b]).then_inc(s_("query"), 1)
                units = [(b, s) for b in range(B) for s in range(nsub)]
                arrived(pe, f"minus{a}")
                pe.wait_ge(S("pool_set"), POOL_SET["ones"])
                pe.wait_ge(s_("q_zeroed"), before(a, "q_zeroed") + 1)

                def scores(u):
                    b, s = units[u]
                    if s == 0:
                        pe.wait_ge(s_("k_built"), before(a, "k_built") + nsub * (b + 1))
                        pe.wait_ge(s_("q_placed"), before(a, "q_placed") + nsub * (b + 1))
                    for t in range(TB):
                        n = TB * u + t
                        if n >= 2:
                            pe.wait_ge(s_("max_taken"), before(a, "max_taken") + n - 1)
                        for j in range(c["rows"] // 308):
                            last = mm(PS[:, 2 * (n % 2) + j, 0:308], QA[:, b, s, t * 128:(t + 1) * 128],
                                      KA[a][:, b, s, j * 308:(j + 1) * 308])
                        last.then_inc(s_("scores"), 1)

                def maxima(u):
                    b, s = units[u]
                    pe.wait_ge(s_("max_taken"), before(a, "max_taken") + TB * (u + 1))
                    if u == 0:
                        pe.wait_ge(s_("q_placed"), before(a, "q_placed") + nsub * B)
                    for name, n in cleared(u):
                        pe.wait_ge(s_(name), before(a, name) + n)
                    for t in range(TB):
                        last = nc.tensor.transpose(PS[0:nh, 7, t * 128:(t + 1) * 128], mx[:, b, s, t, 0:nh], ident)
                    last.then_inc(s_("max_rows"), 1)

                def cleared(u):
                    if u in (0, 1) or u <= nsub:
                        return []
                    return {(0, 5): [("recs", 1)], (0, 6): [("rms_eps", 1)], (0, 7): [("y_placed", 1)],
                            (1, 3): [("recs", 1)], (2, 3): [("recs", 1)]}[a, u]

                def weigh(u):
                    b, s = units[u]
                    nc_ = len(chunks)
                    pe.wait_ge(s_("max_placed"), before(a, "max_placed") + u + 1)

                    def pv(j):
                        g = u * nc_ + j
                        m = chunks[j][1]
                        pe.wait_ge(s_("p_masked" if a == 1 else "probs"), before(a, "p_masked" if a == 1 else "probs") + g + 1)
                        if j == 0 and u > 0:
                            pe.wait_ge(s_("o_taken"), before(a, "o_taken") + u)
                        last = mm(PS[0:64 + nh, 6, :], VA[a][0:m, b, s % 2, j, :], PT[0:m, g % 4, :],
                                  start=(j == 0), stop=(j == nc_ - 1))
                        last.then_inc(s_("weighed"), 1)

                    for j, (c0, m) in enumerate(chunks):
                        g = u * nc_ + j
                        if g >= 2:
                            pe.wait_ge(s_("probs"), before(a, "probs") + g - 1)
                        mm(PS[0:m, 4 + g % 2, :], KA[a][:, b, s, c0:c0 + m],
                           QA[:, b, s, :]).then_inc(s_("shifted"), 1)
                        if j >= 1:
                            pv(j - 1)
                        if j == 2 and u + 1 < len(units):
                            maxima(u + 1)
                        elif j >= 1:
                            step()
                    pv(nc_ - 1)
                    if nc_ == 3:
                        step()

                def dens(b):
                    pe.wait_ge(s_("o_taken"), before(a, "o_taken") + nsub * (b + 1))
                    pe.wait_ge(s_("max_placed"), before(a, "max_placed") + min(nsub * (b + 1) + 1, len(units)))
                    for t in range(TB):
                        for s in range(nsub):
                            at = t * 32 + s * nh
                            last = nc.tensor.transpose(PS[:, 7, at:at + nh], den[0:nh, s, t * 128:(t + 1) * 128],
                                                       ident[0:nh, 0:nh])
                    last.then_inc(s_("dens"), 1)

                def spread(b, z):
                    if z == 0:
                        pe.wait_ge(s_("recs"), before(a, "recs") + b + 1)
                    else:
                        pe.wait_ge(s_("normed"), before(a, "normed") + b + 1)
                    if z == 0:
                        pe.wait_ge(s_("max_placed"), before(a, "max_placed") + placed(b))
                    for t in range(TB):
                        last = nc.tensor.transpose(PS[:, 7, t * 128:(t + 1) * 128],
                                                   xc[:, z, t * 128:(t + 1) * 128], ident)
                    last.then_inc(s_("rec_bcast"), 1)

                def placed(b):
                    return min(unit[0] + 1, len(units))

                def mean_squares(b):
                    pe.wait_ge(s_("att_sq"), before(a, "att_sq") + b + 1)
                    for t in range(TB):
                        last = mm(PS[:, 7, t * 16:(t + 1) * 16], sq[:, b, t * 128:(t + 1) * 128], C("head8mean"))
                    last.then_inc(s_("rms_ms"), 1)

                def rms_spread(b):
                    pe.wait_ge(s_("rms_wide"), before(a, "rms_wide") + b + 1)
                    pe.wait_ge(s_("max_placed"), before(a, "max_placed") + placed(b))
                    for t in range(TB):
                        last = nc.tensor.transpose(PS[:, 7, t * 128:(t + 1) * 128],
                                                   xc[:, 0, t * 128:(t + 1) * 128], ident)
                    last.then_inc(s_("rms_bcast"), 1)

                def project(b):
                    pe.wait_ge(s_("att_done"), before(a, "att_done") + b + 1)
                    mm(PS[:, 7, :], w[:, 3, :], att[:, b, :]).then_inc(s_("projected"), 1)

                def ending(b):
                    yield lambda: dens(b)
                    yield lambda: spread(b, 0)
                    if a == 0:
                        yield lambda: spread(b, 1)
                        yield lambda: mean_squares(b)
                        yield lambda: rms_spread(b)
                    yield lambda: project(b)

                todo, unit = [], [0]

                def step():
                    if todo:
                        todo.pop(0)()

                scores(0)
                maxima(0)
                for u in range(len(units)):
                    if u + 1 < len(units):
                        scores(u + 1)
                    unit[0] = u + 1
                    weigh(u)
                    if units[u][1] == nsub - 1:
                        todo += ending(units[u][0])
                while todo:
                    step()
                pe.wait_ge(s_("y_placed"), before(a, "y_placed") + B)

            def moe():
                layernorm(1)
                arrived(pe, "rw0")
                for b in range(B):
                    pe.wait_ge(S("ln_h"), 2 + b + 1)
                    for t in range(TB):
                        n = b * TB + t
                        nc.tensor.transpose(PS[:, 4 + b, t * 128:(t + 1) * 128], h[b][:, t * 128:(t + 1) * 128], ident)
                        last = mm(PS[:, 6, n * 8:n * 8 + 8], h[b][:, t * 128:(t + 1) * 128], rw0[:, 0:8])
                    last.then_inc(S("moe_logits"), 1)
                pe.wait_ge(S("moe_prefix"), 1)
                mm(PS[:, 7, 0:64], C("tri"), rt[:, 3, :], stop=False)
                mm(PS[:, 7, 0:64], C("ones"), rt[:, 4, :], start=False).then_inc(S("moe_cum"), 1)
                pe.wait_ge(S("moe_htok"), 2)
                for t in range(NT):
                    pe.wait_ge(S("moe_G"), t + 1)
                    for k in range(2):
                        last = mm(PS[:, k, :], htok[:, t, :], G[:, t % 2, k * 512:(k + 1) * 512],
                                  start=(t == 0), stop=(t == NT - 1))
                    last.then_inc(S("moe_gathered"), 1)
                for t in range(NT):
                    last = nc.tensor.transpose(PS[:, 4 + t // 4, (t % 4) * 128:(t % 4) * 128 + 128],
                                               r8t[:, 5, t:t + 1].to_broadcast([128, 128]), ident)
                last.then_inc(S("moe_slots"), 1)
                for t in range(NT):
                    last = nc.tensor.transpose(PS[:, 6 + t // 4, (t % 4) * 128:(t % 4) * 128 + 128],
                                               r8t[:, 6, t:t + 1].to_broadcast([128, 128]), ident)
                last.then_inc(S("moe_slots"), 1)
                arrived(pe, "w1", "w2")
                pe.wait_ge(S("moe_ein"), 2)
                pe.wait_ge(S("moe_bcopied"), 4)

                def up(e):
                    if e >= 2:
                        pe.wait_ge(S("moe_gelu"), e - 1)
                    for f in range(4):
                        last = mm(PS[:, 4 + e % 2, f * 128:(f + 1) * 128], w1[:, e, f * 128:(f + 1) * 128],
                                  ein[:, e * CAP:(e + 1) * CAP])
                    last.then_inc(S("moe_up"), 1)

                def down(e):
                    pe.wait_ge(S("moe_gelu"), e + 1)
                    if e >= 2:
                        pe.wait_ge(S("moe_eo"), e - 1)
                    for f in range(4):
                        last = mm(PS[:, 6 + e % 2, 0:128], hid[:, e % 2, f * 128:(f + 1) * 128], w2[:, e, f, :],
                                  start=(f == 0), stop=(f == 3))
                    last.then_inc(S("moe_down"), 1)

                def combine(e):
                    pe.wait_ge(S("moe_eo"), e + 1)
                    pe.wait_ge(S("moe_GT"), e + 1)
                    for k in range(2):
                        last = mm(PS[:, 2 + k, :], eo[:, e % 2, :], G[:, e % 2, k * 512:(k + 1) * 512],
                                  start=(e == 0), stop=(e == E - 1))
                    last.then_inc(S("moe_combined"), 1)

                up(0)
                for e in range(E):
                    if e + 1 < E:
                        up(e + 1)
                    if e >= 1:
                        combine(e - 1)
                    down(e)
                combine(E - 1)

            def linear():
                arrived(pe, "rows", "wa1")
                for b in range(B):
                    for j, bias in ((1, "bk1"), (2, "bv1")):
                        o = PS[0:SK, 4, (j - 1) * 256 + b * 128:(j - 1) * 256 + b * 128 + 128]
                        mm(o, ctxr[:, b, 0:SK], wa1[:, j, :], stop=False)
                        last = mm(o, C("ones", 1)[:, 0:SK], R(bias), start=False)
                last.then_inc(S("lin_kv"), 1)
                layernorm(2)
                pe.wait_ge(S("lin_kf"), 1)
                for b in range(B):
                    mm(PS[:, 5, b * 128:(b + 1) * 128], kf[:, b, :], vs[:, b, :])
                    last = mm(PS[:, 5, 256 + b * 16:256 + b * 16 + 16], kf[:, b, :], C("ones", SK)[:, 0:16])
                last.then_inc(S("lin_sum"), 1)
                for b in range(B):
                    pe.wait_ge(S("ln_h"), 2 * 2 + b + 1)
                    mm(PS[:, 6 + b, :], wa1[:, 0, :], h[b]).then_inc(S("lin_q"), 1)
                pe.wait_ge(S("lin_kvm"), 1)
                for b in range(B):
                    pe.wait_ge(S("lin_qf"), b + 1)
                    for t in range(TB):
                        mm(PS[:, 4 + b, t * 16:t * 16 + 16], qf[:, b, :][:, t * 128:(t + 1) * 128], ksh[:, b, :])
                    mm(PS[:, 2 * b, :], kvm[:, b, :], qf[:, b, :]).then_inc(S("lin_num"), 1)
                for b in range(B):
                    pe.wait_ge(S("lin_rec"), b + 1)
                    for t in range(TB):
                        last = nc.tensor.transpose(PS[:, 2 * b + 1, t * 128:(t + 1) * 128],
                                                   xc[:, b, t * 128:(t + 1) * 128], ident)
                    last.then_inc(S("lin_bcast"), 1)
                for b in range(B):
                    pe.wait_ge(S("lin_att"), b + 1)
                    mm(PS[:, 6 + b, :], wa1[:, 3, :], att[:, b, :]).then_inc(S("lin_proj"), 1)

            def rwkv():
                layernorm(3)
                arrived(pe, "wf1")
                for b in range(B):
                    pe.wait_ge(S("mix_in"), 2 * b + 1)
                    mm(PS[:, 4 + 2 * b, :], wf1[:, 0, :], xc[:, b, :]).then_inc(S("mix_up"), 1)
                    pe.wait_ge(S("mix_in"), 2 * b + 2)
                    mm(PS[:, 5 + 2 * b, :], wf1[:, 1, :], sq[:, b, :]).then_inc(S("mix_up"), 1)
                for b in range(B):
                    pe.wait_ge(S("mix_k2"), b + 1)
                    mm(PS[:, 2 * b, :], wf1[:, 2, :], att[:, b, :]).then_inc(S("mix_v"), 1)

            def experts():
                layernorm(5)
                arrived(pe, "rw0")
                for b in range(B):
                    pe.wait_ge(S("ln_h"), 2 * 5 + b + 1)
                    for t in range(TB):
                        n = b * TB + t
                        last = mm(PS[:, 6, n * 8:n * 8 + 8], h[b][:, t * 128:(t + 1) * 128], rw0[:, 8:16])
                last.then_inc(S("ex_logits"), 1)
                arrived(pe, "sw13", "sw2", "ew1", "ew2")

                def ups(n):
                    j, b = divmod(n, 2)
                    if n >= 2:
                        pe.wait_ge(S("ex_act"), n - 1)
                        pe.wait_ge(S("ex_prod"), n - 1)
                    if j < 2:
                        mm(PS[:, 2 + n % 2, :], sw13[:, 0, j * 128:(j + 1) * 128], h[b]).then_inc(S("ex_up"), 1)
                        mm(PS[:, 4 + n % 2, :], sw13[:, 1, j * 128:(j + 1) * 128], h[b]).then_inc(S("ex_up"), 1)
                    else:
                        e = j - 2
                        mm(PS[:, 2 + n % 2, :], ew1[:, e, :], h[b]).then_inc(S("ex_up"), 1)
                        mm(PS[:, 4 + n % 2, :], ident[:, e:e + 1].to_broadcast([128, 128]),
                           combT[:, b * T:(b + 1) * T]).then_inc(S("ex_up"), 1)

                def downs(n):
                    j, b = divmod(n, 2)
                    pe.wait_ge(S("ex_prod"), n + 1)
                    w = sw2[:, j, :] if j < 2 else ew2[:, j - 2, :]
                    mm(PS[:, b, :], w, PTB[:, n % 4, :], start=(j == 0), stop=(j == 9)).then_inc(S("ex_down"), 1)

                ups(0)
                for n in range(1, 21):
                    if n == 4:
                        pe.wait_ge(S("ex_comb"), 1)
                        for t in range(NT):
                            last = nc.tensor.transpose(PS[0:8, 6 + t // 4, (t % 4) * 128:(t % 4) * 128 + 128],
                                                       rt[:, 9, t * 8:t * 8 + 8], ident)
                        last.then_inc(S("ex_combT"), 1)
                        pe.wait_ge(S("ex_combT_placed"), 1)
                    if n < 20:
                        ups(n)
                    downs(n - 1)


            def final_layer():
                layernorm(7)
                arrived(pe, "const3", "wd")
                for b in range(B):
                    pe.wait_ge(S("ln_h"), 2 * 7 + b + 1)
                    mm(PS[0:8, 4 + b, :], rw0[:, 16:24], h[b]).then_inc(S("sp_router"), 1)
                for b in range(B):
                    for t in range(TB):
                        last = nc.tensor.transpose(PS[:, 6 + b, t * 128:(t + 1) * 128], h[b][:, t * 128:(t + 1) * 128],
                                                   ident)
                    last.then_inc(S("sp_tokens"), 1)
                for j in range(3):
                    last = mm(PS[:, j, :], wd[:, j * 128:(j + 1) * 128], h[0])
                last.then_inc(S("d_pair"), 1)
                pe.wait_ge(S("sp_htok"), 1)
                for n in range(NT):
                    b, t = divmod(n, TB)
                    if n == 1:
                        pe.wait_ge(S("sp_htok"), 2)
                    if n >= 2:
                        pe.wait_ge(S("d_v_placed"), n - 1)
                    mm(PS[:, 6 + n % 2, :], h[b][:, t * 128:(t + 1) * 128], wd[:, 1536:2048]).then_inc(S("d_values"), 1)
                pe.wait_ge(S("d_v_placed"), NT)
                pe.wait_ge(S("pool_set"), POOL_SET["last"])

                def prepare(r):
                    b, p = divmod(r, 4)
                    for j in range(3):
                        last = mm(PS[:, j, :], wd[:, p * 384 + j * 128:p * 384 + (j + 1) * 128], h[b])
                    last.then_inc(S("d_pair"), 1)

                def scores(u):
                    r, z = divmod(u, 2)
                    if z == 0:
                        pe.wait_ge(S("d_roped"), 2 * (r + 1))
                    ahead = min(r + (2 if r or z else 1), NU // 2)
                    if u > 0:
                        pe.wait_ge(S("d_max"), u)
                    for t in reversed(range(TB)):
                        if t == TB - 2:
                            pe.wait_ge(S("d_swap"), 4 * ahead)
                            pe.wait_ge(S("d_raw"), 4 * ahead)
                        last = mm(PS[:, t, (3 - t) * 128:512], QK[r % 3][0:64, z, t * 128:(t + 1) * 128],
                                  QK[r % 3][0:64, 2 + z, 0:(t + 1) * 128])
                    last.then_inc(S("d_scores"), 1)

                def maxima(u):
                    pe.wait_ge(S("d_max"), u + 1)
                    if u > 1:
                        pe.wait_ge(S("d_rec"), u - 1)
                    for t in range(TB):
                        last = nc.tensor.transpose(PS[0:1, 7, t * 128:(t + 1) * 128], mxd[:, u % 2, t:t + 1], ident)
                    last.then_inc(S("d_max_row"), 1)

                def dens(u):
                    pe.wait_ge(S("d_taken"), u + 1)
                    pe.wait_ge(S("d_max_placed"), min(u + 2, NU))
                    for t in range(TB):
                        last = mm(PS[:, 7, t:t + 1], denr[0:1, u % 2, t * 128:(t + 1) * 128], C("ones", 1)[:, 0:1])
                    last.then_inc(S("d_dens"), 1)

                def shifted(u, k):
                    r, z = divmod(u, 2)
                    g = 4 * u + k
                    if k == 0:
                        pe.wait_ge(S("d_max_placed"), u + 1)
                    if g >= 2:
                        pe.wait_ge(S("d_probs"), g - 1)
                    mm(PS[:, 4 + g % 2, k * 128:512], QK[r % 3][:, 2 + z, k * 128:(k + 1) * 128],
                       QK[r % 3][:, z, k * 128:512]).then_inc(S("d_shifted"), 1)

                def weigh(u, k):
                    b, hd = divmod(u, NHD)
                    g = 4 * u + k
                    pe.wait_ge(S("d_masked"), g + 1)
                    if k == 0 and u > 0:
                        pe.wait_ge(S("d_taken"), u)
                    mm(PS[0:65, 6, k * 128:512], VD[:, b * TB + k, hd, :], PTB[:, g % 4, k * 128:512],
                       start=(k == 0), stop=(k == 3)).then_inc(S("d_weighed"), 1)

                NU = B * NHD
                scores(0)
                pe.wait_ge(S("d_max"), 1)
                prepare(1)
                maxima(0)
                for u in range(NU):
                    r, z = divmod(u, 2)
                    shifted(u, 0)
                    shifted(u, 1)
                    if u + 1 < NU:
                        scores(u + 1)
                    weigh(u, 0)
                    if u > 0:
                        dens(u - 1)
                    weigh(u, 1)
                    shifted(u, 2)
                    shifted(u, 3)
                    if u + 1 < NU:
                        maxima(u + 1)
                    weigh(u, 2)
                    weigh(u, 3)
                    if z == 0 and r + 2 < NU // 2:
                        prepare(r + 2)
                dens(NU - 1)

                arrived(pe, "wm", "wod", "wom")
                pe.wait_ge(S("sp_selected"), 1)
                for t in range(TB):
                    last = nc.tensor.transpose(PS[:, 0, t * 40:t * 40 + 40], wk[:, t * 128:(t + 1) * 128],
                                               ident[0:40, 0:40])
                last.then_inc(S("sp_sel_cols"), 1)
                pe.wait_ge(S("sp_prefix"), 1)
                mm(PS[:, 1, 0:64], C("tri"), selT[:, 0, :], stop=False)
                mm(PS[:, 1, 0:64], C("ones"), selT[:, 1, :], start=False).then_inc(S("sp_cum"), 1)
                for b in range(B):
                    pe.wait_ge(S("sp_G"), TB * (b + 1))
                    for t in range(TB):
                        last = mm(PS[:, 2, :], htok[:, b * TB + t, :], PTB[:, 4 * b + t, :], start=(t == 0),
                                  stop=(t == TB - 1))
                    last.then_inc(S("sp_gathered"), 1)
                    for t in range(TB):
                        last = mm(PS[0:64, 3, :], C3("tab")[:, t * 64:(t + 1) * 64], PTB[:, 4 * b + t, :],
                                  start=(t == 0), stop=(t == TB - 1))
                    last.then_inc(S("sp_angles"), 1)
                    for q in range(4):
                        if q >= 2 or b:
                            pe.wait_ge(S("sp_GT"), 4 * b + q - 1)
                        for t in range(TB):
                            last = nc.tensor.transpose(PS[:, 4 + q % 2, t * 128:(t + 1) * 128],
                                                       PTB[:, 4 * b + t, q * 128:(q + 1) * 128], ident)
                        last.then_inc(S("sp_turned"), 1)
                    pe.wait_ge(S("sp_x"), b + 1)
                    for hd in range(8):
                        hs = slice(hd * 64, hd * 64 + 64)
                        mm(PS[:, 0, hs], wm[:, hd * 256:hd * 256 + 128], xg[:, hs])
                        last = mm(PS[0:64, 1, hs], wm[:, hd * 256 + 128:hd * 256 + 192], xg[:, hs])
                    last.then_inc(S("sp_qk"), 1)
                    pe.wait_ge(S("sp_trig"), b + 1)
                    pe.wait_ge(S("sp_GT"), 4 * b + 4)
                    for hd in range(8):
                        hs = slice(hd * 64, hd * 64 + 64)
                        mm(PS[0:64, 3, hs], xg[:, hs], wm[:, hd * 256 + 192:hd * 256 + 256])
                        last = mm(PS[0:64, 4, hd:hd + 1], xg[:, hs], rw0[:, 16 + hd:17 + hd])
                    last.then_inc(S("sp_v"), 1)
                    pe.wait_ge(S("sp_roped"), b + 1)
                    for hd in range(8):
                        hs = slice(hd * 64, hd * 64 + 64)
                        last = mm(PS[0:64, 5, hs], sqk[:, 0, hs], sqk[:, 1, hs])
                    last.then_inc(S("sp_scores"), 1)
                    pe.wait_ge(S("sp_p"), b + 1)
                    for hd in range(8):
                        hs = slice(hd * 64, hd * 64 + 64)
                        last = nc.tensor.transpose(PS[0:64, 2, hs], spp[:, hs], ident[0:64, 0:64])
                    last.then_inc(S("sp_pT"), 1)
                    pe.wait_ge(S("sp_pT_placed"), b + 1)
                    pe.wait_ge(S("sp_v_placed"), b + 1)
                    for hd in range(8):
                        hs = slice(hd * 64, hd * 64 + 64)
                        last = mm(PS[0:64, 3, hs], spv[:, 0, hs], spv[:, 1, hs])
                    last.then_inc(S("sp_o"), 1)
                    pe.wait_ge(S("sp_o_placed"), b + 1)
                    for hd in range(8):
                        hs = slice(hd * 64, hd * 64 + 64)
                        last = mm(PS[0:64, hd // 4, (hd % 4) * 128:(hd % 4) * 128 + 128], spo[:, hs], wom[:, hd, :])
                    last.then_inc(S("sp_z"), 1)
                    for q in range(4):
                        n = 4 * b + q
                        pe.wait_ge(S("d_wide"), n + 1)
                        if n >= 2:
                            pe.wait_ge(S("d_normed"), n - 1)
                        else:
                            pe.wait_ge(S("sp_GT"), 4)
                        for t in range(TB):
                            last = nc.tensor.transpose(PS[:, 4 + n % 2, t * 128:(t + 1) * 128],
                                                       wide[:, n % 2, t * 128:(t + 1) * 128], ident)
                        last.then_inc(S("d_spread"), 1)
                    for q in range(4):
                        pe.wait_ge(S("d_normed"), 4 * b + q + 1)
                        mm(PS[:, 6 + b, :], wod[:, q, :], AVT[:, b, q, :], start=(q == 0), stop=False)
                    pe.wait_ge(S("sp_zs"), b + 1)
                    for q in range(4):
                        last = mm(PS[:, 6 + b, :], spz[:, q, :], GT[b][q], start=False, stop=(q == 3))
                    last.then_inc(S("last_y"), 1)
            attention(0, 0, wa0, None)
            moe()
            linear()
            rwkv()
            attention(1, 4, wa2, "bv2")
            experts()
            attention(2, 6, wa3, "bv3")
            final_layer()

        @block.scalar
        def _(act):
            A_ = nc.scalar.activation

            def layernorm(i):
                for b in range(B):
                    act.wait_ge(S("ln_centered"), 2 * i + b + 1)
                    A_(sq[:, b, :], PS[:, 2 * b, :], ACT.Square).then_inc(S("ln_act"), 1)
                    nc.scalar.copy(xc[:, b, :], PS[:, 2 * b, :]).then_inc(S("ln_act"), 1)

            def attention(a, i, kbias, obias, kfunc, qbias):
                c = ATTN[a]
                nsub, nh, qd, mr = c["nsub"], c["nh"], c["qd"], c["mrow"]
                s_ = lambda n: S("at_" + n)
                act.wait_ge(s_("keys"), before(a, "keys") + 1)
                for s in range(nsub):
                    src = PS[0:qd, 4 + s // 2, (s % 2) * 154:(s % 2) * 154 + 154]
                    dst = kT[0:qd, s, :]
                    if a > 0:
                        last = A_(dst, src, kfunc, bias=V(kbias, qd, s))
                    else:
                        last = nc.scalar.copy(dst, src)
                last.then_inc(s_("k_placed"), 1)
                layernorm(i)
                act.wait_ge(s_("q_zeroed"), before(a, "q_zeroed") + 1)
                for b in range(B):
                    for s in range(nsub):
                        if a == 0:
                            act.wait_ge(s_("query"), before(a, "query") + b + 1)
                            nc.scalar.copy(QA[0:qd, b, s, :],
                                           PS[s * qd:(s + 1) * qd, 4 + b, :]).then_inc(s_("q_placed"), 1)
                        else:
                            act.wait_ge(s_("query"), before(a, "query") + nsub * b + s + 1)
                            A_(QA[0:qd, b, s, :], PS[0:qd, 4 + 2 * b + s, :], ACT.Identity,
                               bias=V(qbias, qd, s)).then_inc(s_("q_placed"), 1)
                units = [(b, s) for b in range(B) for s in range(nsub)]
                chunks = c["chunks"]

                def place(u):
                    b, s = units[u]
                    act.wait_ge(s_("max_rows"), before(a, "max_rows") + u + 1)
                    nc.scalar.copy(QA[mr:mr + nh, b, s, :], PS[0:nh, 7, :]).then_inc(s_("max_placed"), 1)

                def square(b):
                    act.wait_ge(s_("att_raw"), before(a, "att_raw") + b + 1)
                    A_(sq[:, b, :], att[:, b, :], ACT.Square).then_inc(s_("att_sq"), 1)

                def project(b):
                    act.wait_ge(s_("projected"), before(a, "projected") + b + 1)
                    A_(yb[:, b, :], PS[:, 7, :], ACT.Identity, bias=V(obias)).then_inc(s_("y_placed"), 1)

                todo = []

                def step():
                    if todo:
                        todo.pop(0)()

                nothing = lambda: None
                place(0)
                for u, (b, s) in enumerate(units):
                    for j, (c0, m) in enumerate(chunks):
                        g = u * len(chunks) + j
                        act.wait_ge(s_("shifted"), before(a, "shifted") + g + 1)
                        if g >= 4:
                            act.wait_ge(s_("weighed"), before(a, "weighed") + g - 3)
                        A_(PT[0:m, g % 4, :], PS[0:m, 4 + g % 2, :], ACT.Exp,
                           scale=c["scale"]).then_inc(s_("probs"), 1)
                        if j == 2 and u + 1 < len(units):
                            place(u + 1)
                        elif j >= 1:
                            step()
                    if len(chunks) == 3:
                        step()
                    if s == nsub - 1:
                        if a == 0:
                            todo += [nothing, nothing, lambda b=b: square(b), nothing, nothing, lambda b=b: project(b)]
                        else:
                            todo += [nothing, nothing, lambda b=b: project(b)]
                while todo:
                    step()

            def moe():
                layernorm(1)
                for b in range(B):
                    act.wait_ge(S("moe_logits"), b + 1)
                    nc.scalar.copy(htok[:, b * TB:(b + 1) * TB, :],
                                   PS[:, 4 + b, :].rearrange("p (t f) -> p t f", t=TB)).then_inc(S("moe_htok"), 1)
                act.wait_ge(S("moe_diff"), 1)
                A_(rt[:, 2, :], rt[:, 1, :], ACT.Exp).then_inc(S("moe_exp"), 1)
                act.wait_ge(S("moe_slots"), 1)
                for k in range(2):
                    nc.scalar.copy(destb[:, k * 512:(k + 1) * 512], PS[:, 4 + k, :]).then_inc(S("moe_bcopied"), 1)
                act.wait_ge(S("moe_slots"), 2)
                for k in range(2):
                    nc.scalar.copy(gateb[:, k * 512:(k + 1) * 512], PS[:, 6 + k, :]).then_inc(S("moe_bcopied"), 1)
                for e in range(E):
                    act.wait_ge(S("moe_up"), e + 1)
                    if e >= 2:
                        act.wait_ge(S("moe_down"), e - 1)
                    A_(hid[:, e % 2, :], PS[:, 4 + e % 2, :], ACT.Gelu_apprx_tanh).then_inc(S("moe_gelu"), 1)

            def linear():
                layernorm(2)
                for b in range(B):
                    act.wait_ge(S("lin_num"), b + 1)
                    nc.scalar.copy(yb[:, b, :], PS[:, 2 * b, :]).then_inc(S("lin_numc"), 1)
                for b in range(B):
                    act.wait_ge(S("lin_proj"), b + 1)
                    act.wait_ge(S("lin_att"), b + 1)
                    A_(yb[:, b, :], PS[:, 6 + b, :], ACT.Identity, bias=V("bo1")).then_inc(S("lin_y"), 1)

            def rwkv():
                layernorm(3)
                for b in range(B):
                    act.wait_ge(S("mix_up"), 2 * b + 1)
                    A_(yb[:, b, :], PS[:, 4 + 2 * b, :], ACT.Sigmoid).then_inc(S("mix_act"), 1)
                    act.wait_ge(S("mix_up"), 2 * b + 2)
                    A_(PTB[:, b, :], PS[:, 5 + 2 * b, :], ACT.Relu).then_inc(S("mix_act"), 1)

            def experts():
                layernorm(5)
                act.wait_ge(S("ex_logits"), 1)
                A_(rt[:, 0, :], PS[:, 6, 0:64], ACT.Sigmoid).then_inc(S("ex_sig"), 1)
                for n in range(20):
                    if n == 4:
                        act.wait_ge(S("ex_combT"), 1)
                        for k in range(2):
                            last = nc.scalar.copy(combT[0:8, k * 512:(k + 1) * 512], PS[0:8, 6 + k, :])
                        last.then_inc(S("ex_combT_placed"), 1)
                    act.wait_ge(S("ex_up"), 2 * n + 1)
                    if n >= 4:
                        act.wait_ge(S("ex_prod"), n - 3)
                    A_(PTB[:, 4 + n % 4, :], PS[:, 2 + n % 2, :],
                       ACT.Silu if n < 4 else ACT.Gelu).then_inc(S("ex_act"), 1)


            def final_layer():
                layernorm(7)
                act.wait_ge(S("sp_cleared"), 1)
                for b in range(B):
                    act.wait_ge(S("sp_router"), b + 1)
                    nc.scalar.copy(wk[32 * b:32 * b + 8, :], PS[0:8, 4 + b, :]).then_inc(S("sp_work"), 1)
                for b in range(B):
                    act.wait_ge(S("sp_tokens"), b + 1)
                    nc.scalar.copy(htok[:, b * TB:(b + 1) * TB, :],
                                   PS[:, 6 + b, :].rearrange("p (t f) -> p t f", t=TB)).then_inc(S("sp_htok"), 1)

                def pair(r, j):
                    act.wait_ge(S("d_pair"), r + 1)
                    if r >= 3:
                        act.wait_ge(S("d_shifted"), 8 * (r - 2))
                    for z in range(2):
                        nc.scalar.copy(QK[r % 3][0:64, 2 * j + z, :],
                                       PS[64 * z:64 * z + 64, j, :]).then_inc(S("d_raw"), 1)

                NU = B * NHD
                pair(0, 0)
                pair(0, 1)
                for n in range(NT):
                    act.wait_ge(S("d_values"), n + 1)
                    nc.scalar.copy(VD[:, n, :, 0:64],
                                   PS[:, 6 + n % 2, :].rearrange("p (h d) -> p h d", h=NHD)).then_inc(S("d_v_placed"), 1)
                pair(1, 0)
                pair(1, 1)
                act.wait_ge(S("pool_set"), POOL_SET["last"])
                act.wait_ge(S("d_max_row"), 1)
                nc.scalar.copy(QK[0][64:65, 0, :], PS[0:1, 7, :]).then_inc(S("d_max_placed"), 1)
                for u in range(NU):
                    r, z = divmod(u, 2)
                    for k in range(4):
                        g = 4 * u + k
                        act.wait_ge(S("d_shifted"), g + 1)
                        if g >= 4:
                            act.wait_ge(S("d_weighed"), g - 3)
                        A_(PTB[:, g % 4, k * 128:512], PS[:, 4 + g % 2, k * 128:512], ACT.Exp,
                           scale=HP ** -0.5).then_inc(S("d_probs"), 1)
                        if k < 2 and z == 1 and 2 <= (r + 2) < NU // 2:
                            pair(r + 2, k)
                    if u + 1 < NU:
                        r1, z1 = divmod(u + 1, 2)
                        act.wait_ge(S("d_max_row"), u + 2)
                        nc.scalar.copy(QK[r1 % 3][64:65, z1, :], PS[0:1, 7, :]).then_inc(S("d_max_placed"), 1)
                for b in range(B):
                    act.wait_ge(S("sp_gathered"), b + 1)
                    if b:
                        act.wait_ge(S("sp_v"), b)
                    nc.scalar.copy(xg, PS[:, 2, :]).then_inc(S("sp_x"), 1)
                    for q in range(4):
                        act.wait_ge(S("sp_turned"), 4 * b + q + 1)
                        nc.scalar.copy(GT[b][q], PS[:, 4 + q % 2, :]).then_inc(S("sp_GT"), 1)
                    act.wait_ge(S("sp_qk"), b + 1)
                    if b:
                        act.wait_ge(S("sp_scores"), b)
                    for j in range(2):
                        nc.scalar.copy(sqk[:, j, :], PS[64 * j:64 * j + 64, 0, :]).then_inc(S("sp_qk_placed"), 1)
                    act.wait_ge(S("sp_v"), b + 1)
                    if b:
                        act.wait_ge(S("sp_o"), b)
                    nc.scalar.copy(spv[:, 0, :], PS[0:64, 3, :]).then_inc(S("sp_v_placed"), 1)
                    if b:
                        act.wait_ge(S("sp_factor"), b)
                    A_(sps[:, 0, :], PS[0:64, 4, 0:8], ACT.Sigmoid).then_inc(S("sp_gate"), 1)
                    act.wait_ge(S("sp_diff"), b + 1)
                    A_(spp, sdiff, ACT.Exp, scale=HP ** -0.5).then_inc(S("sp_p"), 1)
                    act.wait_ge(S("sp_pT"), b + 1)
                    nc.scalar.copy(spv[:, 1, :], PS[0:64, 2, :]).then_inc(S("sp_pT_placed"), 1)
                    act.wait_ge(S("sp_o"), b + 1)
                    nc.scalar.copy(spo, PS[0:64, 3, :]).then_inc(S("sp_o_placed"), 1)
            arrived(act, "cols")
            A_(tg[:], V("g"), ACT.Tanh).then_inc(S("gates"), 1)
            act.wait_ge(S("lam_dots"), 2)
            A_(small[:, 2:4], small[:, 0:2], ACT.Exp).then_inc(S("gates"), 1)
            attention(0, 0, None, "bp", None, None)
            moe()
            linear()
            rwkv()
            attention(1, 4, "bk2", "bo2", ACT.Identity, "bq2")
            experts()
            attention(2, 6, "bk3", "bo3", ACT.Tanh, "bq3")
            final_layer()

        @block.vector
        def _(dve):
            link = Chain(dve, "dve_own")
            v = nc.vector

            def layernorm(i):
                for b in range(B):
                    dve.wait_ge(S("ln_var"), 2 * i + b + 1)
                    v.tensor_scalar(veps[:, b, :], PS[:, 2 * b + 1, 0:TB], EPS, None, ALU.add).then_inc(S("ln_veps"), 1)
                for b in range(B):
                    k = 2 * i + b + 1
                    dve.wait_ge(S("ln_bcast"), k)
                    dve.wait_ge(S("ln_act"), 2 * k)
                    v.tensor_tensor(h[b], xc[:, b, :], PS[:, 2 * b + 1, :], ALU.mult).then_inc(S("ln_h"), 1)

            def widen(dst, src, width):
                n = src.shape[2]
                return v.tensor_copy(dst.rearrange("p (t n w) -> p t n w", t=TB, n=n),
                                     src.unsqueeze(3).to_broadcast([128, TB, n, width]))

            def residual(b, gate):
                v.scalar_tensor_tensor(xb[b], yb[:, b, :], tg[:, gate:gate + 1], xb[b], ALU.mult,
                                       ALU.add).then_inc(S("x_ready"), 1)

            def attention(a, i, layer):
                c = ATTN[a]
                nsub, nh, qd = c["nsub"], c["nh"], c["qd"]
                chunks = c["chunks"]
                s_ = lambda n: S("at_" + n)
                vm = C("vmask8" if nh == 8 else "vmask16").rearrange("p (c f) -> p c f", f=64)
                full = [j for j, (_, m) in enumerate(chunks) if m == 128]
                for b in range(B):
                    dve.wait_ge(s_("values"), before(a, "values") + b + 1)
                    for z in range(2):
                        n = len(full)
                        v.tensor_tensor(VA[a][:, b, z, 0:n, 0:64],
                                        PS[:, 6, 0:n * 128].rearrange("p (c f) -> p c f", f=128)[:, :, z * 64:z * 64 + 64],
                                        vm[:, 0:n, :], ALU.mult)
                        m = chunks[-1][1]
                        at = (n % 4) * 128 + z * 64
                        last = v.tensor_tensor(VA[a][0:m, b, z, n, 0:64], PS[0:m, 6 + n // 4, at:at + 64], vm[0:m, n, :],
                                               ALU.mult)
                    last.then_inc(s_("v_placed"), 1)
                layernorm(i)
                units = [(b, s) for b in range(B) for s in range(nsub)]

                def maxima(u):
                    b, s = units[u]
                    for t in range(TB):
                        n = TB * u + t
                        dve.wait_ge(s_("scores"), before(a, "scores") + n + 1)
                        nb = c["rows"] // 308
                        src = PS[:, 2 * (n % 2):2 * (n % 2) + nb, 0:308].rearrange("p j (h k) -> p j h k", k=SK)
                        if a == 1:
                            dst = sm[:, n % 2, :].rearrange("p (j h k) -> p j h k", j=2, k=SK)
                            for j in range(2):
                                ins = v.tensor_tensor(dst[:, j], src[:, j],
                                                      mbias[:, t, :].unsqueeze(1).to_broadcast([128, 4, SK]), ALU.add)
                            link(ins)
                            src = dst
                        v.tensor_reduce(mx[:, b, s, t, 0:nh].rearrange("p (j h) -> p j h", h=4), src, AX.X, ALU.max).then_inc(s_("max_taken"), 1)

                def take(u):
                    b, s = units[u]
                    for j, (c0, m) in enumerate(chunks):
                        if a == 1:
                            g = u * len(chunks) + j
                            dve.wait_ge(s_("probs"), before(a, "probs") + g + 1)
                            v.scalar_tensor_tensor(PT[0:m, g % 4, :], PT[0:m, g % 4, :], BIG, keep[0:m, j, :],
                                                   ALU.min, ALU.mult).then_inc(s_("p_masked"), 1)
                        if j >= 1 and not (j == 2 and u + 1 < len(units)):
                            step()
                    if len(chunks) == 3:
                        step()
                    dve.wait_ge(s_("weighed"), before(a, "weighed") + len(chunks) * (u + 1))
                    z = s % 2
                    v.tensor_copy(OT[64 * z:64 * z + 64, b, s // 2, :], PS[0:64, 6, :])
                    v.tensor_copy(den[0:nh, s, :], PS[64:64 + nh, 6, :]).then_inc(s_("o_taken"), 1)

                def reciprocals(b):
                    dve.wait_ge(s_("dens"), before(a, "dens") + b + 1)
                    link(v.reciprocal(rec[:, b, :, 0:nsub * nh],
                                      PS[:, 7, 0:128].rearrange("p (t n) -> p t n", t=TB)[:, :, 0:nsub * nh]))
                    for z in range(nsub // 2):
                        ins = widen(xc[:, z, :], rec[:, b, :, 2 * z * nh:2 * (z + 1) * nh], 64 // nh)
                    ins.then_inc(s_("recs"), 1)

                def normalise(b):
                    dve.wait_ge(s_("rec_bcast"), before(a, "rec_bcast") + nsub // 2 * b + 1)
                    if a == 0:
                        v.tensor_tensor(OT[:, b, 0, :], OT[:, b, 0, :], PS[:, 7, :], ALU.mult).then_inc(s_("normed"), 1)
                        dve.wait_ge(s_("normed"), before(a, "normed") + b + 1)
                    else:
                        v.tensor_tensor(att[:, b, :], OT[:, b, 0, :], PS[:, 7, :], ALU.mult).then_inc(s_("att_done"), 1)

                def combine(b):
                    dve.wait_ge(s_("rec_bcast"), before(a, "rec_bcast") + 2 * b + 2)
                    link(v.tensor_tensor(OT[:, b, 1, :], OT[:, b, 1, :], PS[:, 7, :], ALU.mult))
                    v.scalar_tensor_tensor(att[:, b, :], OT[:, b, 1, :], small[:, 4:5], OT[:, b, 0, :],
                                           ALU.mult, ALU.add).then_inc(s_("att_raw"), 1)

                def root(b):
                    dve.wait_ge(s_("rms_ms"), before(a, "rms_ms") + b + 1)
                    v.tensor_scalar(rms[:, b, :], PS[:, 7, 0:64], EPS, None, ALU.add).then_inc(s_("rms_eps"), 1)
                    dve.wait_ge(s_("rms_r"), before(a, "rms_r") + b + 1)
                    widen(xc[:, 0, :], rmsr[:, b, :, :], 8).then_inc(s_("rms_wide"), 1)

                def scale(b):
                    dve.wait_ge(s_("rms_bcast"), before(a, "rms_bcast") + b + 1)
                    v.scalar_tensor_tensor(att[:, b, :], att[:, b, :], small[:, 5:6], PS[:, 7, :], ALU.mult,
                                           ALU.mult).then_inc(s_("att_done"), 1)

                def add(b):
                    dve.wait_ge(s_("y_placed"), before(a, "y_placed") + b + 1)
                    if a == 2:
                        link(v.tensor_tensor(yb[:, b, :], yb[:, b, :], mask3f[:, b * T:(b + 1) * T], ALU.mult))
                    residual(b, layer)

                todo = []

                def step():
                    if todo:
                        todo.pop(0)()

                maxima(0)
                for u, (b, s) in enumerate(units):
                    if u + 1 < len(units):
                        maxima(u + 1)
                    take(u)
                    if s == nsub - 1:
                        if a == 0:
                            todo += [lambda f=f, b=b: f(b) for f in (reciprocals, normalise, combine, root, scale, add)]
                        else:
                            todo += [lambda f=f, b=b: f(b) for f in (reciprocals, normalise, add)]
                while todo:
                    step()

            def first_max(vals, out_, tmp, m):
                v3 = lambda t: t.rearrange("p (t e) -> p t e", e=8)
                link(v.tensor_reduce(m, v3(vals), AX.X, ALU.max))
                link(v.tensor_tensor(v3(tmp), v3(vals), m.unsqueeze(2).to_broadcast([128, 8, 8]), ALU.is_equal))
                link(v.tensor_tensor(tmp, tmp, C("firstw"), ALU.mult))
                link(v.tensor_reduce(m, v3(tmp), AX.X, ALU.max))
                link(v.tensor_tensor(v3(out_), v3(tmp), m.unsqueeze(2).to_broadcast([128, 8, 8]), ALU.is_equal))

            v3 = lambda t: t.rearrange("p (t e) -> p t e", e=8)

            def moe():
                layernorm(1)
                dve.wait_ge(S("moe_logits"), 2)
                link(v.tensor_copy(rt[:, 0, :], PS[:, 6, 0:64]))
                link(v.tensor_reduce(r8t[:, 0, :], v3(rt[:, 0, :]), AX.X, ALU.max))
                v.tensor_tensor(v3(rt[:, 1, :]), v3(rt[:, 0, :]), r8t[:, 0, :].unsqueeze(2).to_broadcast([128, 8, 8]),
                                ALU.subtract).then_inc(S("moe_diff"), 1)
                first_max(rt[:, 0, :], rt[:, 3, :], rt[:, 5, :], r8t[:, 1, :])
                link(v.memset(rt[:, 4, 0:8], 0.0))
                for t in range(1, NT):
                    ins = v.tensor_tensor(rt[:, 4, t * 8:t * 8 + 8], rt[:, 4, t * 8 - 8:t * 8], rt[:, 3, t * 8 - 8:t * 8],
                                          ALU.add)
                    if t < NT - 1:
                        link(ins)
                ins.then_inc(S("moe_prefix"), 1)
                dve.wait_ge(S("moe_exp"), 1)
                link(v.tensor_reduce(r8t[:, 7, :], v3(rt[:, 2, :]), AX.X, ALU.add))
                link(v.reciprocal(r8t[:, 6, :], r8t[:, 7, :]))
                dve.wait_ge(S("moe_cum"), 1)
                link(v.tensor_tensor(rt[:, 6, :], PS[:, 7, 0:64], rt[:, 3, :], ALU.mult))
                link(v.tensor_reduce(r8t[:, 2, :], v3(rt[:, 6, :]), AX.X, ALU.add))
                link(v.tensor_tensor(rt[:, 7, :], C("slot0"), rt[:, 3, :], ALU.mult))
                link(v.tensor_reduce(r8t[:, 3, :], v3(rt[:, 7, :]), AX.X, ALU.add))
                link(v.tensor_scalar(r8t[:, 4, :], r8t[:, 2, :], float(CAP), 4096.0, ALU.is_gt, ALU.mult))
                link(v.tensor_tensor(r8t[:, 4, :], r8t[:, 4, :], r8t[:, 3, :], ALU.add))
                link(v.scalar_tensor_tensor(r8t[:, 5, :], r8t[:, 2, :], -1.0, r8t[:, 4, :], ALU.add, ALU.add))
                dve.wait_ge(S("pool_set"), POOL_SET["iota"])
                for t in range(NT):
                    if t >= 2:
                        dve.wait_ge(S("moe_gathered"), t - 1)
                    v.tensor_scalar(G[:, t % 2, :], pool_iota[:], r8t[:, 5, t:t + 1], None,
                                    ALU.is_equal).then_inc(S("moe_G"), 1)
                dve.wait_ge(S("moe_gathered"), NT)
                for k in range(2):
                    v.tensor_copy(ein[:, k * 512:(k + 1) * 512], PS[:, k, :]).then_inc(S("moe_ein"), 1)
                dve.wait_ge(S("moe_bcopied"), 4)
                for e in range(E):
                    if e >= 2:
                        dve.wait_ge(S("moe_combined"), e - 1)
                    v.tensor_scalar(G[:, e % 2, :], destb[:], C("slotid")[:, e:e + 1], None,
                                    ALU.is_equal).then_inc(S("moe_GT"), 1)
                    dve.wait_ge(S("moe_down"), e + 1)
                    v.tensor_copy(eo[:, e % 2, :], PS[:, 6 + e % 2, 0:128]).then_inc(S("moe_eo"), 1)
                dve.wait_ge(S("moe_combined"), E)
                for b in range(B):
                    link(v.tensor_tensor(yb[:, b, :], gateb[:, b * T:(b + 1) * T], PS[:, 2 + b, :], ALU.mult))
                    residual(b, 4)

            def linear():
                dve.wait_ge(S("lin_kv"), 1)
                link(v.tensor_scalar(kf[:], PS[0:SK, 4, 0:256].rearrange("p (b f) -> p b f", b=B), 8 ** -0.5, 0.0,
                                     ALU.mult, ALU.max))
                link(v.tensor_scalar(kf[:], kf[:], 1e-6, None, ALU.add))
                v.tensor_copy(vs[:], PS[0:SK, 4, 256:512].rearrange("p (b f) -> p b f", b=B)).then_inc(S("lin_kf"), 1)
                layernorm(2)
                dve.wait_ge(S("lin_sum"), 1)
                v.tensor_tensor(kvm[:], PS[:, 5, 0:256].rearrange("p (b f) -> p b f", b=B),
                                C("block8").unsqueeze(1).to_broadcast([128, B, 128]), ALU.mult)
                v.tensor_tensor(ksh[:], PS[:, 5, 256:288].rearrange("p (b f) -> p b f", b=B),
                                C("head8").unsqueeze(1).to_broadcast([128, B, 16]), ALU.mult).then_inc(S("lin_kvm"), 1)
                for b in range(B):
                    dve.wait_ge(S("lin_q"), b + 1)
                    link(v.tensor_scalar(qf[:, b, :], PS[:, 6 + b, :], V("bq1"), 8 ** -0.5, ALU.add, ALU.mult))
                    v.tensor_scalar(qf[:, b, :], qf[:, b, :], 0.0, 1e-6, ALU.max, ALU.add).then_inc(S("lin_qf"), 1)
                for b in range(B):
                    dve.wait_ge(S("lin_num"), b + 1)
                    link(v.tensor_scalar(rms[:, b, :], PS[:, 4 + b, 0:64], 1e-8, None, ALU.add))
                    link(v.reciprocal(rmsr[:, b, :, :], rms[:, b, :].rearrange("p (t n) -> p t n", t=TB)))
                    widen(xc[:, b, :], rmsr[:, b, :, :], 8).then_inc(S("lin_rec"), 1)
                for b in range(B):
                    dve.wait_ge(S("lin_bcast"), b + 1)
                    dve.wait_ge(S("lin_numc"), b + 1)
                    v.tensor_tensor(att[:, b, :], yb[:, b, :], PS[:, 2 * b + 1, :], ALU.mult).then_inc(S("lin_att"), 1)
                for b in range(B):
                    dve.wait_ge(S("lin_y"), b + 1)
                    residual(b, 1)

            def rwkv():
                layernorm(3)
                for b in range(B):
                    dve.wait_ge(S("ln_h"), 2 * 3 + b + 1)
                    for mu, dst in ((0, xc), (1, sq)):
                        link(v.tensor_scalar(dst[:, b, :], hp[:, b, 0:T], small[:, 6 + mu:7 + mu], None, ALU.mult))
                        v.scalar_tensor_tensor(dst[:, b, :], h[b], V("mur" if mu == 0 else "muk"), dst[:, b, :],
                                               ALU.mult, ALU.add).then_inc(S("mix_in"), 1)
                for b in range(B):
                    dve.wait_ge(S("mix_act"), 2 * b + 2)
                    v.tensor_tensor(att[:, b, :], PTB[:, b, :], PTB[:, b, :], ALU.mult).then_inc(S("mix_k2"), 1)
                for b in range(B):
                    dve.wait_ge(S("mix_v"), b + 1)
                    link(v.tensor_tensor(yb[:, b, :], yb[:, b, :], PS[:, 2 * b, :], ALU.mult))
                    residual(b, 5)

            def experts():
                layernorm(5)
                dve.wait_ge(S("ex_sig"), 1)

                def routing():
                    link(v.tensor_tensor(rt[:, 1, :], rt[:, 0, :], V("rbias"), ALU.add))
                    first_max(rt[:, 1, :], rt[:, 2, :], rt[:, 5, :], r8t[:, 0, :])
                    link(v.scalar_tensor_tensor(rt[:, 1, :], rt[:, 2, :], NEG, rt[:, 1, :], ALU.mult, ALU.add))
                    first_max(rt[:, 1, :], rt[:, 3, :], rt[:, 5, :], r8t[:, 0, :])
                    link(v.tensor_tensor(rt[:, 2, :], rt[:, 2, :], rt[:, 3, :], ALU.add))
                    link(v.tensor_tensor(rt[:, 4, :], rt[:, 2, :], rt[:, 0, :], ALU.mult))
                    link(v.tensor_reduce(r8t[:, 1, :], v3(rt[:, 4, :]), AX.X, ALU.add))
                    link(v.tensor_scalar(r8t[:, 2, :], r8t[:, 1, :], 1e-9, None, ALU.add))
                    link(v.reciprocal(r8t[:, 3, :], r8t[:, 2, :]))
                    link(v.tensor_scalar(r8t[:, 4, :], r8t[:, 1, :], 1e-9, None, ALU.is_gt))
                    link(v.tensor_tensor(r8t[:, 3, :], r8t[:, 3, :], r8t[:, 4, :], ALU.mult))
                    link(v.tensor_scalar(r8t[:, 4, :], r8t[:, 4, :], -0.5, 0.5, ALU.mult, ALU.add))
                    link(v.tensor_tensor(v3(rt[:, 4, :]), v3(rt[:, 4, :]),
                                         r8t[:, 3, :].unsqueeze(2).to_broadcast([128, 8, 8]), ALU.mult))
                    link(v.tensor_tensor(v3(rt[:, 2, :]), v3(rt[:, 2, :]),
                                         r8t[:, 4, :].unsqueeze(2).to_broadcast([128, 8, 8]), ALU.mult))
                    v.tensor_tensor(rt[:, 9, :], rt[:, 4, :], rt[:, 2, :], ALU.add).then_inc(S("ex_comb"), 1)

                routing()
                for n in range(20):
                    dve.wait_ge(S("ex_act"), n + 1)
                    dve.wait_ge(S("ex_up"), 2 * n + 2)
                    if n >= 4:
                        dve.wait_ge(S("ex_down"), n - 3)
                    v.tensor_tensor(PTB[:, n % 4, :], PTB[:, 4 + n % 4, :], PS[:, 4 + n % 2, :],
                                    ALU.mult).then_inc(S("ex_prod"), 1)
                for b in range(B):
                    dve.wait_ge(S("ex_down"), 19 + b)
                    v.scalar_tensor_tensor(xb[b], PS[:, b, :], tg[:, 6:7], xb[b], ALU.mult,
                                           ALU.add).then_inc(S("x_ready"), 1)


            def final_layer():
                v.memset(wk, 0.0).then_inc(S("sp_cleared"), 1)
                layernorm(7)

                def swap(r):
                    dve.wait_ge(S("d_pair"), r + 1)
                    if r >= 1:
                        dve.wait_ge(S("d_roped"), 2 * r)
                    for j in range(4):
                        v.tensor_tensor(den4[:, j, :], PS[32 * j:32 * j + 32, 2, :], C3("ropes", 0, 32),
                                        ALU.mult).then_inc(S("d_swap"), 1)

                def maxima(u):
                    dve.wait_ge(S("d_scores"), u + 1)
                    link(v.tensor_tensor(PS[:, 0:4, 384:512], PS[:, 0:4, 384:512],
                                         C3("causal").unsqueeze(1).to_broadcast([128, 4, 128]), ALU.add))
                    for t in range(TB):
                        ins = v.tensor_reduce(mxd[:, u % 2, t:t + 1], PS[:, t, (3 - t) * 128:512], AX.X, ALU.max)
                    ins.then_inc(S("d_max"), 1)

                def diagonal(u, k):
                    g = 4 * u + k
                    dve.wait_ge(S("d_probs"), g + 1)
                    blk = PTB[:, g % 4, k * 128:(k + 1) * 128]
                    v.scalar_tensor_tensor(blk, blk, BIG, C("tri"), ALU.min, ALU.mult).then_inc(S("d_masked"), 1)

                def take(u):
                    b, hd = divmod(u, NHD)
                    dve.wait_ge(S("d_weighed"), 4 * (u + 1))
                    z = hd % 2
                    v.tensor_copy(denr[:, u % 2, :], PS[64:65, 6, :])
                    v.tensor_copy(AVT[64 * z:64 * z + 64, b, hd // 2, :], PS[0:64, 6, :]).then_inc(S("d_taken"), 1)

                def recip(u):
                    b, hd = divmod(u, NHD)
                    dve.wait_ge(S("d_dens"), u + 1)
                    v.reciprocal(recd[:, b, :, hd], PS[:, 7, 0:TB]).then_inc(S("d_rec"), 1)

                def top(n):
                    if n == 0:
                        dve.wait_ge(S("sp_work"), 2)
                    link(v.max(m8[:], wk))
                    link(v.match_replace(wk, m8[:], wk, -BIG))

                NU = B * NHD
                swap(0)
                maxima(0)
                swap(1)
                for u in range(NU):
                    r, z = divmod(u, 2)
                    diagonal(u, 0)
                    diagonal(u, 1)
                    if z == 1 and r + 2 < NU // 2:
                        swap(r + 2)
                    if u + 1 < NU:
                        maxima(u + 1)
                    if u > 0:
                        recip(u - 1)
                    diagonal(u, 2)
                    diagonal(u, 3)
                    if u < SEL // 8:
                        top(u)
                    take(u)
                recip(NU - 1)

                v.tensor_scalar(wk, wk, -BIG, None, ALU.is_equal).then_inc(S("sp_selected"), 1)
                dve.wait_ge(S("sp_sel_cols"), 1)
                for b in range(B):
                    link(v.tensor_copy(selT[:, 0, :].rearrange("p (t n) -> p t n", t=TB)[:, :, 8 * b:8 * b + 8],
                                       PS[:, 0, 0:160].rearrange("p (t n) -> p t n", t=TB)[:, :, 32 * b:32 * b + 8]))
                link(v.memset(selT[:, 1, 0:16], 0.0))
                for t in range(1, TB):
                    ins = v.tensor_tensor(selT[:, 1, t * 16:t * 16 + 16], selT[:, 1, t * 16 - 16:t * 16],
                                          selT[:, 0, t * 16 - 16:t * 16], ALU.add)
                    if t < TB - 1:
                        link(ins)
                ins.then_inc(S("sp_prefix"), 1)
                dve.wait_ge(S("sp_cum"), 1)
                link(v.tensor_tensor(selT[:, 2, :], PS[:, 1, 0:64], selT[:, 0, :], ALU.mult))
                link(v.tensor_scalar(selT[:, 2, :], selT[:, 2, :], -1.0, None, ALU.add))
                for b in range(B):
                    for t in range(TB):
                        at = t * 16 + b * 8
                        v.tensor_tensor(PTB[:, 4 * b + t, :].rearrange("p (h s) -> p h s", h=8),
                                        C3("iota64").unsqueeze(1).to_broadcast([128, 8, 64]),
                                        selT[:, 2, at:at + 8].unsqueeze(2).to_broadcast([128, 8, 64]),
                                        ALU.is_equal).then_inc(S("sp_G"), 1)
                h64 = lambda t: t.rearrange("p (h s) -> p h s", h=8)
                for b in range(B):
                    dve.wait_ge(S("sp_angles"), b + 1)
                    v.tensor_copy(trig[:, 0, :], PS[0:32, 3, :])
                    v.tensor_copy(trig[:, 1, :], PS[32:64, 3, :]).then_inc(S("sp_trig"), 1)
                    dve.wait_ge(S("sp_trig"), b + 1)
                    dve.wait_ge(S("sp_qk"), b + 1)
                    for j in range(2):
                        link(v.tensor_tensor(trig[:, 2 + j, :], PS[32 * j:32 * j + 32, 1, :], trig[:, 1, :], ALU.mult))
                    dve.wait_ge(S("sp_qk_placed"), 2 * (b + 1))
                    link(v.tensor_tensor(sqk[0:32, :, :], sqk[0:32, :, :],
                                         trig[:, 0, :].unsqueeze(1).to_broadcast([32, 2, T]), ALU.mult))
                    v.tensor_tensor(sqk[0:32, :, :], sqk[0:32, :, :], trig[:, 2:4, :], ALU.add).then_inc(S("sp_roped"), 1)
                    dve.wait_ge(S("sp_scores"), b + 1)
                    link(v.tensor_tensor(h64(sdiff), h64(PS[0:64, 5, :]),
                                         C3("causal", 0, 64)[:, 0:64].unsqueeze(1).to_broadcast([64, 8, 64]), ALU.add))
                    link(v.tensor_reduce(sps[:, 1, :], h64(sdiff), AX.X, ALU.max))
                    v.tensor_tensor(h64(sdiff), h64(sdiff), sps[:, 1, :].unsqueeze(2).to_broadcast([64, 8, 64]),
                                    ALU.subtract).then_inc(S("sp_diff"), 1)
                    dve.wait_ge(S("sp_p"), b + 1)
                    link(v.tensor_reduce(sps[:, 2, :], h64(spp), AX.X, ALU.add))
                    link(v.reciprocal(sps[:, 2, :], sps[:, 2, :]))
                    dve.wait_ge(S("sp_gate"), b + 1)
                    v.tensor_tensor(sps[:, 3, :], sps[:, 2, :], sps[:, 0, :], ALU.mult).then_inc(S("sp_factor"), 1)
                    dve.wait_ge(S("sp_factor"), b + 1)
                    dve.wait_ge(S("sp_z"), b + 1)
                    if b:
                        dve.wait_ge(S("last_y"), b)
                    for z in range(2):
                        ins = v.tensor_tensor(
                            spz[64 * z:64 * z + 64, :, :].rearrange("p (a c) d -> p a c d", a=2),
                            PS[0:64, 0:2, :].rearrange("p a (c z d) -> p a c z d", c=2, z=2)[:, :, :, z, :],
                            sps[:, 3, :].rearrange("p (a c z) -> p a c z", a=2, c=2)[:, :, :, z].unsqueeze(3)
                            .to_broadcast([64, 2, 2, 128]), ALU.mult)
                    ins.then_inc(S("sp_zs"), 1)
                    for q in range(4):
                        n = 4 * b + q
                        if n >= 2:
                            dve.wait_ge(S("d_spread"), n - 1)
                        widen(wide[:, n % 2, :], recd[:, b, :, 2 * q:2 * q + 2], 64).then_inc(S("d_wide"), 1)
                        dve.wait_ge(S("d_spread"), n + 1)
                        v.tensor_tensor(AVT[:, b, q, :], AVT[:, b, q, :], PS[:, 4 + n % 2, :],
                                        ALU.mult).then_inc(S("d_normed"), 1)
                    dve.wait_ge(S("last_y"), b + 1)
                    v.scalar_tensor_tensor(xb[b], PS[:, 6 + b, :], tg[:, 7:8], xb[b], ALU.mult,
                                           ALU.add).then_inc(S("x_ready"), 1)
            arrived(dve, "cols", "const")
            link(v.tensor_tensor(small[:, 8:12], V("lq1"), V("lk1"), ALU.mult))
            v.tensor_reduce(small[:, 0:1], small[:, 8:12], AX.X, ALU.add).then_inc(S("lam_dots"), 1)
            dve.wait_ge(S("lam_dots"), 1)
            link(v.tensor_tensor(small[:, 8:12], V("lq2"), V("lk2"), ALU.mult))
            v.tensor_reduce(small[:, 1:2], small[:, 8:12], AX.X, ALU.add).then_inc(S("lam_dots"), 1)
            dve.wait_ge(S("gates"), 2)
            link(v.tensor_tensor(small[:, 4:5], small[:, 3:4], small[:, 2:3], ALU.subtract))
            link(v.tensor_scalar(small[:, 4:5], small[:, 4:5], -LAMBDA_INIT, None, ALU.add))
            link(v.tensor_scalar(small[:, 5:6], V("subln"), 1.0 - LAMBDA_INIT, None, ALU.mult))
            link(v.tensor_scalar(small[:, 6:7], V("mur"), -1.0, 1.0, ALU.mult, ALU.add))
            link(v.tensor_scalar(small[:, 7:8], V("muk"), -1.0, 1.0, ALU.mult, ALU.add))
            dve.wait_ge(S("gates"), 2)
            attention(0, 0, 0)
            moe()
            linear()
            rwkv()
            dve.wait_ge(S("pool_set"), POOL_SET["keep"])
            attention(1, 4, 2)
            experts()
            dve.wait_ge(S("pool_set"), POOL_SET["mask3"])
            attention(2, 6, 3)
            final_layer()

        @block.gpsimd
        def _(pool):
            g = nc.gpsimd

            def layernorm(i):
                for b in range(B):
                    pool.wait_ge(S("ln_veps"), 2 * i + b + 1)
                    g.tensor_tensor(rstd[:, b, :], veps[:, b, :], mhalf[:, 0:TB], ALU.pow).then_inc(S("ln_rstd"), 1)

            def attention(a, i):
                c = ATTN[a]
                nsub, nh, qd, mr = c["nsub"], c["nh"], c["qd"], c["mrow"]
                s_ = lambda n: S("at_" + n)
                pool.wait_ge(s_("k_placed"), before(a, "k_placed") + 1)
                if a == 1:
                    arrived(pool, "minus1")
                g.memset(QA if a == 0 else QA[mr:128, :, 0:nsub], 0.0).then_inc(s_("q_zeroed"), 1)
                pool.wait_ge(s_("q_zeroed"), before(a, "q_zeroed") + 1)
                km = C({0: "kmask4", 1: "kmask8", 2: "kmask16"}[a], qd)
                for b in range(B):
                    for s in range(nsub):
                        g.tensor_tensor(KA[a][0:qd, b, s, :].rearrange("p (n k) -> p n k", k=SK),
                                        kT[0:qd, s, b * SK:(b + 1) * SK].unsqueeze(1).to_broadcast([qd, nh, SK]),
                                        km.unsqueeze(2).to_broadcast([qd, nh, SK]), ALU.mult).then_inc(s_("k_built"), 1)
                layernorm(i)
                if a == 0:
                    for b in range(B):
                        pool.wait_ge(s_("rms_eps"), before(a, "rms_eps") + b + 1)
                        g.tensor_tensor(rmsr[:, b, :, :], rms[:, b, :].rearrange("p (t n) -> p t n", t=TB),
                                        mhalf[:].rearrange("p (t n) -> p t n", t=TB), ALU.pow).then_inc(s_("rms_r"), 1)


            def final_layer():
                layernorm(7)
                g.memset(VD[:, :, :, 64:65], 1.0).then_inc(S("pool_set"), 1)
                pool.wait_ge(S("pool_set"), POOL_SET["last"] - 6)
                for q in range(3):
                    g.memset(QK[q][64:128, 0:2, :], 0.0).then_inc(S("pool_set"), 1)
                    g.memset(QK[q][64:128, 2:4, :], -1.0).then_inc(S("pool_set"), 1)
                for r in range(B * NHD // 2):
                    qk = QK[r % 3][0:32]
                    pool.wait_ge(S("d_raw"), 4 * (r + 1))
                    g.tensor_tensor(qk, qk, C3("ropec", 0, 32).unsqueeze(1).to_broadcast([32, 4, T]),
                                    ALU.mult).then_inc(S("d_roped"), 1)
                    pool.wait_ge(S("d_roped"), 2 * r + 1)
                    pool.wait_ge(S("d_swap"), 4 * (r + 1))
                    g.tensor_tensor(qk, qk, den4[:], ALU.add).then_inc(S("d_roped"), 1)

            g.memset(keys[:, :], 0.0).then_inc(S("pool_set"), 1)
            g.memset(mhalf[:], -0.5).then_inc(S("pool_set"), 1)
            g.memset(hp[:, :, 0:1], 0.0).then_inc(S("pool_set"), 1)
            pool.wait_ge(S("pool_set"), 3)
            arrived(pool, "const")
            for a, one, nh in ((0, "vone8", 8), (2, "vone16", 4)):
                for b in range(B):
                    for z in range(2):
                        last = g.tensor_copy(VA[a][:, b, z, :, 64:64 + nh], C(one).rearrange("p (c n) -> p c n", n=nh))
                        last.then_inc(S("pool_set"), 1)
            attention(0, 0)
            g.iota(pool_iota[:], [[1, 1024]], base=0, channel_multiplier=0,
                   allow_small_or_imprecise_dtypes=True).then_inc(S("pool_set"), 1)
            layernorm(1)
            arrived(pool, "maskr", "maskq", "mask3")
            pool.wait_ge(S("moe_down"), E)
            g.tensor_scalar(keep, maskr[:], -1.0, 1.0, ALU.mult, ALU.add).then_inc(S("pool_set"), 1)
            g.tensor_scalar(mbias[:], maskq[:], NEG, None, ALU.mult).then_inc(S("pool_set"), 1)
            g.tensor_copy(mask3f[:], mask3).then_inc(S("pool_set"), 1)
            layernorm(2)
            layernorm(3)
            attention(1, 4)
            layernorm(5)
            attention(2, 6)
            final_layer()


def layout(i):
    f = np.float32
    A = {}
    A["xT"] = i["x"].reshape(N, D).T
    c = i["ctx_1024"].transpose(2, 0, 1)
    A["ctx"] = np.tile(c, (1, 1, 8)).reshape(D, -1)

    def pack(*ws):
        return np.concatenate([w for w in ws], 1)

    for l, o in ((0, "Wp"), (1, "Wo"), (2, "Wo"), (3, "Wo")):
        A[f"wa{l}"] = pack(*(i[f"L{l}_xattn_{n}"].T for n in ("Wq", "Wk", "Wv", o)))
    A["wf1"] = pack(*(i[f"L1_ffn_{n}"].T for n in ("W_r", "W_k", "W_v")))
    A["rw0"] = pack(i["L0_ffn_router_w"], i["L2_ffn_router_w"].T, i["L3_ffn_mosa_router_w"])
    A["w1"] = i["L0_ffn_w1"].transpose(1, 0, 2).reshape(D, -1)
    A["w2"] = i["L0_ffn_w2"].reshape(E, 4, 128, D).transpose(2, 0, 1, 3).reshape(128, -1)
    A["sw13"] = pack(i["L2_ffn_sw1"], i["L2_ffn_sw3"])
    A["sw2"] = i["L2_ffn_sw2"].reshape(2, 128, D).transpose(1, 0, 2).reshape(128, -1)
    A["ew1"] = i["L2_ffn_ew1"].transpose(1, 0, 2).reshape(D, -1)
    A["ew2"] = i["L2_ffn_ew2"].transpose(1, 0, 2).reshape(128, -1)
    swapped = np.r_[ROT // 2:ROT, 0:ROT // 2]
    w = i["L3_ffn_dense_wqkv"]
    q, k, v = w[:, :, 0:HP], w[:, :, HP:2 * HP], w[:, :, 2 * HP:]
    parts = []
    for p in range(0, NHD, 2):
        parts += [q[:, p], q[:, p + 1], k[:, p], k[:, p + 1], q[:, p][:, swapped], q[:, p + 1][:, swapped],
                  k[:, p][:, swapped], k[:, p + 1][:, swapped]]
    A["wd"] = pack(*parts, v.reshape(D, -1))
    w = i["L3_ffn_mosa_wqkv"]
    q, k, v = w[:, :, 0:HP], w[:, :, HP:2 * HP], w[:, :, 2 * HP:]
    A["wm"] = pack(*(t for n in range(8) for t in (q[:, n], k[:, n], q[:, n][:, swapped], k[:, n][:, swapped], v[:, n])))
    A["wod"] = i["L3_ffn_dense_wo"].reshape(4, 128, D).transpose(1, 0, 2).reshape(128, -1)
    A["wom"] = i["L3_ffn_mosa_wo"].reshape(8, 64, D).transpose(1, 0, 2).reshape(64, -1)
    cols = np.zeros((128, COLS["_"]), f)

    def put(name, a):
        lo, hi = COLS[name]
        cols[:a.shape[0], lo:hi] = a

    put("g", np.tile(np.concatenate([i["g_xattn"], i["g_ffn"]])[None], (128, 1)))
    for n in ("lq1", "lk1", "lq2", "lk2"):
        put(n, np.tile(i["L0_xattn_" + n][None], (128, 1)))
    put("subln", np.tile(i["L0_xattn_subln_w"], 16)[:, None])
    for name, key in (("bp", "L0_xattn_bp"), ("bo1", "L1_xattn_bo"), ("bo2", "L2_xattn_bo"), ("bo3", "L3_xattn_bo"),
                      ("bq1", "L1_xattn_bq"), ("mur", "L1_ffn_mu_r"), ("muk", "L1_ffn_mu_k")):
        put(name, i[key][:, None])
    for l in (2, 3):
        put(f"bq{l}", i[f"L{l}_xattn_bq"].reshape(2, 64).T)
        put(f"bk{l}", i[f"L{l}_xattn_bk"].reshape(2, 64).T)
    put("rbias", np.tile(i["L2_ffn_router_bias"][None], (128, 8)))
    A["cols"] = cols
    A["rows"] = np.concatenate([i["L1_xattn_bk"], i["L1_xattn_bv"], i["L2_xattn_bv"], i["L3_xattn_bv"]])[None]
    m = i["mask_1x1xSxS2_bk1"].reshape(T, SK)
    A["maskr"] = m.T[np.arange(5 * 128) % SK].reshape(5, 128, T).transpose(1, 0, 2).reshape(128, -1)
    A["maskq"] = m.reshape(TB, 128, SK).transpose(1, 0, 2).reshape(128, -1)
    A["mask3"] = np.tile(i["mask_BxSx1_ik1"].reshape(1, N), (128, 1))
    A.update(constants())
    return {k_: np.ascontiguousarray(a) for k_, a in A.items()}


def kernel(**inputs):
    import concourse.bacc as _bacc
    from concourse.bass_utils import run_bass_kernel_spmd as _run

    arrays = layout({k: np.asarray(a) for k, a in inputs.items()})
    nc = _bacc.Bacc("TRN2", target_bir_lowering=False, num_devices=1)
    A = {k: nc.dram_tensor(k + "_dram", a.shape, mybir.dt.from_np(a.dtype), kind="ExternalInput").ap()
         for k, a in arrays.items()}
    out = nc.dram_tensor("out_dram", (D, N), F32, kind="ExternalOutput").ap()
    build(nc, A, out)
    r = _run(nc, [{k + "_dram": a for k, a in arrays.items()}], core_ids=[0])
    y = r.results[0]["out_dram"]
    return np.ascontiguousarray(y.T).reshape(B, T, D)
```

```python
from contextlib import ExitStack

import numpy as np
import concourse.bass as bass
from concourse import mybir

F32 = mybir.dt.float32
I32 = mybir.dt.int32
U8 = mybir.dt.uint8
ALU = mybir.AluOpType
ACT = mybir.ActivationFunctionType
AX = mybir.AxisListType

D = 128
B = 2
T = 512
N = B * T
NT = N // 128
TB = T // 128
SK = 77
E = 8
CAP = N // E
F = 512
EPS = 1e-5
BIG = 3.0e38
NEG = -1.0e30
LAMBDA_INIT = 0.8 - 0.6 * float(np.exp(-0.3 * 4))

ATTN = [dict(layer=0, nsub=4, nh=8, qd=32, mrow=32, scale=0.5),
        dict(layer=2, nsub=2, nh=8, qd=64, mrow=64, scale=8 ** -0.5),
        dict(layer=3, nsub=2, nh=4, qd=64, mrow=64, scale=128 ** -0.5)]
for _c in ATTN:
    _c["rows"] = _c["nh"] * SK
    _c["chunks"] = [(c, min(128, _c["rows"] - c)) for c in range(0, _c["rows"], 128)]

KBANK = [4, 7, 6]
VBANK = [(6, 6), (2, 4), (2, 3)]

PREFETCHED = (1, 5, 7)


def centre_bank(i, b):
    return 5 if b and i in PREFETCHED else 2 * b


NHD = 8
HP = 64
ROT = 32
SEL = T // 8

FIRST_SPARSE = 4
SPARSE = [(0, "columns"), (0, "ranks")]
for _b in range(B):
    SPARSE += [(_b, s) for s in ("gather", "angles", "turn0", "swapped", "qk", "v", "turn1", "scores", "turn2",
                                 "weights", "turn3", "sums", "out0", "out1")]
SLOTS = SPARSE[:2] + [(0, None)] * 2 + SPARSE[2:16] + [(0, "y")] + SPARSE[16:]


def made(b, s):
    return SPARSE.index((b, s)) + 1


def slot(u, j):
    n = 3 * (u - FIRST_SPARSE) + j
    return SLOTS[n] if 0 <= n < len(SLOTS) else (0, None)


def signals(c):
    units = B * c["nsub"]
    parts = units * len(c["chunks"])
    first = B if c["layer"] == 0 else 0
    return dict(q_zeroed=1, keys=1, k_placed=1, values=B, v_placed=B, query=B if c["layer"] == 0 else units, q_placed=units,
                k_built=units, scores=units * TB, max_taken=units * TB, max_rows=units, max_placed=units,
                shifted=parts, probs=parts, weighed=parts, p_masked=parts if c["layer"] == 2 else 0, o_taken=units,
                dens=B, recs=B, rec_bcast=B * c["nsub"] // 2, normed=first, att_raw=first, att_sq=first, rms_ms=first, rms_eps=first, rms_r=first,
                rms_wide=first, rms_bcast=first, att_done=B, projected=B, y_placed=B)


POOL_SET = dict(ones=11, iota=12, keep=14, mask3=15, slots=19, last=24)


def before(a, name):
    return sum(signals(c)[name] for c in ATTN[:a])


def columns(*widths):
    at, out = 0, {}
    for name, w in widths:
        out[name] = (at, at + w)
        at += w
    out["_"] = at
    return out


CONST = columns(("ident", 128), ("center", 128), ("tri", 128), ("ones", 128), ("mean", 1),
                ("head8", 16), ("head8mean", 16), ("block8", 128), ("firstw", 64), ("slot0", 64),
                ("slotid", 8), ("vmask8", 320), ("vmask16", 192), ("vone8", 40), ("vone16", 12),
                ("kmask4", 8), ("kmask8", 8), ("kmask16", 4))
CONST3 = columns(("causal", 128), ("ropec", 512), ("ropes", 512), ("tab", 256), ("iota64", 64))
COLS = columns(("g", 8), ("lq1", 4), ("lk1", 4), ("lq2", 4), ("lk2", 4), ("subln", 1), ("bp", 1),
               ("bv2", 1), ("bv3", 1), ("bo1", 1), ("bo2", 1), ("bo3", 1), ("bq1", 1), ("mur", 1), ("muk", 1),
               ("bq2", 2), ("bk2", 2), ("bq3", 2), ("bk3", 2), ("rbias", 64))
ROWS = columns(("bk1", 128), ("bv1", 128))


def constants():
    c = np.zeros((128, CONST["_"]), np.float32)
    p = np.arange(128)

    def put(name, a):
        lo, hi = CONST[name]
        c[:a.shape[0], lo:hi] = a.reshape(a.shape[0], -1)

    put("ident", np.eye(128))
    put("center", np.eye(128) - 1.0 / D)
    put("tri", p[:, None] <= p[None, :])
    put("ones", np.ones((128, 128)))
    put("mean", np.full((128, 1), 1.0 / D))
    put("head8", p[:, None] // 8 == np.arange(16))
    put("head8mean", (p[:, None] // 8 == np.arange(16)) / 8.0)
    put("block8", p[:, None] // 8 == p[None, :] // 8)
    put("firstw", np.tile(8.0 - np.arange(8), (128, 8)))
    put("slot0", np.tile(CAP * np.arange(8.0), (128, 8)))
    put("slotid", p[:, None] + CAP * np.arange(8.0))
    r8 = p[:, None] + 128 * np.arange(5)
    r16 = p[:, None] + 128 * np.arange(3)
    f = np.arange(64)
    put("vmask8", r8[:, :, None] // SK == f // 8)
    put("vmask16", r16[:, :, None] // SK == f // 16)
    put("vone8", r8[:, :, None] // SK == np.arange(8))
    put("vone16", r16[:, :, None] // SK == np.arange(4))
    put("kmask4", np.arange(32)[:, None] // 4 == np.arange(8))
    put("kmask8", f[:, None] // 8 == np.arange(8))
    put("kmask16", f[:, None] // 16 == np.arange(4))

    d = np.zeros((128, CONST3["_"]), np.float32)

    def put3(name, a):
        lo, hi = CONST3[name]
        d[:a.shape[0], lo:hi] = a.reshape(a.shape[0], -1)

    put3("causal", np.where(p[None, :] > p[:, None], NEG, 0.0))
    half = ROT // 2
    inv = (10000.0 ** (-np.arange(half, dtype=np.float32) / half)).astype(np.float32)
    ang = (np.arange(T, dtype=np.float32)[:, None] * inv).astype(np.float32)
    cos, sin = np.cos(ang), np.sin(ang)
    cos2 = np.concatenate([cos, cos], 1)
    sin2 = np.concatenate([-sin, sin], 1)
    put3("ropec", cos2.T)
    put3("ropes", sin2.T)
    put3("tab", np.concatenate([cos2, sin2], 1).reshape(TB, 128, 64).transpose(1, 0, 2))
    put3("iota64", np.tile(np.arange(64.0), (128, 1)))

    def minus(nh, copies):
        m = np.zeros((nh, copies, nh, SK), np.float32)
        for h in range(nh):
            m[h, :, h] = -1.0
        return m.reshape(nh, -1)

    return {"const": c, "const3": d,
            "minus0": minus(8, 8), "minus1": minus(8, 4), "minus2": minus(4, 4)}


def build(nc, A, out):
    with ExitStack() as ctx:
        sems = {}

        def S(name):
            if name not in sems:
                sems[name] = ctx.enter_context(nc.semaphore(name))
            return sems[name]

        def sb(name, shape, dt=F32):
            return ctx.enter_context(nc.sbuf_tensor(name, shape, dt))

        PS = ctx.enter_context(nc.psum_tensor("PS", [128, 8, 512], F32))

        cst = sb("cst", [128, CONST["_"]])
        cst3 = sb("cst3", [128, CONST3["_"]])
        cols = sb("cols", [128, COLS["_"]])
        rows = sb("rows", [1, ROWS["_"]])
        x = sb("x", [128, N])
        ctxr = sb("ctxr", [128, B, 8 * SK])
        ctxf = ctxr[:].rearrange("p b k -> p (b k)")
        wa = sb("wa", [128, 4, 4, 128])
        wa0, wa1, wa2, wa3 = (wa[:, n] for n in range(4))
        wf1 = sb("wf1", [128, 3, 128])
        rw0 = sb("rw0", [128, 24])
        wmoe = sb("wmoe", [128, 2 * E * F])
        w1 = wmoe[:, 0:E * F].rearrange("p (e f) -> p e f", e=E)
        w2 = wmoe[:, E * F:2 * E * F].rearrange("p (e c d) -> p e c d", e=E, c=4)
        sw13 = sb("sw13", [128, 2, 256])
        sw2 = sb("sw2", [128, 2, 128])
        wlate = sb("wlate", [128, 3 * 512 + 512])
        ew1 = wlate[:, 0:1024].rearrange("p (e f) -> p e f", e=E)
        ew2 = wlate[:, 1024:2048].rearrange("p (e f) -> p e f", e=E)
        wd = sb("wd", [128, 3 * 512 + 512])
        wm = wlate
        wod = sb("wod", [128, 4, 128])
        wom = sb("wom", [64, 8, 128])
        maskr = sb("maskr", [128, 5, 512], U8)
        maskq = sb("maskq", [128, TB, SK], U8)
        mask3f = sb("mask3", [128, N])
        mask3 = mask3f[:].bitcast(I32)

        def C(name, p=128):
            lo, hi = CONST[name]
            return cst[0:p, lo:hi]

        def C3(name, p0=0, p=128):
            lo, hi = CONST3[name]
            return cst3[p0:p, lo:hi]

        def V(name, p=128, j=None):
            lo, hi = COLS[name]
            return cols[0:p, lo:hi] if j is None else cols[0:p, lo + j:lo + j + 1]

        def R(name):
            lo, hi = ROWS[name]
            return rows[0:1, lo:hi]

        ident = C("ident")

        sq = sb("sq", [128, B, T])
        xc = sb("xc", [128, B, T])
        veps = sb("veps", [128, B, TB])
        rstd = sb("rstd", [128, B, TB])
        mhalf = sb("mhalf", [128, 64])
        hp = sb("hp", [128, B, T + 1])
        h = [hp[:, b, 1:T + 1] for b in range(B)]
        tg = sb("tg", [128, 8])
        small = sb("small", [128, 16])
        kT = sb("kT", [64, 4, B * SK])
        keys = sb("keys", [128, 8 * 8 * SK])
        half_ = 4 * 8 * SK
        KA = [keys[:, :].rearrange("p (b s k) -> p b s k", b=B, s=4),
              keys[:, 0:half_].rearrange("p (b s k) -> p b s k", b=B, s=2),
              keys[:, half_:half_ + 4 * 4 * SK].rearrange("p (b s k) -> p b s k", b=B, s=2)]
        VD = [keys[:, n * 768:(n + 1) * 768] for n in range(6)] + [mask3f[:, 0:768], ctxf[:, 0:768]]
        va8 = sb("va8", [128, B, 2, 5, 72])
        VA = [va8, va8, sb("va16", [128, B, 2, 3, 68])]
        PTB = sb("PTB", [128, 8, T])
        QA = PTB[:].rearrange("p (b s) t -> p b s t", b=B)
        mx = sb("mx", [128, B, 4, TB, 8])
        PT = sb("PT", [128, 4, T])
        OT = sb("OT", [128, B, 2, T])
        G = OT[:].rearrange("p b z t -> p b (z t)")
        qf = OT[:, 0]
        den4 = sb("den4", [32, 4, T])
        den = den4[0:8]
        rec = sb("rec", [128, B, TB, 32])
        att = sb("att", [128, B, T])
        rms = sb("rms", [128, B, 64])
        rmsr = sb("rmsr", [128, B, TB, 16])
        yb = sb("yb", [128, B, T])
        keep = wmoe[:, E * F:E * F + 5 * T].rearrange("p (c t) -> p c t", c=5)
        mbias = sb("mbias", [128, TB, SK])
        sm = wmoe[:, 0:4 * 308].rearrange("p (n k) -> p n k", n=2)
        pool_iota = sb("pool_iota", [128, 1024])
        htok = sb("htok", [128, NT, 128])
        wider = htok[:].rearrange("p (z t) f -> p z (t f)", z=2)
        r8t = sb("r8t", [128, 10, 8])
        ein = PT[:, 2:4].rearrange("p a t -> p (a t)")
        hid = PT[:, 0:2]
        eo = sb("eo", [128, 2, 128])
        destb = sq[:].rearrange("p b t -> p (b t)")
        gateb = xc[:].rearrange("p b t -> p (b t)")
        kf = sb("kf", [SK, B, 128])
        vs = sb("vs", [SK, B, 128])
        kvm = sb("kvm", [128, B, 128])
        ksh = sb("ksh", [128, B, 16])
        rt = sb("rt", [128, 10, 64])
        QK = [wmoe[:, 0:4 * T].rearrange("p (j t) -> p j t", j=4),
              wmoe[:, 4 * T:8 * T].rearrange("p (j t) -> p j t", j=4), PTB[:, 4:8]]
        AVT = wmoe[:, 8 * T:16 * T].rearrange("p (b n t) -> p b n t", b=B, n=4)
        GT = [sq[:, 0, :], sq[:, 1, :], xc[:, 0, :], xc[:, 1, :]]
        xg = att[:, 0, :]
        sqk = OT[0:64, 0]
        spv = OT[0:64, 1]
        spp = att[0:64, 1, :]
        spo = yb[0:64, 0, :]
        sdiff = yb[0:64, 1, :]
        sps = sb("sps", [64, 4, 8])
        trig = wa[0:32].rearrange("p n a d -> p n (a d)")
        spz = rt[:, 0:8, :].rearrange("p (q a) c -> p q (a c)", q=4)
        mxd = sb("mxd", [128, 2, TB])
        recd = sb("recd", [128, TB, 2])
        dend = pool_iota[:].rearrange("p (r t) -> p r t", r=2)
        wide = sw13[:].rearrange("p a t -> p (a t)")
        wk = yb[0:40, 0, :]
        m8 = sb("m8", [40, 8])
        selT = sb("selT", [128, 3, 64])

        block = ctx.enter_context(nc.Block())

        loads = [[("xT", x[:]), ("const", cst[:])],
                 [("wa0", wa0), ("ctx", ctxr[:]), ("cols", cols[:]), ("minus0", keys[32:40, :])],
                 [("rw0", rw0[:]), ("w1", wmoe[:, 0:E * F]), ("w2", wmoe[:, E * F:2 * E * F])],
                 [("rows", rows[:]), ("wa1", wa1), ("wf1", wf1[:])],
                 [("wa2", wa2), ("minus1", keys[64:72, 0:half_]), ("maskr", maskr[:]), ("maskq", maskq[:]),
                  ("mask3", mask3)],
                 [("sw13", sw13[:]), ("sw2", sw2[:]), ("ew1", wlate[:, 0:1024]), ("ew2", wlate[:, 1024:2048])],
                 [("wa3", wa3), ("minus2", keys[64:68, half_:half_ + 16 * SK])],
                 [("const3", cst3[:]), ("wd", wd[:]), ("wod", wod[:]), ("wom", wom[:])],
                 [("wm", wm[:])]]
        lot = {name: n for n, group in enumerate(loads) for name, _ in group}

        @block.sync
        def _(sp):
            for n, group in enumerate(loads):
                if n == lot["wm"]:
                    sp.wait_ge(S("x_ready"), 2 * 6)
                if n == lot["minus1"]:
                    sp.wait_ge(S("x_ready"), 2)
                for name, dst in group:
                    if name == "minus0":
                        sp.wait_ge(S("pool_set"), 1)
                    shape, src = dst.shape, A[name]
                    if len(shape) == 3:
                        src = src.rearrange("p (a b) -> p a b", a=shape[1])
                    elif len(shape) == 4:
                        src = src.rearrange("p (a b c) -> p a b c", a=shape[1], b=shape[2])
                    sp.dma_start(dst, src).then_inc(S(f"loaded_{n}"), 16)
            for b in range(B):
                sp.wait_ge(S("x_ready"), 2 * 8 + b + 1 - 2)
                sp.dma_start(out[:, b * T:(b + 1) * T], x[:, b * T:(b + 1) * T]).then_inc(S("stored"), 16)
            sp.wait_ge(S("stored"), 16 * B)

        def arrived(eng, *names):
            for n in sorted({lot[name] for name in names}):
                eng.wait_ge(S(f"loaded_{n}"), 16 * len(loads[n]))

        class Chain:

            def __init__(self, eng, name):
                self.eng, self.name, self.n = eng, name, 0

            def __call__(self, ins):
                self.n += 1
                ins.then_inc(S(self.name), 1)
                self.eng.wait_ge(S(self.name), self.n)

        xb = [x[:, b * T:(b + 1) * T] for b in range(B)]

        @block.tensor
        def _(pe):
            def mm(o, l, r, start=True, stop=True):
                return nc.tensor.matmul(o, l, r, start=start, stop=stop, skip_group_check=True)

            def ln_centre(i, b):
                if i > 0:
                    pe.wait_ge(S("x_ready"), 2 * i + b - 1)
                elif b == 0:
                    arrived(pe, "xT", "const")
                mm(PS[:, centre_bank(i, b), :], C("center"), xb[b]).then_inc(S("ln_centered"), 1)

            def ln_variance(i, b):
                pe.wait_ge(S("ln_act"), 2 * (2 * i + b) + 1)
                for t in range(TB):
                    last = mm(PS[:, 2 * b + 1, t:t + 1], sq[:, b, t * 128:(t + 1) * 128], C("mean"))
                last.then_inc(S("ln_var"), 1)

            def ln_spread(i, b):
                pe.wait_ge(S("ln_rstd"), 2 * i + b + 1)
                for t in range(TB):
                    last = nc.tensor.transpose(PS[:, 2 * b + 1, t * 128:(t + 1) * 128],
                                               rstd[:, b, t:t + 1].to_broadcast([128, 128]), ident)
                last.then_inc(S("ln_bcast"), 1)

            def layernorm(i):
                for part in (ln_centre, ln_variance, ln_spread):
                    for b in range(B):
                        part(i, b)

            def context(a, w, vbias):
                c = ATTN[a]
                nsub, qd, chunks = c["nsub"], c["qd"], c["chunks"]
                s_ = lambda n: S("at_" + n)
                arrived(pe, *(["ctx", "wa0"] if a == 0 else [f"wa{c['layer']}"]))
                for s in range(nsub):
                    last = mm(PS[0:qd, KBANK[a] + s // 2, (s % 2) * 154:(s % 2) * 154 + 154], w[:, 1, s * qd:(s + 1) * qd],
                              ctxr[:, :, 0:SK])
                if vbias:
                    last = mm(PS[:, KBANK[a], 400:401], w[:, 3, :], V(vbias))
                last.then_inc(s_("keys"), 1)
                for b in range(B):
                    if b == 1 and a == 0:
                        pe.wait_ge(s_("v_placed"), 1)
                    for j, (c0, m) in enumerate(chunks):
                        o = PS[0:m, VBANK[a][b] + j // 4, (j % 4) * 128:(j % 4) * 128 + 128]
                        last = mm(o, ctxr[:, b, c0:c0 + m], w[:, 2, :])
                    last.then_inc(s_("values"), 1)

            def attention(a, i, w):
                c = ATTN[a]
                nsub, nh, qd, mr = c["nsub"], c["nh"], c["qd"], c["mrow"]
                chunks = c["chunks"]
                s_ = lambda n: S("at_" + n)
                if a == 0:
                    context(0, w, None)
                layernorm(i)
                pe.wait_ge(s_("k_placed"), before(a, "k_placed") + 1)
                for b in range(B):
                    pe.wait_ge(S("ln_h"), 2 * i + b + 1)
                    if a == 0:
                        mm(PS[:, 4 + b, :], w[:, 0, :], h[b]).then_inc(s_("query"), 1)
                    else:
                        if b == 1:
                            pe.wait_ge(s_("v_placed"), before(a, "v_placed") + 2)
                        for s in range(nsub):
                            mm(PS[0:qd, 4 + 2 * b + s, :], w[:, 0, s * qd:(s + 1) * qd], h[b]).then_inc(s_("query"), 1)
                units = [(b, s) for b in range(B) for s in range(nsub)]
                arrived(pe, f"minus{a}")
                pe.wait_ge(S("pool_set"), POOL_SET["ones"])
                pe.wait_ge(s_("q_zeroed"), before(a, "q_zeroed") + 1)

                def scores(u):
                    b, s = units[u]
                    if s == 0:
                        pe.wait_ge(s_("k_built"), before(a, "k_built") + nsub * (b + 1))
                        pe.wait_ge(s_("q_placed"), before(a, "q_placed") + nsub * (b + 1))
                    for t in range(TB):
                        n = TB * u + t
                        if n >= 2:
                            pe.wait_ge(s_("max_taken"), before(a, "max_taken") + n - 1)
                        for j in range(c["rows"] // 308):
                            last = mm(PS[:, 2 * (n % 2) + j, 0:308], QA[:, b, s, t * 128:(t + 1) * 128],
                                      KA[a][:, b, s, j * 308:(j + 1) * 308])
                        last.then_inc(s_("scores"), 1)

                def maxima(u):
                    b, s = units[u]
                    pe.wait_ge(s_("max_taken"), before(a, "max_taken") + TB * (u + 1))
                    if u == 0:
                        pe.wait_ge(s_("q_placed"), before(a, "q_placed") + nsub * B)
                    for name, n in cleared(u):
                        pe.wait_ge(s_(name), before(a, name) + n)
                    for t in range(TB):
                        last = nc.tensor.transpose(PS[0:nh, 7, t * 128:(t + 1) * 128], mx[:, b, s, t, 0:nh], ident)
                    last.then_inc(s_("max_rows"), 1)

                def cleared(u):
                    if u in (0, 1) or u <= nsub:
                        return []
                    return {(0, 5): [("recs", 1)], (0, 6): [("rms_eps", 1)], (0, 7): [("rms_eps", 1)],
                            (1, 3): [("recs", 1)], (2, 3): [("recs", 1)]}[a, u]

                def weigh(u):
                    b, s = units[u]
                    nc_ = len(chunks)
                    pe.wait_ge(s_("max_placed"), before(a, "max_placed") + u + 1)

                    def pv(j):
                        g = u * nc_ + j
                        m = chunks[j][1]
                        pe.wait_ge(s_("p_masked" if a == 1 else "probs"), before(a, "p_masked" if a == 1 else "probs") + g + 1)
                        if j == 0 and u > 0:
                            pe.wait_ge(s_("o_taken"), before(a, "o_taken") + u)
                        last = mm(PS[0:64 + nh, 6, :], VA[a][0:m, b, s % 2, j, :], PT[0:m, g % 4, :],
                                  start=(j == 0), stop=(j == nc_ - 1))
                        last.then_inc(s_("weighed"), 1)

                    for j, (c0, m) in enumerate(chunks):
                        g = u * nc_ + j
                        if g >= 2:
                            pe.wait_ge(s_("probs"), before(a, "probs") + g - 1)
                        mm(PS[0:m, 4 + g % 2, :], KA[a][:, b, s, c0:c0 + m],
                           QA[:, b, s, :]).then_inc(s_("shifted"), 1)
                        if j >= 1:
                            pv(j - 1)
                        if j == 2 and u + 1 < len(units):
                            maxima(u + 1)
                        elif j >= 1:
                            step()
                    pv(nc_ - 1)
                    if nc_ == 3:
                        step()

                def dens(b):
                    if b == 1:
                        pe.wait_ge(s_("y_placed"), before(a, "y_placed") + 1)
                    pe.wait_ge(s_("o_taken"), before(a, "o_taken") + nsub * (b + 1))
                    pe.wait_ge(s_("max_placed"), before(a, "max_placed") + min(nsub * (b + 1) + 1, len(units)))
                    for t in range(TB):
                        for s in range(nsub):
                            at = t * 32 + s * nh
                            last = nc.tensor.transpose(PS[:, 7, at:at + nh], den[0:nh, s, t * 128:(t + 1) * 128],
                                                       ident[0:nh, 0:nh])
                    last.then_inc(s_("dens"), 1)

                def spread(b, z):
                    if z == 0:
                        pe.wait_ge(s_("recs"), before(a, "recs") + b + 1)
                    else:
                        pe.wait_ge(s_("normed"), before(a, "normed") + b + 1)
                    if z == 0:
                        pe.wait_ge(s_("max_placed"), before(a, "max_placed") + placed(b))
                    for t in range(TB):
                        last = nc.tensor.transpose(PS[:, 7, t * 128:(t + 1) * 128],
                                                   wider[:, z, t * 128:(t + 1) * 128], ident)
                    last.then_inc(s_("rec_bcast"), 1)

                def placed(b):
                    return min(unit[0] + 1, len(units))

                def mean_squares(b):
                    pe.wait_ge(s_("att_sq"), before(a, "att_sq") + b + 1)
                    for t in range(TB):
                        last = mm(PS[:, 7, t * 16:(t + 1) * 16], sq[:, b, t * 128:(t + 1) * 128], C("head8mean"))
                    last.then_inc(s_("rms_ms"), 1)

                def rms_spread(b):
                    pe.wait_ge(s_("rms_wide"), before(a, "rms_wide") + b + 1)
                    pe.wait_ge(s_("max_placed"), before(a, "max_placed") + placed(b))
                    for t in range(TB):
                        last = nc.tensor.transpose(PS[:, 7, t * 128:(t + 1) * 128],
                                                   wider[:, 0, t * 128:(t + 1) * 128], ident)
                    last.then_inc(s_("rms_bcast"), 1)

                def project(b):
                    pe.wait_ge(s_("att_done"), before(a, "att_done") + b + 1)
                    mm(PS[:, 7, :], w[:, 3, :], att[:, b, :]).then_inc(s_("projected"), 1)

                def ending(b):
                    yield lambda: dens(b)
                    yield lambda: spread(b, 0)
                    if a == 0:
                        yield lambda: spread(b, 1)
                        yield lambda: mean_squares(b)
                        if b == 0:
                            for _ in range(3):
                                yield lambda: None
                        yield lambda: rms_spread(b)
                    yield lambda: project(b)

                todo, unit = [], [0]

                def step():
                    if todo:
                        todo.pop(0)()

                scores(0)
                maxima(0)
                for u in range(len(units)):
                    if u + 1 < len(units):
                        scores(u + 1)
                    unit[0] = u + 1
                    weigh(u)
                    if units[u][1] == nsub - 1:
                        todo += ending(units[u][0])
                ln_centre(i + 1, 0)
                step()
                ln_variance(i + 1, 0)
                step()
                ln_spread(i + 1, 0)
                while todo:
                    step()
                pe.wait_ge(s_("y_placed"), before(a, "y_placed") + B)

            def moe():
                arrived(pe, "rw0")
                for b in range(B):
                    if b == 0:
                        ln_centre(1, 1)
                    else:
                        ln_variance(1, 1)
                        ln_spread(1, 1)
                    pe.wait_ge(S("ln_h"), 2 + b + 1)
                    for t in range(TB):
                        n = b * TB + t
                        nc.tensor.transpose(PS[:, 4 + b, t * 128:(t + 1) * 128], h[b][:, t * 128:(t + 1) * 128], ident)
                        last = mm(PS[:, 6, n * 8:n * 8 + 8], h[b][:, t * 128:(t + 1) * 128], rw0[:, 0:8])
                    last.then_inc(S("moe_logits"), 1)
                pe.wait_ge(S("moe_htok"), 2)
                context(1, wa2, "bv2")
                pe.wait_ge(S("at_k_placed"), 2)
                pe.wait_ge(S("moe_prefix"), 1)
                mm(PS[:, 7, 0:64], C("tri"), rt[:, 3, :], stop=False)
                mm(PS[:, 7, 0:64], C("ones"), rt[:, 4, :], start=False).then_inc(S("moe_cum"), 1)
                for t in range(NT):
                    pe.wait_ge(S("moe_G"), t + 1)
                    for k in range(2):
                        last = mm(PS[:, k, :], htok[:, t, :], G[:, t % 2, k * 512:(k + 1) * 512],
                                  start=(t == 0), stop=(t == NT - 1))
                    last.then_inc(S("moe_gathered"), 1)
                pe.wait_ge(S("at_v_placed"), 4)
                context(2, wa3, "bv3")
                pe.wait_ge(S("at_k_placed"), 3)
                for t in range(NT):
                    last = nc.tensor.transpose(PS[:, 4 + t // 4, (t % 4) * 128:(t % 4) * 128 + 128],
                                               r8t[:, 5, t:t + 1].to_broadcast([128, 128]), ident)
                last.then_inc(S("moe_slots"), 1)
                for t in range(NT):
                    last = nc.tensor.transpose(PS[:, 6 + t // 4, (t % 4) * 128:(t % 4) * 128 + 128],
                                               r8t[:, 6, t:t + 1].to_broadcast([128, 128]), ident)
                last.then_inc(S("moe_slots"), 1)
                arrived(pe, "w1", "w2")
                pe.wait_ge(S("at_v_placed"), 6)
                pe.wait_ge(S("moe_ein"), 2)
                pe.wait_ge(S("moe_bcopied"), 4)

                def up(e):
                    if e >= 2:
                        pe.wait_ge(S("moe_gelu"), e - 1)
                    for f in range(4):
                        last = mm(PS[:, 4 + e % 2, f * 128:(f + 1) * 128], w1[:, e, f * 128:(f + 1) * 128],
                                  ein[:, e * CAP:(e + 1) * CAP])
                    last.then_inc(S("moe_up"), 1)

                def down(e):
                    pe.wait_ge(S("moe_gelu"), e + 1)
                    if e >= 2:
                        pe.wait_ge(S("moe_eo"), e - 1)
                    for f in range(4):
                        last = mm(PS[:, 6 + e % 2, 0:128], hid[:, e % 2, f * 128:(f + 1) * 128], w2[:, e, f, :],
                                  start=(f == 0), stop=(f == 3))
                    last.then_inc(S("moe_down"), 1)

                def combine(e):
                    pe.wait_ge(S("moe_eo"), e + 1)
                    pe.wait_ge(S("moe_GT"), e + 1)
                    for k in range(2):
                        last = mm(PS[:, 2 + k, :], eo[:, e % 2, :], G[:, e % 2, k * 512:(k + 1) * 512],
                                  start=(e == 0), stop=(e == E - 1))
                    last.then_inc(S("moe_combined"), 1)

                up(0)
                for e in range(E):
                    if e + 1 < E:
                        up(e + 1)
                    if e >= 1:
                        combine(e - 1)
                    down(e)
                combine(E - 1)

            def linear():
                arrived(pe, "rows", "wa1")
                for b in range(B):
                    for j, bias in ((1, "bk1"), (2, "bv1")):
                        o = PS[0:SK, 4, (j - 1) * 256 + b * 128:(j - 1) * 256 + b * 128 + 128]
                        mm(o, ctxr[:, b, 0:SK], wa1[:, j, :], stop=False)
                        last = mm(o, C("ones", 1)[:, 0:SK], R(bias), start=False)
                last.then_inc(S("lin_kv"), 1)
                layernorm(2)
                pe.wait_ge(S("lin_kf"), 1)
                for b in range(B):
                    mm(PS[:, 5, b * 128:(b + 1) * 128], kf[:, b, :], vs[:, b, :])
                    last = mm(PS[:, 5, 256 + b * 16:256 + b * 16 + 16], kf[:, b, :], C("ones", SK)[:, 0:16])
                last.then_inc(S("lin_sum"), 1)
                for b in range(B):
                    pe.wait_ge(S("ln_h"), 2 * 2 + b + 1)
                    mm(PS[:, 6 + b, :], wa1[:, 0, :], h[b]).then_inc(S("lin_q"), 1)
                pe.wait_ge(S("lin_kvm"), 1)
                for b in range(B):
                    pe.wait_ge(S("lin_qf"), b + 1)
                    for t in range(TB):
                        mm(PS[:, 4 + b, t * 16:t * 16 + 16], qf[:, b, :][:, t * 128:(t + 1) * 128], ksh[:, b, :])
                    mm(PS[:, 2 * b, :], kvm[:, b, :], qf[:, b, :]).then_inc(S("lin_num"), 1)
                for b in range(B):
                    pe.wait_ge(S("lin_rec"), b + 1)
                    for t in range(TB):
                        last = nc.tensor.transpose(PS[:, 2 * b + 1, t * 128:(t + 1) * 128],
                                                   xc[:, b, t * 128:(t + 1) * 128], ident)
                    last.then_inc(S("lin_bcast"), 1)
                for b in range(B):
                    pe.wait_ge(S("lin_att"), b + 1)
                    mm(PS[:, 6 + b, :], wa1[:, 3, :], att[:, b, :]).then_inc(S("lin_proj"), 1)

            def rwkv():
                layernorm(3)
                arrived(pe, "wf1")
                for b in range(B):
                    pe.wait_ge(S("mix_in"), 2 * b + 1)
                    mm(PS[:, 4 + 2 * b, :], wf1[:, 0, :], xc[:, b, :]).then_inc(S("mix_up"), 1)
                    pe.wait_ge(S("mix_in"), 2 * b + 2)
                    mm(PS[:, 5 + 2 * b, :], wf1[:, 1, :], sq[:, b, :]).then_inc(S("mix_up"), 1)
                for b in range(B):
                    pe.wait_ge(S("mix_k2"), b + 1)
                    mm(PS[:, 2 * b, :], wf1[:, 2, :], att[:, b, :]).then_inc(S("mix_v"), 1)

            def experts():
                arrived(pe, "sw13", "sw2", "ew1", "ew2")

                def ups(n):
                    j, b = divmod(n, 2)
                    if n >= 2:
                        pe.wait_ge(S("ex_act"), n - 1)
                        pe.wait_ge(S("ex_prod"), n - 1)
                    if j < 2:
                        mm(PS[:, 2 + n % 2, :], sw13[:, 0, j * 128:(j + 1) * 128], h[b]).then_inc(S("ex_up"), 1)
                        mm(PS[:, 4 + n % 2, :], sw13[:, 1, j * 128:(j + 1) * 128], h[b]).then_inc(S("ex_up"), 1)
                    else:
                        e = j - 2
                        mm(PS[:, 2 + n % 2, :], ew1[:, e, :], h[b]).then_inc(S("ex_up"), 1)
                        for t in range(TB):
                            at = (b * TB + t) * 8 + e
                            last = nc.tensor.transpose(PS[:, 4 + n % 2, t * 128:(t + 1) * 128],
                                                       rt[:, 9, at:at + 1].to_broadcast([128, 128]), ident)
                        last.then_inc(S("ex_up"), 1)

                def downs(n):
                    j, b = divmod(n, 2)
                    pe.wait_ge(S("ex_prod"), n + 1)
                    w = sw2[:, j, :] if j < 2 else ew2[:, j - 2, :]
                    mm(PS[:, b, :], w, PTB[:, n % 4, :], start=(j == 0), stop=(j == 9)).then_inc(S("ex_down"), 1)

                def logits(b):
                    for t in range(TB):
                        n = b * TB + t
                        last = mm(PS[:, 6, n * 8:n * 8 + 8], h[b][:, t * 128:(t + 1) * 128], rw0[:, 8:16])
                    return last

                pe.wait_ge(S("ln_h"), 2 * 5 + 1)
                ln_centre(5, 1)
                logits(0)
                ln_variance(5, 1)
                ups(0)
                ln_spread(5, 1)
                pe.wait_ge(S("ln_h"), 2 * 5 + 2)
                logits(1).then_inc(S("ex_logits"), 1)
                for n in range(1, 21):
                    if n == 4:
                        pe.wait_ge(S("ex_comb"), 1)
                    if n < 20:
                        ups(n)
                    downs(n - 1)


            def final_layer():
                arrived(pe, "const3", "wd")

                def prepare(r):
                    b, p = divmod(r, 4)
                    for j in range(3):
                        last = mm(PS[:, j, :], wd[:, p * 384 + j * 128:p * 384 + (j + 1) * 128], h[b])
                    last.then_inc(S("d_pair"), 1)

                def router(b):
                    mm(PS[0:8, 4 + b, :], rw0[:, 16:24], h[b]).then_inc(S("sp_router"), 1)
                    for t in range(TB):
                        last = nc.tensor.transpose(PS[:, 6 + b, t * 128:(t + 1) * 128], h[b][:, t * 128:(t + 1) * 128],
                                                   ident)
                    last.then_inc(S("sp_tokens"), 1)

                def values(n):
                    b, t = divmod(n, TB)
                    mm(PS[:, 6 + n % 2, :], h[b][:, t * 128:(t + 1) * 128], wd[:, 1536:2048]).then_inc(S("d_values"), 1)

                def scores(u):
                    r, z = divmod(u, 2)
                    if u == 0:
                        pe.wait_ge(S("d_first"), 2)
                    else:
                        pe.wait_ge(S("d_roped"), 2 * (r + 1))
                        pe.wait_ge(S("d_max"), u)
                    for t in reversed(range(TB)):
                        if t == TB - 2:
                            pe.wait_ge(S("d_swap"), 4 * min(r + 2, NU // 2))
                            pe.wait_ge(S("d_raw"), 4 * min(r + 2, NU // 2))
                            if z == 1 and r >= 2:
                                pe.wait_ge(S("d_normed"), r - 1)
                        last = mm(PS[:, t, (3 - t) * 128:512], QK[r % 3][0:64, z, t * 128:(t + 1) * 128],
                                  QK[r % 3][0:64, 2 + z, 0:(t + 1) * 128])
                    last.then_inc(S("d_scores"), 1)

                def maxima(u):
                    pe.wait_ge(S("d_max"), u + 1)
                    for t in range(TB):
                        last = nc.tensor.transpose(PS[0:1, 3, t * 128:(t + 1) * 128], mxd[:, u % 2, t:t + 1], ident)
                    last.then_inc(S("d_max_row"), 1)

                def shifted(u, k):
                    r, z = divmod(u, 2)
                    g = 4 * u + k
                    if k == 0:
                        pe.wait_ge(S("d_max_placed"), u + 1)
                    if g >= 2:
                        pe.wait_ge(S("d_probs"), g - 1)
                    mm(PS[:, 4 + g % 2, k * 128:512], QK[r % 3][:, 2 + z, k * 128:(k + 1) * 128],
                       QK[r % 3][:, z, k * 128:512]).then_inc(S("d_shifted"), 1)

                def weigh(u, k):
                    b, hd = divmod(u, NHD)
                    g = 4 * u + k
                    pe.wait_ge(S("d_masked"), g + 1)
                    if k == 0 and u > 0:
                        pe.wait_ge(S("d_taken"), u)
                        pe.wait_ge(S("d_den"), u)
                    at = hd // 2 * 192 + hd % 2 * 64
                    mm(PS[:, 6, k * 128:512], VD[b * TB + k][:, at:at + 128], PTB[:, g % 4, k * 128:512],
                       start=(k == 0), stop=(k == 3)).then_inc(S("d_weighed"), 1)

                def dens(p):
                    if p == NU // 2 - 1:
                        pe.wait_ge(S("d_den"), NU)
                    for t in range(TB):
                        last = mm(PS[:, 0, 2 * t:2 * t + 2], dend[:, p % 2, t * 128:(t + 1) * 128], ident[:, 0:128:64])
                    last.then_inc(S("d_dens"), 1)

                def spread(p):
                    pe.wait_ge(S("d_wide"), p + 1)
                    for t in range(TB):
                        last = nc.tensor.transpose(PS[:, 1, t * 128:(t + 1) * 128], wide[:, t * 128:(t + 1) * 128], ident)
                    last.then_inc(S("d_spread"), 1)

                def sparse(b, s):
                    if s is None:
                        return
                    if (b, s) == (1, "gather"):
                        pe.wait_ge(S("x_ready"), 2 * 7 + 1)
                    elif s != "columns":
                        pe.wait_ge(S("sp_taken"), made(b, s) - 1 if s != "y" else made(b, "out1"))
                    heads = [slice(hd * 64, hd * 64 + 64) for hd in range(8)]
                    if s == "columns":
                        pe.wait_ge(S("sp_selected"), 1)
                        for t in range(TB):
                            last = nc.tensor.transpose(PS[:, 7, t * 40:t * 40 + 40], wk[:, t * 128:(t + 1) * 128],
                                                       ident[0:40, 0:40])
                    elif s == "ranks":
                        mm(PS[:, 7, 0:64], C("tri"), selT[:, 0, :], stop=False)
                        last = mm(PS[:, 7, 0:64], C("ones"), selT[:, 1, :], start=False)
                    elif s == "gather":
                        pe.wait_ge(S("sp_G"), TB * (b + 1))
                        for t in range(TB):
                            last = mm(PS[:, 7, :], htok[:, b * TB + t, :], PT[:, t, :], start=(t == 0), stop=(t == TB - 1))
                    elif s == "angles":
                        for t in range(TB):
                            last = mm(PS[0:64, 7, :], C3("tab")[:, t * 64:(t + 1) * 64], PT[:, t, :], start=(t == 0),
                                      stop=(t == TB - 1))
                    elif s[:4] == "turn":
                        q = int(s[4:])
                        for t in range(TB):
                            last = nc.tensor.transpose(PS[:, 7, t * 128:(t + 1) * 128], PT[:, t, q * 128:(q + 1) * 128],
                                                       ident)
                    elif s == "swapped":
                        for hd, hs in enumerate(heads):
                            mm(PS[64:128, 7, hd:hd + 1], xg[:, hs], rw0[:, 16 + hd:17 + hd])
                        for hd, hs in enumerate(heads):
                            last = mm(PS[0:64, 7, hs], wm[:, hd * 256 + 128:hd * 256 + 192], xg[:, hs])
                    elif s == "qk":
                        pe.wait_ge(S("sp_gate"), b + 1)
                        for hd, hs in enumerate(heads):
                            last = mm(PS[:, 7, hs], wm[:, hd * 256:hd * 256 + 128], xg[:, hs])
                    elif s == "v":
                        for hd, hs in enumerate(heads):
                            last = mm(PS[0:64, 7, hs], xg[:, hs], wm[:, hd * 256 + 192:hd * 256 + 256])
                    elif s == "scores":
                        pe.wait_ge(S("sp_roped"), b + 1)
                        for hs in heads:
                            last = mm(PS[0:64, 7, hs], sqk[:, 0, hs], sqk[:, 1, hs])
                    elif s == "weights":
                        pe.wait_ge(S("sp_p"), b + 1)
                        for hs in heads:
                            last = nc.tensor.transpose(PS[0:64, 7, hs], spp[:, hs], ident[0:64, 0:64])
                    elif s == "sums":
                        for hs in heads:
                            last = mm(PS[0:64, 7, hs], spv[:, 0, hs], spv[:, 1, hs])
                    elif s in ("out0", "out1"):
                        for j in range(4):
                            hd = 4 * int(s[-1]) + j
                            last = mm(PS[0:64, 7, j * 128:(j + 1) * 128], spo[:, heads[hd]], wom[:, hd, :])
                    elif s == "y":
                        pe.wait_ge(S("d_normed"), NHD // 2 * (b + 1))
                        for q in range(4):
                            mm(PS[:, 7, :], wod[:, q, :], AVT[:, b, q, :], start=(q == 0), stop=False)
                        for q in range(4):
                            last = mm(PS[:, 7, :], spz[:, q, :], GT[q], start=False, stop=(q == 3))
                    last.then_inc(S("last_y" if s == "y" else "sp_product"), 1)

                NU = B * NHD
                pe.wait_ge(S("ln_h"), 2 * 7 + 1)
                prepare(0)
                ln_centre(7, 1)
                router(0)
                ln_variance(7, 1)
                for n in range(TB):
                    if n == 0:
                        pe.wait_ge(S("sp_htok"), 1)
                    if n == 2:
                        ln_spread(7, 1)
                    if n >= 2:
                        pe.wait_ge(S("d_v_placed"), n - 1)
                    values(n)
                pe.wait_ge(S("ln_h"), 2 * 7 + 2)
                pe.wait_ge(S("d_v_placed"), TB)
                router(1)
                pe.wait_ge(S("d_raw"), 4)
                pe.wait_ge(S("d_swap"), 4)
                prepare(1)
                values(4)
                pe.wait_ge(S("sp_htok"), 2)
                values(5)
                scores(0)
                for n in (6, 7):
                    pe.wait_ge(S("d_v_placed"), n - 1)
                    values(n)
                pe.wait_ge(S("pool_set"), POOL_SET["slots"])
                maxima(0)
                for u in range(NU):
                    r, z = divmod(u, 2)
                    shifted(u, 0)
                    shifted(u, 1)
                    if u + 1 < NU:
                        scores(u + 1)
                    if u == 0:
                        pe.wait_ge(S("d_v_placed"), NT)
                        pe.wait_ge(S("pool_set"), POOL_SET["last"])
                    weigh(u, 0)
                    if u == FIRST_SPARSE:
                        arrived(pe, "wm", "wod", "wom")
                    sparse(*slot(u, 0))
                    weigh(u, 1)
                    shifted(u, 2)
                    shifted(u, 3)
                    if u + 1 < NU:
                        maxima(u + 1)
                    if z == 1 and r > 0:
                        dens(r - 1)
                    sparse(*slot(u, 1))
                    if z == 0 and r + 2 < NU // 2:
                        prepare(r + 2)
                    weigh(u, 2)
                    weigh(u, 3)
                    if z == 1 and r > 0:
                        spread(r - 1)
                    sparse(*slot(u, 2))
                pe.wait_ge(S("d_normed"), NU // 2 - 1)
                dens(NU // 2 - 1)
                spread(NU // 2 - 1)
                sparse(1, "y")
            attention(0, 0, wa0)
            moe()
            linear()
            rwkv()
            attention(1, 4, wa2)
            experts()
            attention(2, 6, wa3)
            final_layer()

        @block.scalar
        def _(act):
            A_ = nc.scalar.activation

            def ln_squares(i, b):
                act.wait_ge(S("ln_centered"), 2 * i + b + 1)
                A_(sq[:, b, :], PS[:, centre_bank(i, b), :], ACT.Square).then_inc(S("ln_act"), 1)
                nc.scalar.copy(xc[:, b, :], PS[:, centre_bank(i, b), :]).then_inc(S("ln_act"), 1)

            def layernorm(i):
                for b in range(B):
                    ln_squares(i, b)

            def context(a, kbias, kfunc, obias):
                c = ATTN[a]
                nsub, qd = c["nsub"], c["qd"]
                s_ = lambda n: S("at_" + n)
                act.wait_ge(s_("keys"), before(a, "keys") + 1)
                if a > 0:
                    act.wait_ge(s_("k_built"), before(a, "k_built"))
                    A_(small[:, 11 + a:12 + a], PS[:, KBANK[a], 400:401], ACT.Identity, bias=V(obias))
                for s in range(nsub):
                    src = PS[0:qd, KBANK[a] + s // 2, (s % 2) * 154:(s % 2) * 154 + 154]
                    dst = kT[0:qd, s, :]
                    if a > 0:
                        last = A_(dst, src, kfunc, bias=V(kbias, qd, s))
                    else:
                        last = nc.scalar.copy(dst, src)
                last.then_inc(s_("k_placed"), 1)

            def attention(a, i, qbias):
                c = ATTN[a]
                nsub, nh, qd, mr = c["nsub"], c["nh"], c["qd"], c["mrow"]
                s_ = lambda n: S("at_" + n)
                if a == 0:
                    context(0, None, None, None)
                layernorm(i)
                act.wait_ge(s_("q_zeroed"), before(a, "q_zeroed") + 1)
                for b in range(B):
                    for s in range(nsub):
                        if a == 0:
                            act.wait_ge(s_("query"), before(a, "query") + b + 1)
                            nc.scalar.copy(QA[0:qd, b, s, :],
                                           PS[s * qd:(s + 1) * qd, 4 + b, :]).then_inc(s_("q_placed"), 1)
                        else:
                            act.wait_ge(s_("query"), before(a, "query") + nsub * b + s + 1)
                            A_(QA[0:qd, b, s, :], PS[0:qd, 4 + 2 * b + s, :], ACT.Identity,
                               bias=V(qbias, qd, s)).then_inc(s_("q_placed"), 1)
                units = [(b, s) for b in range(B) for s in range(nsub)]
                chunks = c["chunks"]

                def place(u):
                    b, s = units[u]
                    act.wait_ge(s_("max_rows"), before(a, "max_rows") + u + 1)
                    nc.scalar.copy(QA[mr:mr + nh, b, s, :], PS[0:nh, 7, :]).then_inc(s_("max_placed"), 1)

                def square(b):
                    act.wait_ge(s_("att_raw"), before(a, "att_raw") + b + 1)
                    A_(sq[:, b, :], att[:, b, :], ACT.Square).then_inc(s_("att_sq"), 1)

                def root(b):
                    if b == 1:
                        act.wait_ge(s_("rms_eps"), 2)
                        A_(rmsr[:, b, :, :], rms[:, b, :].rearrange("p (t n) -> p t n", t=TB),
                           ACT.Sqrt).then_inc(s_("rms_r"), 1)

                def project(b):
                    act.wait_ge(s_("projected"), before(a, "projected") + b + 1)
                    A_(yb[:, b, :], PS[:, 7, :], ACT.Identity,
                       bias=V("bp") if a == 0 else small[:, 11 + a:12 + a]).then_inc(s_("y_placed"), 1)

                todo = []

                def step():
                    if todo:
                        todo.pop(0)()

                nothing = lambda: None
                place(0)
                for u, (b, s) in enumerate(units):
                    for j, (c0, m) in enumerate(chunks):
                        g = u * len(chunks) + j
                        act.wait_ge(s_("shifted"), before(a, "shifted") + g + 1)
                        if g >= 4:
                            act.wait_ge(s_("weighed"), before(a, "weighed") + g - 3)
                        A_(PT[0:m, g % 4, :], PS[0:m, 4 + g % 2, :], ACT.Exp,
                           scale=c["scale"]).then_inc(s_("probs"), 1)
                        if j == 2 and u + 1 < len(units):
                            place(u + 1)
                        elif j >= 1:
                            step()
                    if len(chunks) == 3:
                        step()
                    if s == nsub - 1:
                        if a == 0:
                            todo += [nothing, nothing, lambda b=b: square(b), lambda b=b: root(b)]
                            todo += [nothing] * (4 if b == 0 else 1) + [lambda b=b: project(b)]
                        else:
                            todo += [nothing, nothing, lambda b=b: project(b)]
                ln_squares(i + 1, 0)
                while todo:
                    step()

            def moe():
                ln_squares(1, 1)
                for b in range(B):
                    act.wait_ge(S("moe_logits"), b + 1)
                    nc.scalar.copy(htok[:, b * TB:(b + 1) * TB, :],
                                   PS[:, 4 + b, :].rearrange("p (t f) -> p t f", t=TB)).then_inc(S("moe_htok"), 1)
                act.wait_ge(S("moe_diff"), 1)
                A_(rt[:, 2, :], rt[:, 1, :], ACT.Exp).then_inc(S("moe_exp"), 1)
                context(1, "bk2", ACT.Identity, "bo2")
                context(2, "bk3", ACT.Tanh, "bo3")
                act.wait_ge(S("moe_slots"), 1)
                for k in range(2):
                    nc.scalar.copy(destb[:, k * 512:(k + 1) * 512], PS[:, 4 + k, :]).then_inc(S("moe_bcopied"), 1)
                act.wait_ge(S("moe_slots"), 2)
                for k in range(2):
                    nc.scalar.copy(gateb[:, k * 512:(k + 1) * 512], PS[:, 6 + k, :]).then_inc(S("moe_bcopied"), 1)
                for e in range(E):
                    act.wait_ge(S("moe_up"), e + 1)
                    if e >= 2:
                        act.wait_ge(S("moe_down"), e - 1)
                    A_(hid[:, e % 2, :], PS[:, 4 + e % 2, :], ACT.Gelu_apprx_tanh).then_inc(S("moe_gelu"), 1)

            def linear():
                layernorm(2)
                for b in range(B):
                    act.wait_ge(S("lin_num"), b + 1)
                    nc.scalar.copy(yb[:, b, :], PS[:, 2 * b, :]).then_inc(S("lin_numc"), 1)
                for b in range(B):
                    act.wait_ge(S("lin_proj"), b + 1)
                    act.wait_ge(S("lin_att"), b + 1)
                    A_(yb[:, b, :], PS[:, 6 + b, :], ACT.Identity, bias=V("bo1")).then_inc(S("lin_y"), 1)

            def rwkv():
                layernorm(3)
                for b in range(B):
                    act.wait_ge(S("mix_up"), 2 * b + 1)
                    A_(yb[:, b, :], PS[:, 4 + 2 * b, :], ACT.Sigmoid).then_inc(S("mix_act"), 1)
                    act.wait_ge(S("mix_up"), 2 * b + 2)
                    A_(PTB[:, b, :], PS[:, 5 + 2 * b, :], ACT.Relu).then_inc(S("mix_act"), 1)

            def experts():
                ln_squares(5, 1)
                act.wait_ge(S("ex_logits"), 1)
                A_(rt[:, 0, :], PS[:, 6, 0:64], ACT.Sigmoid).then_inc(S("ex_sig"), 1)
                for n in range(20):
                    act.wait_ge(S("ex_up"), 2 * n + 1)
                    if n >= 4:
                        act.wait_ge(S("ex_prod"), n - 3)
                    A_(PTB[:, 4 + n % 4, :], PS[:, 2 + n % 2, :],
                       ACT.Silu if n < 4 else ACT.Gelu).then_inc(S("ex_act"), 1)


            def final_layer():
                def pair(r, j):
                    act.wait_ge(S("d_pair"), r + 1)
                    if r >= 3:
                        act.wait_ge(S("d_shifted"), 8 * (r - 2))
                    for z in range(2):
                        nc.scalar.copy(QK[r % 3][0:64, 2 * j + z, :],
                                       PS[64 * z:64 * z + 64, j, :]).then_inc(S("d_raw"), 1)

                def router(b):
                    act.wait_ge(S("sp_router"), b + 1)
                    nc.scalar.copy(wk[32 * b:32 * b + 8, :], PS[0:8, 4 + b, :]).then_inc(S("sp_work"), 1)
                    act.wait_ge(S("sp_tokens"), b + 1)
                    nc.scalar.copy(htok[:, b * TB:(b + 1) * TB, :],
                                   PS[:, 6 + b, :].rearrange("p (t f) -> p t f", t=TB)).then_inc(S("sp_htok"), 1)

                def values(n):
                    act.wait_ge(S("d_values"), n + 1)
                    nc.scalar.copy(VD[n].rearrange("p (q c d) -> p q c d", q=4, c=3)[:, :, 0:3:2, :],
                                   PS[:, 6 + n % 2, :].rearrange("p (q c d) -> p q c d", q=4, c=2)
                                   ).then_inc(S("d_v_placed"), 1)

                def max_row(u):
                    r, z = divmod(u, 2)
                    act.wait_ge(S("d_max_row"), u + 1)
                    nc.scalar.copy(QK[r % 3][64:65, z, :], PS[0:1, 3, :]).then_inc(S("d_max_placed"), 1)

                def sparse(b, s):
                    if s in ("gather", "v", "weights", "sums") or s and s[:4] == "turn":
                        out, p = {"gather": (xg, 128), "v": (spv[:, 0, :], 64), "weights": (spv[:, 1, :], 64),
                                  "sums": (spo, 64)}.get(s) or (GT[int(s[4:])], 128)
                        act.wait_ge(S("sp_product"), made(b, s))
                        nc.scalar.copy(out, PS[0:p, 7, :]).then_inc(S("sp_taken"), 1)
                    elif s == "qk":
                        act.wait_ge(S("sp_product"), made(b, s))
                        nc.scalar.copy(sqk[:, 0, :], PS[0:64, 7, :])
                        nc.scalar.copy(sqk[:, 1, :], PS[64:128, 7, :]).then_inc(S("sp_taken"), 1)
                    elif s == "swapped":
                        act.wait_ge(S("sp_product"), made(b, s))
                        A_(sps[:, 0, :], PS[64:128, 7, 0:8], ACT.Exp, scale=-1.0).then_inc(S("sp_gate"), 1)
                    elif s == "scores":
                        act.wait_ge(S("sp_diff"), b + 1)
                        A_(spp, sdiff, ACT.Exp, scale=HP ** -0.5).then_inc(S("sp_p"), 1)

                NU = B * NHD
                pair(0, 0)
                pair(0, 1)
                ln_squares(7, 1)
                act.wait_ge(S("sp_cleared"), 1)
                router(0)
                for n in range(TB):
                    values(n)
                router(1)
                pair(1, 0)
                pair(1, 1)
                for n in range(TB, NT):
                    values(n)
                act.wait_ge(S("pool_set"), POOL_SET["slots"])
                max_row(0)
                for u in range(NU):
                    r, z = divmod(u, 2)
                    for k in range(4):
                        g = 4 * u + k
                        act.wait_ge(S("d_shifted"), g + 1)
                        if g >= 4:
                            act.wait_ge(S("d_weighed"), g - 3)
                        A_(PTB[:, g % 4, k * 128:512], PS[:, 4 + g % 2, k * 128:512], ACT.Exp,
                           scale=HP ** -0.5).then_inc(S("d_probs"), 1)
                        if k == 1:
                            sparse(*slot(u, 0))
                    if u == 0:
                        act.wait_ge(S("pool_set"), POOL_SET["last"])
                    if u + 1 < NU:
                        max_row(u + 1)
                    sparse(*slot(u, 1))
                    if z == 0 and r + 2 < NU // 2:
                        pair(r + 2, 0)
                        pair(r + 2, 1)
                    act.wait_ge(S("d_weighed"), 4 * (u + 1))
                    if z == 0 and r >= 2:
                        act.wait_ge(S("d_dens"), r - 1)
                    nc.scalar.copy(dend[64 * z:64 * z + 64, r % 2, :],
                                   PS[64 - 64 * z:128 - 64 * z, 6, :]).then_inc(S("d_den"), 1)
                    sparse(*slot(u, 2))
            arrived(act, "cols")
            A_(tg[:], V("g"), ACT.Tanh).then_inc(S("gates"), 1)
            act.wait_ge(S("lam_dots"), 2)
            A_(small[:, 2:4], small[:, 0:2], ACT.Exp).then_inc(S("gates"), 1)
            attention(0, 0, None)
            moe()
            linear()
            rwkv()
            attention(1, 4, "bq2")
            experts()
            attention(2, 6, "bq3")
            final_layer()

        @block.vector
        def _(dve):
            link = Chain(dve, "dve_own")
            v = nc.vector

            def ln_eps(i, b):
                dve.wait_ge(S("ln_var"), 2 * i + b + 1)
                v.tensor_scalar(veps[:, b, :], PS[:, 2 * b + 1, 0:TB], EPS, None, ALU.add).then_inc(S("ln_veps"), 1)

            def ln_scale(i, b):
                k = 2 * i + b + 1
                dve.wait_ge(S("ln_bcast"), k)
                dve.wait_ge(S("ln_act"), 2 * k)
                v.tensor_tensor(h[b], xc[:, b, :], PS[:, 2 * b + 1, :], ALU.mult).then_inc(S("ln_h"), 1)

            def layernorm(i):
                for part in (ln_eps, ln_scale):
                    for b in range(B):
                        part(i, b)

            def widen(dst, src, width):
                n = src.shape[2]
                return v.tensor_copy(dst.rearrange("p (t n w) -> p t n w", t=TB, n=n),
                                     src.unsqueeze(3).to_broadcast([128, TB, n, width]))

            def residual(b, gate):
                v.scalar_tensor_tensor(xb[b], yb[:, b, :], tg[:, gate:gate + 1], xb[b], ALU.mult,
                                       ALU.add).then_inc(S("x_ready"), 1)

            def context(a):
                c = ATTN[a]
                nh, chunks = c["nh"], c["chunks"]
                s_ = lambda n: S("at_" + n)
                vm = C("vmask8" if nh == 8 else "vmask16").rearrange("p (c f) -> p c f", f=64)
                full = [j for j, (_, m) in enumerate(chunks) if m == 128]
                for b in range(B):
                    dve.wait_ge(s_("values"), before(a, "values") + b + 1)
                    for z in range(2):
                        n = len(full)
                        v.tensor_tensor(VA[a][:, b, z, 0:n, 0:64],
                                        PS[:, VBANK[a][b], 0:n * 128].rearrange("p (c f) -> p c f", f=128)[:, :, z * 64:z * 64 + 64],
                                        vm[:, 0:n, :], ALU.mult)
                        m = chunks[-1][1]
                        at = (n % 4) * 128 + z * 64
                        last = v.tensor_tensor(VA[a][0:m, b, z, n, 0:64], PS[0:m, VBANK[a][b] + n // 4, at:at + 64], vm[0:m, n, :],
                                               ALU.mult)
                    last.then_inc(s_("v_placed"), 1)

            def attention(a, i, layer):
                c = ATTN[a]
                nsub, nh, qd = c["nsub"], c["nh"], c["qd"]
                chunks = c["chunks"]
                s_ = lambda n: S("at_" + n)
                if a == 0:
                    context(0)
                layernorm(i)
                units = [(b, s) for b in range(B) for s in range(nsub)]

                def maxima(u):
                    b, s = units[u]
                    for t in range(TB):
                        n = TB * u + t
                        dve.wait_ge(s_("scores"), before(a, "scores") + n + 1)
                        nb = c["rows"] // 308
                        src = PS[:, 2 * (n % 2):2 * (n % 2) + nb, 0:308].rearrange("p j (h k) -> p j h k", k=SK)
                        if a == 1:
                            dst = sm[:, n % 2, :].rearrange("p (j h k) -> p j h k", j=2, k=SK)
                            for j in range(2):
                                ins = v.tensor_tensor(dst[:, j], src[:, j],
                                                      mbias[:, t, :].unsqueeze(1).to_broadcast([128, 4, SK]), ALU.add)
                            link(ins)
                            src = dst
                        v.tensor_reduce(mx[:, b, s, t, 0:nh].rearrange("p (j h) -> p j h", h=4), src, AX.X, ALU.max).then_inc(s_("max_taken"), 1)

                def take(u):
                    b, s = units[u]
                    for j, (c0, m) in enumerate(chunks):
                        if a == 1:
                            g = u * len(chunks) + j
                            dve.wait_ge(s_("probs"), before(a, "probs") + g + 1)
                            v.scalar_tensor_tensor(PT[0:m, g % 4, :], PT[0:m, g % 4, :], BIG, keep[0:m, j, :],
                                                   ALU.min, ALU.mult).then_inc(s_("p_masked"), 1)
                        if j >= 1 and not (j == 2 and u + 1 < len(units)):
                            step()
                    if len(chunks) == 3:
                        step()
                    dve.wait_ge(s_("weighed"), before(a, "weighed") + len(chunks) * (u + 1))
                    z = s % 2
                    v.tensor_copy(OT[64 * z:64 * z + 64, b, s // 2, :], PS[0:64, 6, :])
                    v.tensor_copy(den[0:nh, s, :], PS[64:64 + nh, 6, :]).then_inc(s_("o_taken"), 1)

                def reciprocals(b):
                    dve.wait_ge(s_("dens"), before(a, "dens") + b + 1)
                    link(v.reciprocal(rec[:, b, :, 0:nsub * nh],
                                      PS[:, 7, 0:128].rearrange("p (t n) -> p t n", t=TB)[:, :, 0:nsub * nh]))
                    for z in range(nsub // 2):
                        ins = widen(wider[:, z, :], rec[:, b, :, 2 * z * nh:2 * (z + 1) * nh], 64 // nh)
                    ins.then_inc(s_("recs"), 1)

                def normalise(b):
                    dve.wait_ge(s_("rec_bcast"), before(a, "rec_bcast") + nsub // 2 * b + 1)
                    if a == 0:
                        v.tensor_tensor(OT[:, b, 0, :], OT[:, b, 0, :], PS[:, 7, :], ALU.mult).then_inc(s_("normed"), 1)
                        dve.wait_ge(s_("normed"), before(a, "normed") + b + 1)
                    else:
                        v.tensor_tensor(att[:, b, :], OT[:, b, 0, :], PS[:, 7, :], ALU.mult).then_inc(s_("att_done"), 1)

                def combine(b):
                    dve.wait_ge(s_("rec_bcast"), before(a, "rec_bcast") + 2 * b + 2)
                    link(v.tensor_tensor(OT[:, b, 1, :], OT[:, b, 1, :], PS[:, 7, :], ALU.mult))
                    v.scalar_tensor_tensor(att[:, b, :], OT[:, b, 1, :], small[:, 4:5], OT[:, b, 0, :],
                                           ALU.mult, ALU.add).then_inc(s_("att_raw"), 1)

                def root(b):
                    dve.wait_ge(s_("rms_ms"), before(a, "rms_ms") + b + 1)
                    if b == 0:
                        v.tensor_scalar(rms[:, b, :], PS[:, 7, 0:64], EPS, None, ALU.add).then_inc(s_("rms_eps"), 1)
                    else:
                        link(v.tensor_scalar(rms[:, b, :], PS[:, 7, 0:64], EPS, None, ALU.add))
                        v.reciprocal(rms[:, b, :], rms[:, b, :]).then_inc(s_("rms_eps"), 1)

                def repeat(b):
                    dve.wait_ge(s_("rms_r"), before(a, "rms_r") + b + 1)
                    widen(wider[:, 0, :], rmsr[:, b, :, :], 8).then_inc(s_("rms_wide"), 1)

                def scale(b):
                    dve.wait_ge(s_("rms_bcast"), before(a, "rms_bcast") + b + 1)
                    v.scalar_tensor_tensor(att[:, b, :], att[:, b, :], small[:, 5:6], PS[:, 7, :], ALU.mult,
                                           ALU.mult).then_inc(s_("att_done"), 1)

                def add(b):
                    dve.wait_ge(s_("y_placed"), before(a, "y_placed") + b + 1)
                    if a == 2:
                        link(v.tensor_tensor(yb[:, b, :], yb[:, b, :], mask3f[:, b * T:(b + 1) * T], ALU.mult))
                    residual(b, layer)

                todo = []

                def step():
                    if todo:
                        todo.pop(0)()

                maxima(0)
                for u, (b, s) in enumerate(units):
                    if u + 1 < len(units):
                        maxima(u + 1)
                    take(u)
                    if s == nsub - 1:
                        if a == 0:
                            idle = [lambda b: None] * 2 if b == 0 else []
                            todo += [lambda f=f, b=b: f(b) for f in
                                     [reciprocals, normalise, combine, root] + idle + [repeat, scale, add]]
                        else:
                            todo += [lambda f=f, b=b: f(b) for f in (reciprocals, normalise, add)]
                step()
                ln_eps(i + 1, 0)
                step()
                ln_scale(i + 1, 0)
                while todo:
                    step()

            def first_max(vals, out_, tmp, m):
                v3 = lambda t: t.rearrange("p (t e) -> p t e", e=8)
                link(v.tensor_reduce(m, v3(vals), AX.X, ALU.max))
                link(v.tensor_tensor(v3(tmp), v3(vals), m.unsqueeze(2).to_broadcast([128, 8, 8]), ALU.is_equal))
                link(v.tensor_tensor(tmp, tmp, C("firstw"), ALU.mult))
                link(v.tensor_reduce(m, v3(tmp), AX.X, ALU.max))
                link(v.tensor_tensor(v3(out_), v3(tmp), m.unsqueeze(2).to_broadcast([128, 8, 8]), ALU.is_equal))

            v3 = lambda t: t.rearrange("p (t e) -> p t e", e=8)

            def moe():
                ln_eps(1, 1)
                ln_scale(1, 1)
                dve.wait_ge(S("moe_logits"), 2)
                link(v.tensor_copy(rt[:, 0, :], PS[:, 6, 0:64]))
                link(v.tensor_reduce(r8t[:, 0, :], v3(rt[:, 0, :]), AX.X, ALU.max))
                v.tensor_tensor(v3(rt[:, 1, :]), v3(rt[:, 0, :]), r8t[:, 0, :].unsqueeze(2).to_broadcast([128, 8, 8]),
                                ALU.subtract).then_inc(S("moe_diff"), 1)
                first_max(rt[:, 0, :], rt[:, 3, :], rt[:, 5, :], r8t[:, 1, :])
                link(v.memset(rt[:, 4, 0:8], 0.0))
                for t in range(1, NT):
                    ins = v.tensor_tensor(rt[:, 4, t * 8:t * 8 + 8], rt[:, 4, t * 8 - 8:t * 8], rt[:, 3, t * 8 - 8:t * 8],
                                          ALU.add)
                    if t < NT - 1:
                        link(ins)
                ins.then_inc(S("moe_prefix"), 1)
                dve.wait_ge(S("moe_exp"), 1)
                link(v.tensor_reduce(r8t[:, 7, :], v3(rt[:, 2, :]), AX.X, ALU.add))
                link(v.reciprocal(r8t[:, 6, :], r8t[:, 7, :]))
                dve.wait_ge(S("moe_cum"), 1)
                link(v.tensor_tensor(rt[:, 6, :], PS[:, 7, 0:64], rt[:, 3, :], ALU.mult))
                link(v.tensor_reduce(r8t[:, 2, :], v3(rt[:, 6, :]), AX.X, ALU.add))
                link(v.tensor_tensor(rt[:, 7, :], C("slot0"), rt[:, 3, :], ALU.mult))
                link(v.tensor_reduce(r8t[:, 3, :], v3(rt[:, 7, :]), AX.X, ALU.add))
                link(v.tensor_scalar(r8t[:, 4, :], r8t[:, 2, :], float(CAP), 4096.0, ALU.is_gt, ALU.mult))
                link(v.tensor_tensor(r8t[:, 4, :], r8t[:, 4, :], r8t[:, 3, :], ALU.add))
                link(v.scalar_tensor_tensor(r8t[:, 5, :], r8t[:, 2, :], -1.0, r8t[:, 4, :], ALU.add, ALU.add))
                dve.wait_ge(S("pool_set"), POOL_SET["iota"])
                for t in range(NT):
                    if t >= 2:
                        dve.wait_ge(S("moe_gathered"), t - 1)
                    if t == 2:
                        context(1)
                    v.tensor_scalar(G[:, t % 2, :], pool_iota[:], r8t[:, 5, t:t + 1], None,
                                    ALU.is_equal).then_inc(S("moe_G"), 1)
                dve.wait_ge(S("moe_gathered"), NT)
                for k in range(2):
                    v.tensor_copy(ein[:, k * 512:(k + 1) * 512], PS[:, k, :]).then_inc(S("moe_ein"), 1)
                context(2)
                dve.wait_ge(S("moe_bcopied"), 4)
                for e in range(E):
                    if e >= 2:
                        dve.wait_ge(S("moe_combined"), e - 1)
                    v.tensor_scalar(G[:, e % 2, :], destb[:], C("slotid")[:, e:e + 1], None,
                                    ALU.is_equal).then_inc(S("moe_GT"), 1)
                    dve.wait_ge(S("moe_down"), e + 1)
                    v.tensor_copy(eo[:, e % 2, :], PS[:, 6 + e % 2, 0:128]).then_inc(S("moe_eo"), 1)
                dve.wait_ge(S("moe_combined"), E)
                for b in range(B):
                    link(v.tensor_tensor(yb[:, b, :], gateb[:, b * T:(b + 1) * T], PS[:, 2 + b, :], ALU.mult))
                    residual(b, 4)

            def linear():
                dve.wait_ge(S("lin_kv"), 1)
                link(v.tensor_scalar(kf[:], PS[0:SK, 4, 0:256].rearrange("p (b f) -> p b f", b=B), 8 ** -0.5, 0.0,
                                     ALU.mult, ALU.max))
                link(v.tensor_scalar(kf[:], kf[:], 1e-6, None, ALU.add))
                v.tensor_copy(vs[:], PS[0:SK, 4, 256:512].rearrange("p (b f) -> p b f", b=B)).then_inc(S("lin_kf"), 1)
                layernorm(2)
                dve.wait_ge(S("lin_sum"), 1)
                v.tensor_tensor(kvm[:], PS[:, 5, 0:256].rearrange("p (b f) -> p b f", b=B),
                                C("block8").unsqueeze(1).to_broadcast([128, B, 128]), ALU.mult)
                v.tensor_tensor(ksh[:], PS[:, 5, 256:288].rearrange("p (b f) -> p b f", b=B),
                                C("head8").unsqueeze(1).to_broadcast([128, B, 16]), ALU.mult).then_inc(S("lin_kvm"), 1)
                for b in range(B):
                    dve.wait_ge(S("lin_q"), b + 1)
                    link(v.tensor_scalar(qf[:, b, :], PS[:, 6 + b, :], V("bq1"), 8 ** -0.5, ALU.add, ALU.mult))
                    v.tensor_scalar(qf[:, b, :], qf[:, b, :], 0.0, 1e-6, ALU.max, ALU.add).then_inc(S("lin_qf"), 1)
                for b in range(B):
                    dve.wait_ge(S("lin_num"), b + 1)
                    link(v.tensor_scalar(rms[:, b, :], PS[:, 4 + b, 0:64], 1e-8, None, ALU.add))
                    link(v.reciprocal(rmsr[:, b, :, :], rms[:, b, :].rearrange("p (t n) -> p t n", t=TB)))
                    widen(xc[:, b, :], rmsr[:, b, :, :], 8).then_inc(S("lin_rec"), 1)
                for b in range(B):
                    dve.wait_ge(S("lin_bcast"), b + 1)
                    dve.wait_ge(S("lin_numc"), b + 1)
                    v.tensor_tensor(att[:, b, :], yb[:, b, :], PS[:, 2 * b + 1, :], ALU.mult).then_inc(S("lin_att"), 1)
                for b in range(B):
                    dve.wait_ge(S("lin_y"), b + 1)
                    residual(b, 1)

            def rwkv():
                layernorm(3)
                for b in range(B):
                    dve.wait_ge(S("ln_h"), 2 * 3 + b + 1)
                    for mu, dst in ((0, xc), (1, sq)):
                        link(v.tensor_scalar(dst[:, b, :], hp[:, b, 0:T], small[:, 6 + mu:7 + mu], None, ALU.mult))
                        v.scalar_tensor_tensor(dst[:, b, :], h[b], V("mur" if mu == 0 else "muk"), dst[:, b, :],
                                               ALU.mult, ALU.add).then_inc(S("mix_in"), 1)
                for b in range(B):
                    dve.wait_ge(S("mix_act"), 2 * b + 2)
                    v.tensor_tensor(att[:, b, :], PTB[:, b, :], PTB[:, b, :], ALU.mult).then_inc(S("mix_k2"), 1)
                for b in range(B):
                    dve.wait_ge(S("mix_v"), b + 1)
                    link(v.tensor_tensor(yb[:, b, :], yb[:, b, :], PS[:, 2 * b, :], ALU.mult))
                    residual(b, 5)

            def experts():
                ln_eps(5, 1)
                ln_scale(5, 1)
                dve.wait_ge(S("ex_sig"), 1)

                def routing():
                    link(v.tensor_tensor(rt[:, 1, :], rt[:, 0, :], V("rbias"), ALU.add))
                    first_max(rt[:, 1, :], rt[:, 2, :], rt[:, 5, :], r8t[:, 0, :])
                    link(v.scalar_tensor_tensor(rt[:, 1, :], rt[:, 2, :], NEG, rt[:, 1, :], ALU.mult, ALU.add))
                    first_max(rt[:, 1, :], rt[:, 3, :], rt[:, 5, :], r8t[:, 0, :])
                    link(v.tensor_tensor(rt[:, 2, :], rt[:, 2, :], rt[:, 3, :], ALU.add))
                    link(v.tensor_tensor(rt[:, 4, :], rt[:, 2, :], rt[:, 0, :], ALU.mult))
                    link(v.tensor_reduce(r8t[:, 1, :], v3(rt[:, 4, :]), AX.X, ALU.add))
                    link(v.tensor_scalar(r8t[:, 2, :], r8t[:, 1, :], 1e-9, None, ALU.add))
                    link(v.reciprocal(r8t[:, 3, :], r8t[:, 2, :]))
                    link(v.tensor_scalar(r8t[:, 4, :], r8t[:, 1, :], 1e-9, None, ALU.is_gt))
                    link(v.tensor_tensor(r8t[:, 3, :], r8t[:, 3, :], r8t[:, 4, :], ALU.mult))
                    link(v.tensor_scalar(r8t[:, 4, :], r8t[:, 4, :], -0.5, 0.5, ALU.mult, ALU.add))
                    link(v.tensor_tensor(v3(rt[:, 4, :]), v3(rt[:, 4, :]),
                                         r8t[:, 3, :].unsqueeze(2).to_broadcast([128, 8, 8]), ALU.mult))
                    link(v.tensor_tensor(v3(rt[:, 2, :]), v3(rt[:, 2, :]),
                                         r8t[:, 4, :].unsqueeze(2).to_broadcast([128, 8, 8]), ALU.mult))
                    v.tensor_tensor(rt[:, 9, :], rt[:, 4, :], rt[:, 2, :], ALU.add).then_inc(S("ex_comb"), 1)

                routing()
                for n in range(20):
                    dve.wait_ge(S("ex_act"), n + 1)
                    dve.wait_ge(S("ex_up"), 2 * n + 2)
                    if n >= 4:
                        dve.wait_ge(S("ex_down"), n - 3)
                    v.tensor_tensor(PTB[:, n % 4, :], PTB[:, 4 + n % 4, :], PS[:, 4 + n % 2, :],
                                    ALU.mult).then_inc(S("ex_prod"), 1)
                for b in range(B):
                    dve.wait_ge(S("ex_down"), 19 + b)
                    v.scalar_tensor_tensor(xb[b], PS[:, b, :], tg[:, 6:7], xb[b], ALU.mult,
                                           ALU.add).then_inc(S("x_ready"), 1)


            def final_layer():
                v.memset(wk, 0.0).then_inc(S("sp_cleared"), 1)

                def swap(r):
                    dve.wait_ge(S("d_pair"), r + 1)
                    if r >= 1:
                        dve.wait_ge(S("d_roped"), 2 * r)
                    for j in range(4):
                        v.tensor_tensor(den4[:, j, :], PS[32 * j:32 * j + 32, 2, :], C3("ropes", 0, 32),
                                        ALU.mult).then_inc(S("d_swap"), 1)

                def maxima(u):
                    dve.wait_ge(S("d_scores"), u + 1)
                    link(v.tensor_tensor(PS[:, 0:4, 384:512], PS[:, 0:4, 384:512],
                                         C3("causal").unsqueeze(1).to_broadcast([128, 4, 128]), ALU.add))
                    for t in range(TB):
                        ins = v.tensor_reduce(mxd[:, u % 2, t:t + 1], PS[:, t, (3 - t) * 128:512], AX.X, ALU.max)
                    ins.then_inc(S("d_max"), 1)

                def diagonal(u, k):
                    g = 4 * u + k
                    dve.wait_ge(S("d_probs"), g + 1)
                    blk = PTB[:, g % 4, k * 128:(k + 1) * 128]
                    v.scalar_tensor_tensor(blk, blk, BIG, C("tri"), ALU.min, ALU.mult).then_inc(S("d_masked"), 1)

                def take(u):
                    b, hd = divmod(u, NHD)
                    mine = slice(64 * (hd % 2), 64 * (hd % 2) + 64)
                    dve.wait_ge(S("d_weighed"), 4 * (u + 1))
                    v.tensor_copy(AVT[mine, b, hd // 2, :], PS[mine, 6, :]).then_inc(S("d_taken"), 1)

                def recip(p):
                    dve.wait_ge(S("d_dens"), p + 1)
                    link(v.reciprocal(recd[:], PS[:, 0, 0:2 * TB].rearrange("p (t n) -> p t n", n=2)))
                    widen(wide, recd[:], 64).then_inc(S("d_wide"), 1)

                def norm(p):
                    b, q = divmod(p, 4)
                    dve.wait_ge(S("d_spread"), p + 1)
                    v.tensor_tensor(AVT[:, b, q, :], AVT[:, b, q, :], PS[:, 1, :], ALU.mult).then_inc(S("d_normed"), 1)

                def top(n):
                    if n == 0:
                        dve.wait_ge(S("sp_work"), 2)
                    link(v.max(m8[:], wk))
                    link(v.match_replace(wk, m8[:], wk, -BIG))

                def one_hots(b):
                    for t in range(TB):
                        at = t * 16 + b * 8
                        v.tensor_tensor(PT[:, t, :].rearrange("p (h s) -> p h s", h=8),
                                        C3("iota64").unsqueeze(1).to_broadcast([128, 8, 64]),
                                        selT[:, 2, at:at + 8].unsqueeze(2).to_broadcast([128, 8, 64]),
                                        ALU.is_equal).then_inc(S("sp_G"), 1)

                h64 = lambda t: t.rearrange("p (h s) -> p h s", h=8)

                def sparse(b, s):
                    def product():
                        dve.wait_ge(S("sp_product"), made(b, s))
                    if s == "columns":
                        product()
                        for c in range(B):
                            link(v.tensor_copy(selT[:, 0, :].rearrange("p (t n) -> p t n", t=TB)[:, :, 8 * c:8 * c + 8],
                                               PS[:, 7, 0:160].rearrange("p (t n) -> p t n", t=TB)[:, :, 32 * c:32 * c + 8]))
                        link(v.memset(selT[:, 1, 0:16], 0.0))
                        for t in range(1, TB):
                            ins = v.tensor_tensor(selT[:, 1, t * 16:t * 16 + 16], selT[:, 1, t * 16 - 16:t * 16],
                                                  selT[:, 0, t * 16 - 16:t * 16], ALU.add)
                            if t < TB - 1:
                                link(ins)
                        ins.then_inc(S("sp_taken"), 1)
                    elif s == "ranks":
                        product()
                        v.tensor_tensor(selT[:, 2, :], PS[:, 7, 0:64], selT[:, 0, :], ALU.mult).then_inc(S("sp_taken"), 1)
                        dve.wait_ge(S("sp_taken"), made(b, s))
                        link(v.tensor_scalar(selT[:, 2, :], selT[:, 2, :], -1.0, None, ALU.add))
                        one_hots(0)
                    elif s == "angles":
                        product()
                        v.tensor_copy(trig[:, 0, :], PS[0:32, 7, :])
                        v.tensor_copy(trig[:, 1, :], PS[32:64, 7, :]).then_inc(S("sp_taken"), 1)
                    elif s == "swapped":
                        product()
                        for j in range(2):
                            ins = v.tensor_tensor(trig[:, 2 + j, :], PS[32 * j:32 * j + 32, 7, :], trig[:, 1, :], ALU.mult)
                        ins.then_inc(S("sp_taken"), 1)
                    elif s == "qk":
                        dve.wait_ge(S("sp_taken"), made(b, s))
                        link(v.tensor_tensor(sqk[0:32, :, :], sqk[0:32, :, :],
                                             trig[:, 0, :].unsqueeze(1).to_broadcast([32, 2, T]), ALU.mult))
                        v.tensor_tensor(sqk[0:32, :, :], sqk[0:32, :, :], trig[:, 2:4, :],
                                        ALU.add).then_inc(S("sp_roped"), 1)
                    elif s == "scores":
                        product()
                        v.tensor_tensor(h64(sdiff), h64(PS[0:64, 7, :]),
                                        C3("causal", 0, 64)[:, 0:64].unsqueeze(1).to_broadcast([64, 8, 64]),
                                        ALU.add).then_inc(S("sp_taken"), 1)
                        dve.wait_ge(S("sp_taken"), made(b, s))
                        link(v.tensor_reduce(sps[:, 1, :], h64(sdiff), AX.X, ALU.max))
                        v.tensor_tensor(h64(sdiff), h64(sdiff), sps[:, 1, :].unsqueeze(2).to_broadcast([64, 8, 64]),
                                        ALU.subtract).then_inc(S("sp_diff"), 1)
                    elif s == "weights":
                        dve.wait_ge(S("sp_p"), b + 1)
                        link(v.tensor_reduce(sps[:, 2, :], h64(spp), AX.X, ALU.add))
                        dve.wait_ge(S("sp_gate"), b + 1)
                        link(v.scalar_tensor_tensor(sps[:, 3, :], sps[:, 0, :], 1.0, sps[:, 2, :], ALU.add, ALU.mult))
                        link(v.reciprocal(sps[:, 3, :], sps[:, 3, :]))
                    elif s == "turn3" and b == 0:
                        product()
                        one_hots(1)
                    elif s in ("out0", "out1"):
                        a = int(s[-1])
                        product()
                        for z in range(2):
                            ins = v.tensor_tensor(
                                spz[64 * z:64 * z + 64, 2 * a:2 * a + 2, :],
                                PS[0:64, 7, :].rearrange("p (c z d) -> p c z d", c=2, z=2)[:, :, z, :],
                                sps[:, 3, 4 * a:4 * a + 4].rearrange("p (c z) -> p c z", c=2)[:, :, z].unsqueeze(2)
                                .to_broadcast([64, 2, 128]), ALU.mult)
                        ins.then_inc(S("sp_taken"), 1)
                    elif s == "y":
                        dve.wait_ge(S("last_y"), b + 1)
                        v.scalar_tensor_tensor(xb[b], PS[:, 7, :], tg[:, 7:8], xb[b], ALU.mult,
                                               ALU.add).then_inc(S("x_ready"), 1)

                NU = B * NHD
                swap(0)
                ln_eps(7, 1)
                dve.wait_ge(S("d_swap"), 4)
                dve.wait_ge(S("d_raw"), 4)
                first = QK[0][0:32, 0:4:2, :]
                v.tensor_tensor(first, first, C3("ropec", 0, 32).unsqueeze(1).to_broadcast([32, 2, T]),
                                ALU.mult).then_inc(S("d_first"), 1)
                dve.wait_ge(S("d_first"), 1)
                v.tensor_tensor(first, first, den4[:, 0:4:2, :], ALU.add).then_inc(S("d_first"), 1)
                ln_scale(7, 1)
                for n in range(4):
                    top(n)
                swap(1)
                maxima(0)
                for u in range(NU):
                    r, z = divmod(u, 2)
                    diagonal(u, 0)
                    diagonal(u, 1)
                    if u + 1 < NU:
                        maxima(u + 1)
                    sparse(*slot(u, 0))
                    diagonal(u, 2)
                    diagonal(u, 3)
                    sparse(*slot(u, 1))
                    if z == 0 and r + 2 < NU // 2:
                        swap(r + 2)
                    if z == 1 and r > 0:
                        recip(r - 1)
                    if 4 + u < SEL // 8:
                        top(4 + u)
                    if 4 + u == SEL // 8 - 1:
                        v.tensor_scalar(wk, wk, -BIG, None, ALU.is_equal).then_inc(S("sp_selected"), 1)
                    take(u)
                    if z == 1 and r > 0:
                        norm(r - 1)
                    sparse(*slot(u, 2))
                recip(NU // 2 - 1)
                norm(NU // 2 - 1)
                sparse(1, "y")
            arrived(dve, "cols", "const")
            link(v.tensor_tensor(small[:, 8:12], V("lq1"), V("lk1"), ALU.mult))
            v.tensor_reduce(small[:, 0:1], small[:, 8:12], AX.X, ALU.add).then_inc(S("lam_dots"), 1)
            dve.wait_ge(S("lam_dots"), 1)
            link(v.tensor_tensor(small[:, 8:12], V("lq2"), V("lk2"), ALU.mult))
            v.tensor_reduce(small[:, 1:2], small[:, 8:12], AX.X, ALU.add).then_inc(S("lam_dots"), 1)
            dve.wait_ge(S("gates"), 2)
            link(v.tensor_tensor(small[:, 4:5], small[:, 3:4], small[:, 2:3], ALU.subtract))
            link(v.tensor_scalar(small[:, 4:5], small[:, 4:5], -LAMBDA_INIT, None, ALU.add))
            link(v.tensor_scalar(small[:, 5:6], V("subln"), 1.0 - LAMBDA_INIT, None, ALU.mult))
            link(v.tensor_scalar(small[:, 6:7], V("mur"), -1.0, 1.0, ALU.mult, ALU.add))
            link(v.tensor_scalar(small[:, 7:8], V("muk"), -1.0, 1.0, ALU.mult, ALU.add))
            dve.wait_ge(S("gates"), 2)
            attention(0, 0, 0)
            moe()
            linear()
            rwkv()
            dve.wait_ge(S("pool_set"), POOL_SET["keep"])
            attention(1, 4, 2)
            experts()
            dve.wait_ge(S("pool_set"), POOL_SET["mask3"])
            attention(2, 6, 3)
            final_layer()

        @block.gpsimd
        def _(pool):
            g = nc.gpsimd

            def layernorm(i):
                for b in range(B):
                    pool.wait_ge(S("ln_veps"), 2 * i + b + 1)
                    g.tensor_tensor(rstd[:, b, :], veps[:, b, :], mhalf[:, 0:TB], ALU.pow).then_inc(S("ln_rstd"), 1)

            def zero_queries(a):
                c = ATTN[a]
                if a > 0:
                    pool.wait_ge(S("ln_rstd"), 8 if a == 1 else 12)
                g.memset(QA if a == 0 else QA[c["mrow"]:128, :, 0:c["nsub"]], 0.0).then_inc(S("at_q_zeroed"), 1)
                pool.wait_ge(S("at_q_zeroed"), a + 1)

            def build(a, b):
                c = ATTN[a]
                qd = c["qd"]
                km = C({0: "kmask4", 1: "kmask8", 2: "kmask16"}[a], qd)
                if b == 0:
                    pool.wait_ge(S("at_k_placed"), before(a, "k_placed") + 1)
                for s in range(c["nsub"]):
                    g.tensor_tensor(KA[a][0:qd, b, s, :].rearrange("p (n k) -> p n k", k=SK),
                                    kT[0:qd, s, b * SK:(b + 1) * SK].unsqueeze(1).to_broadcast([qd, c["nh"], SK]),
                                    km.unsqueeze(2).to_broadcast([qd, c["nh"], SK]), ALU.mult).then_inc(S("at_k_built"), 1)

            def final_layer():
                layernorm(7)

                def rope(r):
                    qk, swapped = QK[r % 3][0:32], den4[:]
                    if r == 0:
                        qk, swapped = qk[:, 1:4:2, :], den4[:, 1:4:2, :]
                    pool.wait_ge(S("d_raw"), 4 * (r + 1))
                    g.tensor_tensor(qk, qk, C3("ropec", 0, 32).unsqueeze(1).to_broadcast([32, qk.shape[1], T]),
                                    ALU.mult).then_inc(S("d_roped"), 1)
                    pool.wait_ge(S("d_roped"), 2 * r + 1)
                    pool.wait_ge(S("d_swap"), 4 * (r + 1))
                    g.tensor_tensor(qk, qk, swapped, ALU.add).then_inc(S("d_roped"), 1)

                rope(0)
                g.memset(QK[2][64:128, 0:2, :], 0.0).then_inc(S("pool_set"), 1)
                g.memset(QK[2][64:128, 2:4, :], -1.0).then_inc(S("pool_set"), 1)
                pool.wait_ge(S("d_roped"), 2)
                pool.wait_ge(S("pool_set"), POOL_SET["slots"] + 2)
                for ones in (keys[:, 0:6 * 768], mask3f[:, 0:768], ctxf[:, 0:768]):
                    g.memset(ones.rearrange("p (n d) -> p n d", d=192)[:, :, 64:128], 1.0).then_inc(S("pool_set"), 1)
                pool.wait_ge(S("pool_set"), POOL_SET["last"])
                for r in range(1, B * NHD // 2):
                    rope(r)

            g.memset(keys[:, :], 0.0).then_inc(S("pool_set"), 1)
            g.memset(mhalf[:], -0.5).then_inc(S("pool_set"), 1)
            g.memset(hp[:, :, 0:1], 0.0).then_inc(S("pool_set"), 1)
            pool.wait_ge(S("pool_set"), 3)
            arrived(pool, "const")
            for a, one, nh in ((0, "vone8", 8), (2, "vone16", 4)):
                for b in range(B):
                    for z in range(2):
                        last = g.tensor_copy(VA[a][:, b, z, :, 64:64 + nh], C(one).rearrange("p (c n) -> p c n", n=nh))
                        last.then_inc(S("pool_set"), 1)
            zero_queries(0)
            build(0, 0)
            layernorm(0)
            build(0, 1)
            pool.wait_ge(S("at_rms_eps"), 1)
            g.tensor_tensor(rmsr[:, 0, :, :], rms[:, 0, :].rearrange("p (t n) -> p t n", t=TB),
                            mhalf[:].rearrange("p (t n) -> p t n", t=TB), ALU.pow).then_inc(S("at_rms_r"), 1)
            g.iota(pool_iota[:], [[1, 1024]], base=0, channel_multiplier=0,
                   allow_small_or_imprecise_dtypes=True).then_inc(S("pool_set"), 1)
            layernorm(1)
            arrived(pool, "minus1")
            for a in (1, 2):
                for b in range(B):
                    build(a, b)
            arrived(pool, "maskr", "maskq", "mask3")
            pool.wait_ge(S("moe_down"), E)
            g.tensor_scalar(keep, maskr[:], -1.0, 1.0, ALU.mult, ALU.add).then_inc(S("pool_set"), 1)
            g.tensor_scalar(mbias[:], maskq[:], NEG, None, ALU.mult).then_inc(S("pool_set"), 1)
            g.tensor_copy(mask3f[:], mask3).then_inc(S("pool_set"), 1)
            layernorm(2)
            layernorm(3)
            pool.wait_ge(S("x_ready"), 2 * 4)
            zero_queries(1)
            layernorm(4)
            layernorm(5)
            pool.wait_ge(S("ln_rstd"), 2 * 6)
            for q in range(2):
                g.memset(QK[q][64:128, 0:2, :], 0.0).then_inc(S("pool_set"), 1)
                g.memset(QK[q][64:128, 2:4, :], -1.0).then_inc(S("pool_set"), 1)
            pool.wait_ge(S("x_ready"), 2 * 6)
            zero_queries(2)
            layernorm(6)
            final_layer()


def layout(i):
    f = np.float32
    A = {}
    A["xT"] = i["x"].reshape(N, D).T
    c = i["ctx_1024"].transpose(2, 0, 1)
    A["ctx"] = np.tile(c, (1, 1, 8)).reshape(D, -1)

    def pack(*ws):
        return np.concatenate([w for w in ws], 1)

    for l, o in ((0, "Wp"), (1, "Wo"), (2, "Wo"), (3, "Wo")):
        A[f"wa{l}"] = pack(*(i[f"L{l}_xattn_{n}"].T for n in ("Wq", "Wk", "Wv", o)))
    A["wf1"] = pack(*(i[f"L1_ffn_{n}"].T for n in ("W_r", "W_k", "W_v")))
    A["rw0"] = pack(i["L0_ffn_router_w"], i["L2_ffn_router_w"].T, i["L3_ffn_mosa_router_w"])
    A["w1"] = i["L0_ffn_w1"].transpose(1, 0, 2).reshape(D, -1)
    A["w2"] = i["L0_ffn_w2"].reshape(E, 4, 128, D).transpose(2, 0, 1, 3).reshape(128, -1)
    A["sw13"] = pack(i["L2_ffn_sw1"], i["L2_ffn_sw3"])
    A["sw2"] = i["L2_ffn_sw2"].reshape(2, 128, D).transpose(1, 0, 2).reshape(128, -1)
    A["ew1"] = i["L2_ffn_ew1"].transpose(1, 0, 2).reshape(D, -1)
    A["ew2"] = i["L2_ffn_ew2"].transpose(1, 0, 2).reshape(128, -1)
    swapped = np.r_[ROT // 2:ROT, 0:ROT // 2]
    w = i["L3_ffn_dense_wqkv"]
    q, k, v = w[:, :, 0:HP], w[:, :, HP:2 * HP], w[:, :, 2 * HP:]
    parts = []
    for p in range(0, NHD, 2):
        parts += [q[:, p], q[:, p + 1], k[:, p], k[:, p + 1], q[:, p][:, swapped], q[:, p + 1][:, swapped],
                  k[:, p][:, swapped], k[:, p + 1][:, swapped]]
    A["wd"] = pack(*parts, v.reshape(D, -1))
    w = i["L3_ffn_mosa_wqkv"]
    q, k, v = w[:, :, 0:HP], w[:, :, HP:2 * HP], w[:, :, 2 * HP:]
    A["wm"] = pack(*(t for n in range(8) for t in (q[:, n], k[:, n], q[:, n][:, swapped], k[:, n][:, swapped], v[:, n])))
    A["wod"] = i["L3_ffn_dense_wo"].reshape(4, 128, D).transpose(1, 0, 2).reshape(128, -1)
    A["wom"] = i["L3_ffn_mosa_wo"].reshape(8, 64, D).transpose(1, 0, 2).reshape(64, -1)
    cols = np.zeros((128, COLS["_"]), f)

    def put(name, a):
        lo, hi = COLS[name]
        cols[:a.shape[0], lo:hi] = a

    put("g", np.tile(np.concatenate([i["g_xattn"], i["g_ffn"]])[None], (128, 1)))
    for n in ("lq1", "lk1", "lq2", "lk2"):
        put(n, np.tile(i["L0_xattn_" + n][None], (128, 1)))
    put("subln", np.tile(i["L0_xattn_subln_w"], 16)[:, None])
    for name, key in (("bp", "L0_xattn_bp"), ("bv2", "L2_xattn_bv"), ("bv3", "L3_xattn_bv"),
                      ("bo1", "L1_xattn_bo"), ("bo2", "L2_xattn_bo"), ("bo3", "L3_xattn_bo"),
                      ("bq1", "L1_xattn_bq"), ("mur", "L1_ffn_mu_r"), ("muk", "L1_ffn_mu_k")):
        put(name, i[key][:, None])
    for l in (2, 3):
        put(f"bq{l}", i[f"L{l}_xattn_bq"].reshape(2, 64).T)
        put(f"bk{l}", i[f"L{l}_xattn_bk"].reshape(2, 64).T)
    put("rbias", np.tile(i["L2_ffn_router_bias"][None], (128, 8)))
    A["cols"] = cols
    A["rows"] = np.concatenate([i["L1_xattn_bk"], i["L1_xattn_bv"]])[None]
    m = i["mask_1x1xSxS2_bk1"].reshape(T, SK)
    A["maskr"] = m.T[np.arange(5 * 128) % SK].reshape(5, 128, T).transpose(1, 0, 2).reshape(128, -1)
    A["maskq"] = m.reshape(TB, 128, SK).transpose(1, 0, 2).reshape(128, -1)
    A["mask3"] = np.tile(i["mask_BxSx1_ik1"].reshape(1, N), (128, 1))
    A.update(constants())
    return {k_: np.ascontiguousarray(a) for k_, a in A.items()}


def kernel(**inputs):
    import concourse.bacc as _bacc
    from concourse.bass_utils import run_bass_kernel_spmd as _run

    arrays = layout({k: np.asarray(a) for k, a in inputs.items()})
    nc = _bacc.Bacc("TRN2", target_bir_lowering=False, num_devices=1)
    A = {k: nc.dram_tensor(k + "_dram", a.shape, mybir.dt.from_np(a.dtype), kind="ExternalInput").ap()
         for k, a in arrays.items()}
    out = nc.dram_tensor("out_dram", (D, N), F32, kind="ExternalOutput").ap()
    build(nc, A, out)
    r = _run(nc, [{k + "_dram": a for k, a in arrays.items()}], core_ids=[0])
    y = r.results[0]["out_dram"]
    return np.ascontiguousarray(y.T).reshape(B, T, D)
```

```python
from contextlib import ExitStack

import numpy as np
import concourse.bass as bass
from concourse import mybir

F32 = mybir.dt.float32
I32 = mybir.dt.int32
U8 = mybir.dt.uint8
ALU = mybir.AluOpType
ACT = mybir.ActivationFunctionType
AX = mybir.AxisListType

D = 128
B = 2
T = 512
N = B * T
NT = N // 128
TB = T // 128
SK = 77
E = 8
CAP = N // E
F = 512
EPS = 1e-5
BIG = 3.0e38
NEG = -1.0e30
LAMBDA_INIT = 0.8 - 0.6 * float(np.exp(-0.3 * 4))

ATTN = [dict(layer=0, nsub=4, nh=8, qd=32, scale=0.5),
        dict(layer=2, nsub=2, nh=8, qd=64, scale=8 ** -0.5),
        dict(layer=3, nsub=2, nh=4, qd=64, scale=128 ** -0.5)]
for _c in ATTN:
    _c["rows"] = _c["nh"] * SK
    _c["chunks"] = [(c, min(128, _c["rows"] - c)) for c in range(0, _c["rows"], 128)]

KBANK = [4, 7, 6]
VBANK = [(6, 6), (2, 4), (2, 3)]

PREFETCHED = (1, 5, 7)


def centre_bank(i, b):
    return 5 if b and i in PREFETCHED else 2 * b


NHD = 8
HP = 64
ROT = 32
SEL = T // 8

FIRST_SPARSE = 4
SPARSE = [(0, "columns"), (0, "ranks")]
for _b in range(B):
    SPARSE += [(_b, s) for s in ("gather", "angles", "turn0", "swapped", "qk", "v", "turn1", "scores", "turn2",
                                 "weights", "turn3", "sums", "out0", "out1")]
SLOTS = SPARSE[:2] + [(0, None)] * 2 + SPARSE[2:16] + [(0, "y")] + SPARSE[16:]


def made(b, s):
    return SPARSE.index((b, s)) + 1


def pair_bank(r, j):
    return j if r < 2 else (4, 5, 4)[j]


ORDER = (3, 2, 0, 1)

GROUPS = [(4, [(3, 0), (3, 1), (3, 2), (3, 3)]), (5, [(2, 0), (2, 1), (2, 2), (0, 0)]), (1, [(1, 0), (1, 1)])]


def slot(u, j):
    n = 3 * (u - FIRST_SPARSE) + j
    return SLOTS[n] if 0 <= n < len(SLOTS) else (0, None)


def pool_tiles(c):
    return [0, 1, 2, 3] if c["layer"] == 2 else [0, 2]


TURNED_BANK = [0, 1, 4, 5, 2]


def signals(c):
    units = B * c["nsub"]
    parts = units * len(c["chunks"])
    first = B if c["layer"] == 0 else 0
    return dict(q_zeroed=1, keys=1, k_placed=1, values=B, v_placed=B, query=B if c["layer"] == 0 else units, q_placed=units,
                k_built=units, scores=units * TB, left=len(pool_tiles(c)) * units,
                max_taken=len(pool_tiles(c)) * units, diffs=(TB - len(pool_tiles(c))) * units,
                pool_diffs=len(pool_tiles(c)) * units, exps=units * TB,
                turned_keys=parts, even=units * ((len(c["chunks"]) + 1) // 2), odd=units * (len(c["chunks"]) // 2),
                weighed=units, o_taken=units,
                rms_eps=first, rms_r=first, rms_done=first, turned=B, att_done=B, projected=B, y_placed=B)


def tile_done(a, name, u, t):
    tiles = pool_tiles(ATTN[a])
    if name == "diffs":
        tiles = [k for k in range(TB) if k not in tiles]
    return before(a, name) + len(tiles) * u + tiles.index(t) + 1


def copied(a, u, j):
    c, side = ATTN[a], "odd" if j % 2 else "even"
    per = (len(c["chunks"]) + 1 - j % 2) // 2
    return before(a, side) + per * u + j // 2 + 1


POOL_SET = dict(ones=11, iota=12, mbias=13, mask3=14, last=17)


def before(a, name):
    return sum(signals(c)[name] for c in ATTN[:a])


def columns(*widths):
    at, out = 0, {}
    for name, w in widths:
        out[name] = (at, at + w)
        at += w
    out["_"] = at
    return out


CONST = columns(("ident", 128), ("center", 128), ("tri", 128), ("ones", 128), ("mean", 1),
                ("head8", 16), ("block8", 128), ("firstw", 64), ("slot0", 64),
                ("slotid", 8), ("vmask8", 320), ("vmask16", 192), ("vone8", 40), ("vone16", 12),
                ("kmask4", 8), ("kmask8", 8), ("kmask16", 4))
CONST3 = columns(("causal", 128), ("ropec", 512), ("ropes", 512), ("tab", 256), ("iota64", 64))
COLS = columns(("g", 8), ("lq1", 4), ("lk1", 4), ("lq2", 4), ("lk2", 4), ("subln", 1), ("bp", 1),
               ("bv2", 1), ("bv3", 1), ("bo1", 1), ("bo2", 1), ("bo3", 1), ("bq1", 1), ("mur", 1), ("muk", 1),
               ("bq2", 2), ("bk2", 2), ("bq3", 2), ("bk3", 2), ("rbias", 64))
ROWS = columns(("bk1", 128), ("bv1", 128))


def constants():
    c = np.zeros((128, CONST["_"]), np.float32)
    p = np.arange(128)

    def put(name, a):
        lo, hi = CONST[name]
        c[:a.shape[0], lo:hi] = a.reshape(a.shape[0], -1)

    put("ident", np.eye(128))
    put("center", np.eye(128) - 1.0 / D)
    put("tri", p[:, None] <= p[None, :])
    put("ones", np.ones((128, 128)))
    put("mean", np.full((128, 1), 1.0 / D))
    put("head8", p[:, None] // 8 == np.arange(16))
    put("block8", p[:, None] // 8 == p[None, :] // 8)
    put("firstw", np.tile(8.0 - np.arange(8), (128, 8)))
    put("slot0", np.tile(CAP * np.arange(8.0), (128, 8)))
    put("slotid", p[:, None] + CAP * np.arange(8.0))
    r8 = p[:, None] + 128 * np.arange(5)
    r16 = p[:, None] + 128 * np.arange(3)
    f = np.arange(64)
    put("vmask8", r8[:, :, None] // SK == f // 8)
    put("vmask16", r16[:, :, None] // SK == f // 16)
    put("vone8", r8[:, :, None] // SK == np.arange(8))
    put("vone16", r16[:, :, None] // SK == np.arange(4))
    put("kmask4", np.arange(32)[:, None] // 4 == np.arange(8))
    put("kmask8", f[:, None] // 8 == np.arange(8))
    put("kmask16", f[:, None] // 16 == np.arange(4))

    d = np.zeros((128, CONST3["_"]), np.float32)

    def put3(name, a):
        lo, hi = CONST3[name]
        d[:a.shape[0], lo:hi] = a.reshape(a.shape[0], -1)

    put3("causal", np.where(p[None, :] > p[:, None], NEG, 0.0))
    half = ROT // 2
    inv = (10000.0 ** (-np.arange(half, dtype=np.float32) / half)).astype(np.float32)
    ang = (np.arange(T, dtype=np.float32)[:, None] * inv).astype(np.float32)
    cos, sin = np.cos(ang), np.sin(ang)
    cos2 = np.concatenate([cos, cos], 1)
    sin2 = np.concatenate([-sin, sin], 1)
    put3("ropec", cos2.T)
    put3("ropes", sin2.T)
    put3("tab", np.concatenate([cos2, sin2], 1).reshape(TB, 128, 64).transpose(1, 0, 2))
    put3("iota64", np.tile(np.arange(64.0), (128, 1)))

    return {"const": c, "const3": d}


def build(nc, A, out):
    with ExitStack() as ctx:
        sems = {}

        def S(name):
            if name not in sems:
                sems[name] = ctx.enter_context(nc.semaphore(name))
            return sems[name]

        def sb(name, shape, dt=F32):
            return ctx.enter_context(nc.sbuf_tensor(name, shape, dt))

        PS = ctx.enter_context(nc.psum_tensor("PS", [128, 8, 512], F32))

        cst = sb("cst", [128, CONST["_"]])
        cst3 = sb("cst3", [128, CONST3["_"]])
        cols = sb("cols", [128, COLS["_"]])
        rows = sb("rows", [1, ROWS["_"]])
        x = sb("x", [128, N])
        ctxr = sb("ctxr", [128, B, 8 * SK])
        ctxf = ctxr[:].rearrange("p b k -> p (b k)")
        wa = sb("wa", [128, 4, 4, 128])
        wa0, wa1, wa2, wa3 = (wa[:, n] for n in range(4))
        wf1 = sb("wf1", [128, 3, 128])
        rw0 = sb("rw0", [128, 24])
        wmoe = sb("wmoe", [128, 2 * E * F])
        w1 = wmoe[:, 0:E * F].rearrange("p (e f) -> p e f", e=E)
        w2 = wmoe[:, E * F:2 * E * F].rearrange("p (e c d) -> p e c d", e=E, c=4)
        sw13 = sb("sw13", [128, 2, 256])
        sw2 = sb("sw2", [128, 2, 128])
        wlate = sb("wlate", [128, 3 * 512 + 512])
        ew1 = wlate[:, 0:1024].rearrange("p (e f) -> p e f", e=E)
        ew2 = wlate[:, 1024:2048].rearrange("p (e f) -> p e f", e=E)
        wd = sb("wd", [128, 3 * 512 + 512])
        wm = wlate
        wod = sb("wod", [128, 4, 128])
        wom = sb("wom", [64, 8, 128])
        maskq = sb("maskq", [128, TB, SK], U8)
        mask3f = sb("mask3", [128, N])
        mask3 = mask3f[:].bitcast(I32)

        def C(name, p=128):
            lo, hi = CONST[name]
            return cst[0:p, lo:hi]

        def C3(name, p0=0, p=128):
            lo, hi = CONST3[name]
            return cst3[p0:p, lo:hi]

        def V(name, p=128, j=None):
            lo, hi = COLS[name]
            return cols[0:p, lo:hi] if j is None else cols[0:p, lo + j:lo + j + 1]

        def R(name):
            lo, hi = ROWS[name]
            return rows[0:1, lo:hi]

        ident = C("ident")

        sq = sb("sq", [128, B, T])
        xc = sb("xc", [128, B, T])
        veps = sb("veps", [128, B, TB])
        rstd = sb("rstd", [128, B, TB])
        mhalf = sb("mhalf", [128, TB])
        hp = sb("hp", [128, B, T + 1])
        h = [hp[:, b, 1:T + 1] for b in range(B)]
        tg = sb("tg", [128, 8])
        small = sb("small", [128, 16])
        kT = sb("kT", [64, 4, B * SK])
        keys = sb("keys", [128, 8 * 8 * SK])
        keys_cut = 4 * 8 * SK
        KA = [keys[:, :].rearrange("p (b s k) -> p b s k", b=B, s=4),
              keys[:, 0:keys_cut].rearrange("p (b s k) -> p b s k", b=B, s=2),
              keys[:, keys_cut:keys_cut + 4 * 4 * SK].rearrange("p (b s k) -> p b s k", b=B, s=2)]
        VD = [keys[:, n * 768:(n + 1) * 768] for n in range(6)] + [mask3f[:, 0:768], ctxf[:, 0:768]]
        va8 = sb("va8", [128, B, 2, 5, 72])
        VA = [va8, va8, sb("va16", [128, B, 2, 3, 68])]
        PTB = sb("PTB", [128, 8, T])
        QA = PTB[:].rearrange("p (b s) t -> p b s t", b=B)
        mx = sb("mx", [128, 2, 8])
        PT = sb("PT", [128, 4, T])
        OT = sb("OT", [128, B, 2, T])
        G = OT[:].rearrange("p b z t -> p b (z t)")
        qf = OT[:, 0]
        den4 = sb("den4", [32, 4, T])
        rec = sb("rec", [128, B, TB, 32])
        att = sb("att", [128, B, T])
        rms = sb("rms", [128, B, 64])
        rmsr = sb("rmsr", [128, B, TB, 16])
        yb = sb("yb", [128, B, T])
        mbias = sb("mbias", [128, TB, SK])
        pool_iota = sb("pool_iota", [128, 1024])
        htok = sb("htok", [128, NT, 128])
        htokf = htok[:].rearrange("p n f -> p (n f)")
        WQ = [[wlate[:, t * 616:(t + 1) * 616] for t in range(3)] + [xc[:].rearrange("p b t -> p (b t)")[:, 0:616]],
              [wmoe[:, E * F + t * 616:E * F + (t + 1) * 616] for t in range(4)]]
        WQ = [WQ[0], WQ[1], WQ[1]]
        WK = [[PT[:, j, :] for j in range(4)] + [htokf[:, 0:T]], [PT[:, j, :] for j in range(4)] + [pool_iota[:, 0:T]]]
        WK = [WK[0], WK[1], WK[1]]
        r8t = sb("r8t", [128, 10, 8])
        ein = PT[:, 2:4].rearrange("p a t -> p (a t)")
        hid = PT[:, 0:2]
        eo = sb("eo", [128, 2, 128])
        destb = sq[:].rearrange("p b t -> p (b t)")
        gateb = xc[:].rearrange("p b t -> p (b t)")
        kf = sb("kf", [SK, B, 128])
        vs = sb("vs", [SK, B, 128])
        kvm = sb("kvm", [128, B, 128])
        ksh = sb("ksh", [128, B, 16])
        rt = sb("rt", [128, 10, 64])
        QK = [wmoe[:, 0:4 * T].rearrange("p (j t) -> p j t", j=4),
              wmoe[:, 4 * T:8 * T].rearrange("p (j t) -> p j t", j=4), PTB[:, 4:8]]
        AVT = wmoe[:, 8 * T:16 * T].rearrange("p (b n t) -> p b n t", b=B, n=4)
        GT = [sq[:, 0, :], sq[:, 1, :], xc[:, 0, :], xc[:, 1, :]]
        xg = att[:, 0, :]
        sqk = OT[0:64, 0]
        spv = OT[0:64, 1]
        spp = att[0:64, 1, :]
        spo = yb[0:64, 0, :]
        sdiff = yb[0:64, 1, :]
        sps = sb("sps", [64, 4, 8])
        trig = wa[0:32].rearrange("p n a d -> p n (a d)")
        spz = rt[:, 0:8, :].rearrange("p (q a) c -> p q (a c)", q=4)
        mxd = sb("mxd", [128, 2, TB])
        PQ = [eo[:].rearrange("p a f -> p (a f)")[:, 0:128], kvm[:].rearrange("p b f -> p (b f)"), ctxf[:, 768:768 + 384],
              va8[:].rearrange("p b z c n -> p (b z c n)")[:, 0:512]]
        recd = sb("recd", [128, TB, 2])
        dend = pool_iota[:].rearrange("p (r t) -> p r t", r=2)
        wide = sw13[:].rearrange("p a t -> p (a t)")
        wk = yb[0:40, 0, :]
        m8 = sb("m8", [40, 8])
        selT = sb("selT", [128, 3, 64])

        block = ctx.enter_context(nc.Block())

        loads = [[("xT", x[:]), ("const", cst[:])],
                 [("wa0", wa0), ("ctx", ctxr[:]), ("cols", cols[:])],
                 [("rw0", rw0[:]), ("w1", wmoe[:, 0:E * F]), ("w2", wmoe[:, E * F:2 * E * F])],
                 [("rows", rows[:]), ("wa1", wa1), ("wf1", wf1[:])],
                 [("wa2", wa2), ("maskq", maskq[:]),
                  ("mask3", mask3)],
                 [("sw13", sw13[:]), ("sw2", sw2[:]), ("ew1", wlate[:, 0:1024]), ("ew2", wlate[:, 1024:2048])],
                 [("wa3", wa3)],
                 [("const3", cst3[:]), ("wd", wd[:]), ("wod", wod[:]), ("wom", wom[:])],
                 [("wm", wm[:])]]
        lot = {name: n for n, group in enumerate(loads) for name, _ in group}

        @block.sync
        def _(sp):
            for n, group in enumerate(loads):
                if n == lot["wm"]:
                    sp.wait_ge(S("x_ready"), 2 * 6)
                if n == lot["ew1"]:
                    sp.wait_ge(S("x_ready"), 2)
                for name, dst in group:
                    shape, src = dst.shape, A[name]
                    if len(shape) == 3:
                        src = src.rearrange("p (a b) -> p a b", a=shape[1])
                    elif len(shape) == 4:
                        src = src.rearrange("p (a b c) -> p a b c", a=shape[1], b=shape[2])
                    sp.dma_start(dst, src).then_inc(S(f"loaded_{n}"), 16)
            for b in range(B):
                sp.wait_ge(S("x_ready"), 2 * 8 + b + 1 - 2)
                sp.dma_start(out[:, b * T:(b + 1) * T], x[:, b * T:(b + 1) * T]).then_inc(S("stored"), 16)
            sp.wait_ge(S("stored"), 16 * B)

        def arrived(eng, *names):
            for n in sorted({lot[name] for name in names}):
                eng.wait_ge(S(f"loaded_{n}"), 16 * len(loads[n]))

        class Chain:

            def __init__(self, eng, name):
                self.eng, self.name, self.n = eng, name, 0

            def __call__(self, ins):
                self.n += 1
                ins.then_inc(S(self.name), 1)
                self.eng.wait_ge(S(self.name), self.n)

        xb = [x[:, b * T:(b + 1) * T] for b in range(B)]

        @block.tensor
        def _(pe):
            def mm(o, l, r, start=True, stop=True):
                return nc.tensor.matmul(o, l, r, start=start, stop=stop, skip_group_check=True)

            def ln_centre(i, b):
                if i > 0:
                    pe.wait_ge(S("x_ready"), 2 * i + b - 1)
                elif b == 0:
                    arrived(pe, "xT", "const")
                mm(PS[:, centre_bank(i, b), :], C("center"), xb[b]).then_inc(S("ln_centered"), 1)

            def ln_variance(i, b):
                pe.wait_ge(S("ln_act"), 2 * (2 * i + b) + 1)
                for t in range(TB):
                    last = mm(PS[:, 2 * b + 1, t:t + 1], sq[:, b, t * 128:(t + 1) * 128], C("mean"))
                last.then_inc(S("ln_var"), 1)

            def ln_spread(i, b):
                pe.wait_ge(S("ln_rstd"), 2 * i + b + 1)
                for t in range(TB):
                    last = nc.tensor.transpose(PS[:, 2 * b + 1, t * 128:(t + 1) * 128],
                                               rstd[:, b, t:t + 1].to_broadcast([128, 128]), ident)
                last.then_inc(S("ln_bcast"), 1)

            def layernorm(i):
                for part in (ln_centre, ln_variance, ln_spread):
                    for b in range(B):
                        part(i, b)

            def context(a, w, vbias):
                c = ATTN[a]
                nsub, qd, chunks = c["nsub"], c["qd"], c["chunks"]
                s_ = lambda n: S("at_" + n)
                arrived(pe, *(["ctx", "wa0"] if a == 0 else [f"wa{c['layer']}"]))
                for s in range(nsub):
                    last = mm(PS[0:qd, KBANK[a] + s // 2, (s % 2) * 154:(s % 2) * 154 + 154], w[:, 1, s * qd:(s + 1) * qd],
                              ctxr[:, :, 0:SK])
                if vbias:
                    last = mm(PS[:, KBANK[a], 400:401], w[:, 3, :], V(vbias))
                last.then_inc(s_("keys"), 1)
                for b in range(B):
                    if b == 1 and a == 0:
                        pe.wait_ge(s_("v_placed"), 1)
                    for j, (c0, m) in enumerate(chunks):
                        o = PS[0:m, VBANK[a][b] + j // 4, (j % 4) * 128:(j % 4) * 128 + 128]
                        last = mm(o, ctxr[:, b, c0:c0 + m], w[:, 2, :])
                    last.then_inc(s_("values"), 1)

            def attention(a, i, w):
                c = ATTN[a]
                nsub, nh, qd = c["nsub"], c["nh"], c["qd"]
                chunks = c["chunks"]
                s_ = lambda n: S("at_" + n)
                if a == 0:
                    for b in range(B):
                        ln_centre(0, b)
                    context(0, w, None)
                    for part in (ln_variance, ln_spread):
                        for b in range(B):
                            part(0, b)
                else:
                    layernorm(i)
                pe.wait_ge(s_("k_placed"), before(a, "k_placed") + 1)
                for b in range(B):
                    pe.wait_ge(S("ln_h"), 2 * i + b + 1)
                    if a == 0:
                        mm(PS[:, 4 + b, :], w[:, 0, :], h[b]).then_inc(s_("query"), 1)
                    else:
                        if b == 1:
                            pe.wait_ge(s_("v_placed"), before(a, "v_placed") + 2)
                        for s in range(nsub):
                            mm(PS[0:qd, 4 + 2 * b + s, :], w[:, 0, s * qd:(s + 1) * qd], h[b]).then_inc(s_("query"), 1)
                units = [(b, s) for b in range(B) for s in range(nsub)]
                pe.wait_ge(S("pool_set"), POOL_SET["ones"])
                pe.wait_ge(s_("q_zeroed"), before(a, "q_zeroed") + 1)

                def scores(u, t):
                    b, s = units[u]
                    if s == 0 and t == 0:
                        pe.wait_ge(s_("k_built"), before(a, "k_built") + nsub * (b + 1))
                        pe.wait_ge(s_("q_placed"), before(a, "q_placed") + nsub * (b + 1))
                    n = TB * u + t
                    if n >= 2:
                        v_, t_ = divmod(n - 2, TB)
                        name = "left" if t_ in pool_tiles(c) else "diffs"
                        pe.wait_ge(s_(name), tile_done(a, name, v_, t_))
                    if u > 0 and t == 0:
                        pe.wait_ge(s_("even"), copied(a, u - 1, 0))
                        pe.wait_ge(s_("odd"), copied(a, u - 1, 1))
                    if u > 0 and t == 1 and len(chunks) == 5:
                        pe.wait_ge(s_("even"), copied(a, u - 1, 4))
                    for j in range(c["rows"] // 308):
                        last = mm(PS[:, 2 * (n % 2) + j, 0:308], QA[:, b, s, t * 128:(t + 1) * 128],
                                  KA[a][:, b, s, j * 308:(j + 1) * 308])
                    last.then_inc(s_("scores"), 1)

                def turn_keys(u):
                    if u == 0:
                        pe.wait_ge(s_("q_placed"), before(a, "q_placed") + nsub * B)
                    turned = lambda j, t: nc.tensor.transpose(
                        PS[0:chunks[j][1], TURNED_BANK[j], t * 128:(t + 1) * 128],
                        WQ[a][t][:, chunks[j][0]:chunks[j][0] + chunks[j][1]], ident)
                    early = min(len(chunks), 4)
                    pe.wait_ge(s_("exps"), before(a, "exps") + TB * u + TB - 1)
                    for j in range(early):
                        for t in range(TB - 1):
                            turned(j, t)
                    pe.wait_ge(s_("exps"), before(a, "exps") + TB * (u + 1))
                    for j in range(len(chunks)):
                        for t in range(TB - 1 if j < early else 0, TB):
                            last = turned(j, t)
                        last.then_inc(s_("turned_keys"), 1)

                def weigh(u, j):
                    b, s = units[u]
                    m = chunks[j][1]
                    pe.wait_ge(s_("odd" if j % 2 else "even"), copied(a, u, j))
                    if j == 0 and u > 0:
                        pe.wait_ge(s_("o_taken"), before(a, "o_taken") + u)
                    width = 64 + nh
                    for t in range(TB):
                        last = mm(PS[:, 6, t * width:(t + 1) * width], WK[a][j][0:m, t * 128:(t + 1) * 128],
                                  VA[a][0:m, b, s % 2, j, :], start=(j == 0 and t == 0), stop=(j == len(chunks) - 1))
                    if j == len(chunks) - 1:
                        last.then_inc(s_("weighed"), 1)

                def turn(b):
                    if a == 0:
                        pe.wait_ge(s_("rms_done"), b + 1)
                    pe.wait_ge(s_("o_taken"), before(a, "o_taken") + nsub * (b + 1))
                    if b == 1:
                        pe.wait_ge(s_("y_placed"), before(a, "y_placed") + 1)
                    for t in range(TB):
                        last = nc.tensor.transpose(PS[:, 7, t * 128:(t + 1) * 128], OT[:, b, 0, t * 128:(t + 1) * 128],
                                                   ident)
                    last.then_inc(s_("turned"), 1)

                def project(b):
                    pe.wait_ge(s_("att_done"), before(a, "att_done") + b + 1)
                    mm(PS[:, 7, :], w[:, 3, :], att[:, b, :]).then_inc(s_("projected"), 1)

                def ending(b):
                    if a == 0 and b == 0:
                        for _ in range(3):
                            yield lambda: None
                    yield lambda: turn(b)
                    yield lambda: project(b)

                todo = []

                def step():
                    if todo:
                        todo.pop(0)()

                for t in range(TB):
                    scores(0, t)
                for u in range(len(units)):
                    turn_keys(u)
                    if u + 1 < len(units):
                        scores(u + 1, 0)
                        scores(u + 1, 1)
                    weigh(u, 0)
                    if u + 1 < len(units):
                        scores(u + 1, 2)
                        scores(u + 1, 3)
                    weigh(u, 1)
                    step()
                    for j in range(2, len(chunks)):
                        weigh(u, j)
                    if units[u][1] == nsub - 1:
                        todo += ending(units[u][0])
                    if units[u][0] == 1 and u + 1 < len(units):
                        step()
                ln_centre(i + 1, 0)
                if a > 0:
                    step()
                ln_variance(i + 1, 0)
                if a > 0:
                    step()
                ln_spread(i + 1, 0)
                while todo:
                    step()
                pe.wait_ge(s_("y_placed"), before(a, "y_placed") + B)

            def moe():
                arrived(pe, "rw0")
                for b in range(B):
                    if b == 0:
                        ln_centre(1, 1)
                    else:
                        ln_variance(1, 1)
                        ln_spread(1, 1)
                    pe.wait_ge(S("ln_h"), 2 + b + 1)
                    for t in range(TB):
                        n = b * TB + t
                        nc.tensor.transpose(PS[:, 4 + b, t * 128:(t + 1) * 128], h[b][:, t * 128:(t + 1) * 128], ident)
                        last = mm(PS[:, 6, n * 8:n * 8 + 8], h[b][:, t * 128:(t + 1) * 128], rw0[:, 0:8])
                    last.then_inc(S("moe_logits"), 1)
                pe.wait_ge(S("moe_htok"), 2)
                context(1, wa2, "bv2")
                pe.wait_ge(S("at_k_placed"), 2)
                pe.wait_ge(S("moe_prefix"), 1)
                mm(PS[:, 7, 0:64], C("tri"), rt[:, 3, :], stop=False)
                mm(PS[:, 7, 0:64], C("ones"), rt[:, 4, :], start=False).then_inc(S("moe_cum"), 1)
                for t in range(NT):
                    pe.wait_ge(S("moe_G"), t + 1)
                    for k in range(2):
                        last = mm(PS[:, k, :], htok[:, t, :], G[:, t % 2, k * 512:(k + 1) * 512],
                                  start=(t == 0), stop=(t == NT - 1))
                    last.then_inc(S("moe_gathered"), 1)
                pe.wait_ge(S("at_v_placed"), 4)
                context(2, wa3, "bv3")
                pe.wait_ge(S("at_k_placed"), 3)
                for t in range(NT):
                    last = nc.tensor.transpose(PS[:, 4 + t // 4, (t % 4) * 128:(t % 4) * 128 + 128],
                                               r8t[:, 5, t:t + 1].to_broadcast([128, 128]), ident)
                last.then_inc(S("moe_slots"), 1)
                for t in range(NT):
                    last = nc.tensor.transpose(PS[:, 6 + t // 4, (t % 4) * 128:(t % 4) * 128 + 128],
                                               r8t[:, 6, t:t + 1].to_broadcast([128, 128]), ident)
                last.then_inc(S("moe_slots"), 1)
                arrived(pe, "w1", "w2")
                pe.wait_ge(S("at_v_placed"), 6)
                pe.wait_ge(S("moe_ein"), 2)
                pe.wait_ge(S("moe_bcopied"), 4)

                def up(e):
                    if e >= 2:
                        pe.wait_ge(S("moe_gelu"), e - 1)
                    for f in range(4):
                        last = mm(PS[:, 4 + e % 2, f * 128:(f + 1) * 128], w1[:, e, f * 128:(f + 1) * 128],
                                  ein[:, e * CAP:(e + 1) * CAP])
                    last.then_inc(S("moe_up"), 1)

                def down(e):
                    pe.wait_ge(S("moe_gelu"), e + 1)
                    if e >= 2:
                        pe.wait_ge(S("moe_eo"), e - 1)
                    for f in range(4):
                        last = mm(PS[:, 6 + e % 2, 0:128], hid[:, e % 2, f * 128:(f + 1) * 128], w2[:, e, f, :],
                                  start=(f == 0), stop=(f == 3))
                    last.then_inc(S("moe_down"), 1)

                def combine(e):
                    pe.wait_ge(S("moe_eo"), e + 1)
                    pe.wait_ge(S("moe_GT"), e + 1)
                    for k in range(2):
                        last = mm(PS[:, 2 + k, :], eo[:, e % 2, :], G[:, e % 2, k * 512:(k + 1) * 512],
                                  start=(e == 0), stop=(e == E - 1))
                    last.then_inc(S("moe_combined"), 1)

                up(0)
                for e in range(E):
                    if e + 1 < E:
                        up(e + 1)
                    if e >= 1:
                        combine(e - 1)
                    down(e)
                combine(E - 1)

            def linear():
                arrived(pe, "rows", "wa1")
                for b in range(B):
                    for j, bias in ((1, "bk1"), (2, "bv1")):
                        o = PS[0:SK, 4, (j - 1) * 256 + b * 128:(j - 1) * 256 + b * 128 + 128]
                        mm(o, ctxr[:, b, 0:SK], wa1[:, j, :], stop=False)
                        last = mm(o, C("ones", 1)[:, 0:SK], R(bias), start=False)
                last.then_inc(S("lin_kv"), 1)
                layernorm(2)
                pe.wait_ge(S("lin_kf"), 1)
                for b in range(B):
                    mm(PS[:, 5, b * 128:(b + 1) * 128], kf[:, b, :], vs[:, b, :])
                    last = mm(PS[:, 5, 256 + b * 16:256 + b * 16 + 16], kf[:, b, :], C("ones", SK)[:, 0:16])
                last.then_inc(S("lin_sum"), 1)
                for b in range(B):
                    pe.wait_ge(S("ln_h"), 2 * 2 + b + 1)
                    mm(PS[:, 6 + b, :], wa1[:, 0, :], h[b]).then_inc(S("lin_q"), 1)
                pe.wait_ge(S("lin_kvm"), 1)
                for b in range(B):
                    pe.wait_ge(S("lin_qf"), b + 1)
                    for t in range(TB):
                        mm(PS[:, 4 + b, t * 16:t * 16 + 16], qf[:, b, :][:, t * 128:(t + 1) * 128], ksh[:, b, :])
                    mm(PS[:, 2 * b, :], kvm[:, b, :], qf[:, b, :]).then_inc(S("lin_num"), 1)
                for b in range(B):
                    pe.wait_ge(S("lin_rec"), b + 1)
                    for t in range(TB):
                        last = nc.tensor.transpose(PS[:, 2 * b + 1, t * 128:(t + 1) * 128],
                                                   xc[:, b, t * 128:(t + 1) * 128], ident)
                    last.then_inc(S("lin_bcast"), 1)
                for b in range(B):
                    pe.wait_ge(S("lin_att"), b + 1)
                    mm(PS[:, 6 + b, :], wa1[:, 3, :], att[:, b, :]).then_inc(S("lin_proj"), 1)

            def rwkv():
                layernorm(3)
                arrived(pe, "wf1")
                for b in range(B):
                    pe.wait_ge(S("mix_in"), 2 * b + 1)
                    mm(PS[:, 4 + 2 * b, :], wf1[:, 0, :], xc[:, b, :]).then_inc(S("mix_up"), 1)
                    pe.wait_ge(S("mix_in"), 2 * b + 2)
                    mm(PS[:, 5 + 2 * b, :], wf1[:, 1, :], sq[:, b, :]).then_inc(S("mix_up"), 1)
                for b in range(B):
                    pe.wait_ge(S("mix_k2"), b + 1)
                    mm(PS[:, 2 * b, :], wf1[:, 2, :], att[:, b, :]).then_inc(S("mix_v"), 1)

            def experts():
                arrived(pe, "sw13", "sw2", "ew1", "ew2")

                def ups(n):
                    j, b = divmod(n, 2)
                    if n >= 2:
                        pe.wait_ge(S("ex_act"), n - 1)
                        pe.wait_ge(S("ex_prod"), n - 1)
                    if j < 2:
                        mm(PS[:, 2 + n % 2, :], sw13[:, 0, j * 128:(j + 1) * 128], h[b]).then_inc(S("ex_up"), 1)
                        mm(PS[:, 4 + n % 2, :], sw13[:, 1, j * 128:(j + 1) * 128], h[b]).then_inc(S("ex_up"), 1)
                    else:
                        e = j - 2
                        mm(PS[:, 2 + n % 2, :], ew1[:, e, :], h[b]).then_inc(S("ex_up"), 1)
                        for t in range(TB):
                            at = (b * TB + t) * 8 + e
                            last = nc.tensor.transpose(PS[:, 4 + n % 2, t * 128:(t + 1) * 128],
                                                       rt[:, 9, at:at + 1].to_broadcast([128, 128]), ident)
                        last.then_inc(S("ex_up"), 1)

                def downs(n):
                    j, b = divmod(n, 2)
                    pe.wait_ge(S("ex_prod"), n + 1)
                    w = sw2[:, j, :] if j < 2 else ew2[:, j - 2, :]
                    mm(PS[:, b, :], w, PTB[:, n % 4, :], start=(j == 0), stop=(j == 9)).then_inc(S("ex_down"), 1)

                def logits(b):
                    for t in range(TB):
                        n = b * TB + t
                        last = mm(PS[:, 6, n * 8:n * 8 + 8], h[b][:, t * 128:(t + 1) * 128], rw0[:, 8:16])
                    return last

                pe.wait_ge(S("ln_h"), 2 * 5 + 1)
                ln_centre(5, 1)
                logits(0)
                ln_variance(5, 1)
                ups(0)
                ln_spread(5, 1)
                pe.wait_ge(S("ln_h"), 2 * 5 + 2)
                logits(1).then_inc(S("ex_logits"), 1)
                for n in range(1, 21):
                    if n == 4:
                        pe.wait_ge(S("ex_comb"), 1)
                    if n < 20:
                        ups(n)
                    downs(n - 1)


            def final_layer():
                arrived(pe, "const3", "wd")

                def prepare(r, j):
                    b, p = divmod(r, 4)
                    mm(PS[:, pair_bank(r, j), :], wd[:, p * 384 + j * 128:p * 384 + (j + 1) * 128],
                       h[b]).then_inc(S("d_pair"), 1)

                def router(b):
                    mm(PS[0:8, 4 + b, :], rw0[:, 16:24], h[b]).then_inc(S("sp_router"), 1)
                    for t in range(TB):
                        last = nc.tensor.transpose(PS[:, 6 + b, t * 128:(t + 1) * 128], h[b][:, t * 128:(t + 1) * 128],
                                                   ident)
                    last.then_inc(S("sp_tokens"), 1)

                def values(n):
                    b, t = divmod(n, TB)
                    mm(PS[:, 6 + n % 2, :], h[b][:, t * 128:(t + 1) * 128], wd[:, 1536:2048]).then_inc(S("d_values"), 1)

                def scores(u, t):
                    r, z = divmod(u, 2)
                    if u == 0:
                        pe.wait_ge(S("d_first"), 2)
                        pe.wait_ge(S("d_raw"), 8)
                        pe.wait_ge(S("d_swap"), 8)
                    else:
                        pe.wait_ge(S("d_roped"), 2 * (r + 1))
                        if t == 1:
                            pe.wait_ge(S("d_turned"), 3 * u)
                    mm(PS[:, t, (3 - t) * 128:512], QK[r % 3][0:64, z, t * 128:(t + 1) * 128],
                       QK[r % 3][0:64, 2 + z, 0:(t + 1) * 128]).then_inc(S("d_scores"), 1)

                def turn(u, n):
                    pe.wait_ge(S("d_exps"), TB * u + (1, 3, 4)[n])
                    r, z = divmod(u - 1, 2)
                    if n == 0:
                        if u == 0:
                            pe.wait_ge(S("sp_work"), 2)
                        elif z == 0:
                            pe.wait_ge(S("d_swap"), 4 * min(r + 3, NU // 2))
                        elif r > 0:
                            pe.wait_ge(S("d_wide"), r)
                    elif n == 1:
                        if u > 0 and z == 0:
                            pe.wait_ge(S("d_raw"), 4 * min(r + 3, NU // 2))
                        elif u > 0 and r > 0:
                            pe.wait_ge(S("d_normed"), r)
                    bank, blocks = GROUPS[n]
                    for c, (t, k) in enumerate(blocks):
                        last = nc.tensor.transpose(PS[:, bank, c * 128:(c + 1) * 128], PQ[t][:, k * 128:(k + 1) * 128],
                                                   ident)
                    last.then_inc(S("d_groups"), 1)

                def weigh(u, k):
                    b, hd = divmod(u, NHD)
                    pe.wait_ge(S("d_turned"), 3 * u + (3, 3, 2, 1)[k])
                    if k == 3 and u > 0:
                        pe.wait_ge(S("d_taken"), u)
                        pe.wait_ge(S("d_den"), u)
                    at = hd // 2 * 192 + hd % 2 * 64
                    mm(PS[:, 6, k * 128:512], VD[b * TB + k][:, at:at + 128], PTB[:, k, k * 128:512],
                       start=(k == 3), stop=(k == 0)).then_inc(S("d_weighed"), 1)

                def dens(p):
                    pe.wait_ge(S("d_turned"), 3 * min(2 * p + 4, NU) - 2)
                    if p == NU // 2 - 1:
                        pe.wait_ge(S("d_den"), NU)
                    for t in range(TB):
                        last = mm(PS[:, 4, 2 * t:2 * t + 2], dend[:, p % 2, t * 128:(t + 1) * 128], ident[:, 0:128:64])
                    last.then_inc(S("d_dens"), 1)

                def spread(p):
                    pe.wait_ge(S("d_wide"), p + 1)
                    pe.wait_ge(S("d_turned"), 3 * min(2 * p + 4, NU) - 1)
                    for t in range(TB):
                        last = nc.tensor.transpose(PS[:, 5, t * 128:(t + 1) * 128], wide[:, t * 128:(t + 1) * 128], ident)
                    last.then_inc(S("d_spread"), 1)

                def sparse(b, s):
                    if s is None:
                        return
                    if (b, s) == (1, "gather"):
                        pe.wait_ge(S("x_ready"), 2 * 7 + 1)
                    elif s != "columns":
                        pe.wait_ge(S("sp_taken"), made(b, s) - 1 if s != "y" else made(b, "out1"))
                    heads = [slice(hd * 64, hd * 64 + 64) for hd in range(8)]
                    if s == "columns":
                        pe.wait_ge(S("sp_selected"), 1)
                        for t in range(TB):
                            last = nc.tensor.transpose(PS[:, 7, t * 40:t * 40 + 40], wk[:, t * 128:(t + 1) * 128],
                                                       ident[0:40, 0:40])
                    elif s == "ranks":
                        mm(PS[:, 7, 0:64], C("tri"), selT[:, 0, :], stop=False)
                        last = mm(PS[:, 7, 0:64], C("ones"), selT[:, 1, :], start=False)
                    elif s == "gather":
                        pe.wait_ge(S("sp_G"), TB * (b + 1))
                        for t in range(TB):
                            last = mm(PS[:, 7, :], htok[:, b * TB + t, :], PT[:, t, :], start=(t == 0), stop=(t == TB - 1))
                    elif s == "angles":
                        for t in range(TB):
                            last = mm(PS[0:64, 7, :], C3("tab")[:, t * 64:(t + 1) * 64], PT[:, t, :], start=(t == 0),
                                      stop=(t == TB - 1))
                    elif s[:4] == "turn":
                        q = int(s[4:])
                        for t in range(TB):
                            last = nc.tensor.transpose(PS[:, 7, t * 128:(t + 1) * 128], PT[:, t, q * 128:(q + 1) * 128],
                                                       ident)
                    elif s == "swapped":
                        for hd, hs in enumerate(heads):
                            mm(PS[64:128, 7, hd:hd + 1], xg[:, hs], rw0[:, 16 + hd:17 + hd])
                        for hd, hs in enumerate(heads):
                            last = mm(PS[0:64, 7, hs], wm[:, hd * 256 + 128:hd * 256 + 192], xg[:, hs])
                    elif s == "qk":
                        pe.wait_ge(S("sp_gate"), b + 1)
                        for hd, hs in enumerate(heads):
                            last = mm(PS[:, 7, hs], wm[:, hd * 256:hd * 256 + 128], xg[:, hs])
                    elif s == "v":
                        for hd, hs in enumerate(heads):
                            last = mm(PS[0:64, 7, hs], xg[:, hs], wm[:, hd * 256 + 192:hd * 256 + 256])
                    elif s == "scores":
                        pe.wait_ge(S("sp_roped"), b + 1)
                        for hs in heads:
                            last = mm(PS[0:64, 7, hs], sqk[:, 0, hs], sqk[:, 1, hs])
                    elif s == "weights":
                        pe.wait_ge(S("sp_p"), b + 1)
                        for hs in heads:
                            last = nc.tensor.transpose(PS[0:64, 7, hs], spp[:, hs], ident[0:64, 0:64])
                    elif s == "sums":
                        for hs in heads:
                            last = mm(PS[0:64, 7, hs], spv[:, 0, hs], spv[:, 1, hs])
                    elif s in ("out0", "out1"):
                        for j in range(4):
                            hd = 4 * int(s[-1]) + j
                            last = mm(PS[0:64, 7, j * 128:(j + 1) * 128], spo[:, heads[hd]], wom[:, hd, :])
                    elif s == "y":
                        pe.wait_ge(S("d_normed"), NHD // 2 * (b + 1))
                        for q in range(4):
                            mm(PS[:, 7, :], wod[:, q, :], AVT[:, b, q, :], start=(q == 0), stop=False)
                        for q in range(4):
                            last = mm(PS[:, 7, :], spz[:, q, :], GT[q], start=False, stop=(q == 3))
                    last.then_inc(S("last_y" if s == "y" else "sp_product"), 1)

                NU = B * NHD
                pe.wait_ge(S("ln_h"), 2 * 7 + 1)
                for j in range(3):
                    prepare(0, j)
                ln_centre(7, 1)
                router(0)
                ln_variance(7, 1)
                for n in range(TB):
                    if n == 0:
                        pe.wait_ge(S("sp_htok"), 1)
                    if n == 2:
                        ln_spread(7, 1)
                    if n >= 2:
                        pe.wait_ge(S("d_v_placed"), n - 1)
                    values(n)
                pe.wait_ge(S("ln_h"), 2 * 7 + 2)
                pe.wait_ge(S("d_v_placed"), TB)
                router(1)
                pe.wait_ge(S("d_raw"), 4)
                pe.wait_ge(S("d_swap"), 4)
                for j in range(3):
                    prepare(1, j)
                values(4)
                pe.wait_ge(S("sp_htok"), 2)
                values(5)
                for t in ORDER:
                    scores(0, t)
                for n in (6, 7):
                    pe.wait_ge(S("d_v_placed"), n - 1)
                    values(n)
                pe.wait_ge(S("d_v_placed"), NT)
                pe.wait_ge(S("pool_set"), POOL_SET["last"])
                for u in range(NU):
                    r, z = divmod(u, 2)
                    ahead = z == 0 and r + 2 < NU // 2
                    if u == FIRST_SPARSE:
                        arrived(pe, "wm", "wod", "wom")
                    after = lambda *tiles: [scores(u + 1, t) for t in tiles if u + 1 < NU]
                    turn(u, 0)
                    after(3)
                    turn(u, 1)
                    after(2, 0)
                    turn(u, 2)
                    if ahead:
                        pe.wait_ge(S("d_turned"), 3 * u + 2)
                        prepare(r + 2, 0)
                        prepare(r + 2, 1)
                    sparse(*slot(u, 0))
                    after(1)
                    weigh(u, 3)
                    if z == 1 and r > 0:
                        dens(r - 1)
                    weigh(u, 2)
                    if ahead:
                        pe.wait_ge(S("d_raw"), 4 * (r + 2) + 2)
                        prepare(r + 2, 2)
                    weigh(u, 1)
                    sparse(*slot(u, 1))
                    weigh(u, 0)
                    if z == 1 and r > 0:
                        spread(r - 1)
                    sparse(*slot(u, 2))
                pe.wait_ge(S("d_normed"), NU // 2 - 1)
                dens(NU // 2 - 1)
                spread(NU // 2 - 1)
                sparse(1, "y")
            attention(0, 0, wa0)
            moe()
            linear()
            rwkv()
            attention(1, 4, wa2)
            experts()
            attention(2, 6, wa3)
            final_layer()

        @block.scalar
        def _(act):
            A_ = nc.scalar.activation

            def ln_squares(i, b):
                act.wait_ge(S("ln_centered"), 2 * i + b + 1)
                A_(sq[:, b, :], PS[:, centre_bank(i, b), :], ACT.Square).then_inc(S("ln_act"), 1)
                nc.scalar.copy(xc[:, b, :], PS[:, centre_bank(i, b), :]).then_inc(S("ln_act"), 1)

            def layernorm(i):
                for b in range(B):
                    ln_squares(i, b)

            def context(a, kbias, kfunc, obias):
                c = ATTN[a]
                nsub, qd = c["nsub"], c["qd"]
                s_ = lambda n: S("at_" + n)
                act.wait_ge(s_("keys"), before(a, "keys") + 1)
                if a > 0:
                    act.wait_ge(s_("k_built"), before(a, "k_built"))
                    A_(small[:, 11 + a:12 + a], PS[:, KBANK[a], 400:401], ACT.Identity, bias=V(obias))
                for s in range(nsub):
                    src = PS[0:qd, KBANK[a] + s // 2, (s % 2) * 154:(s % 2) * 154 + 154]
                    dst = kT[0:qd, s, :]
                    if a > 0:
                        last = A_(dst, src, kfunc, bias=V(kbias, qd, s))
                    else:
                        last = nc.scalar.copy(dst, src)
                last.then_inc(s_("k_placed"), 1)

            def attention(a, i, qbias):
                c = ATTN[a]
                nsub, nh, qd = c["nsub"], c["nh"], c["qd"]
                s_ = lambda n: S("at_" + n)
                layernorm(i)
                if a == 0:
                    context(0, None, None, None)
                act.wait_ge(s_("q_zeroed"), before(a, "q_zeroed") + 1)
                for b in range(B):
                    for s in range(nsub):
                        if a == 0:
                            act.wait_ge(s_("query"), before(a, "query") + b + 1)
                            nc.scalar.copy(QA[0:qd, b, s, :],
                                           PS[s * qd:(s + 1) * qd, 4 + b, :]).then_inc(s_("q_placed"), 1)
                        else:
                            act.wait_ge(s_("query"), before(a, "query") + nsub * b + s + 1)
                            A_(QA[0:qd, b, s, :], PS[0:qd, 4 + 2 * b + s, :], ACT.Identity,
                               bias=V(qbias, qd, s)).then_inc(s_("q_placed"), 1)
                units = [(b, s) for b in range(B) for s in range(nsub)]
                chunks = c["chunks"]

                def root(b):
                    act.wait_ge(s_("rms_eps"), b + 1)
                    A_(rmsr[:, b, :, :], rms[:, b, :].rearrange("p (t n) -> p t n", t=TB), ACT.Sqrt).then_inc(s_("rms_r"), 1)

                def project(b):
                    act.wait_ge(s_("projected"), before(a, "projected") + b + 1)
                    A_(yb[:, b, :], PS[:, 7, :], ACT.Identity,
                       bias=V("bp") if a == 0 else small[:, 11 + a:12 + a]).then_inc(s_("y_placed"), 1)

                todo = []

                def step():
                    if todo:
                        todo.pop(0)()

                nothing = lambda: None

                def out(u, t):
                    if a != 1:
                        n = TB * u + t
                        nb = c["rows"] // 308
                        act.wait_ge(s_("scores"), before(a, "scores") + n + 1)
                        nc.scalar.copy(WQ[a][t][:, 0:c["rows"]].rearrange("p (j n) -> p j n", j=nb),
                                       PS[:, 2 * (n % 2):2 * (n % 2) + nb, 0:308]).then_inc(s_("left"), 1)

                def weights(u, t):
                    name = "pool_diffs" if t in pool_tiles(c) else "diffs"
                    act.wait_ge(s_(name), tile_done(a, name, u, t))
                    tile = WQ[a][t][:, 0:c["rows"]]
                    A_(tile, tile, ACT.Exp, scale=c["scale"]).then_inc(s_("exps"), 1)

                def unit_weights(u):
                    out(u, 0)
                    weights(u, 0)
                    out(u, 2)
                    for t in range(1, TB):
                        weights(u, t)

                unit_weights(0)
                for u, (b, s) in enumerate(units):
                    for j in range(1, len(chunks), 2):
                        m = chunks[j][1]
                        g = u * len(chunks) + j
                        act.wait_ge(s_("turned_keys"), before(a, "turned_keys") + g + 1)
                        nc.scalar.copy(WK[a][j][0:m, :], PS[0:m, TURNED_BANK[j], :]).then_inc(s_("odd"), 1)
                    if u + 1 < len(units):
                        unit_weights(u + 1)
                    step()
                    if s == nsub - 1:
                        if a == 0:
                            todo += [lambda b=b: root(b)] + [nothing] * (3 if b == 0 else 0)
                        else:
                            todo += [nothing]
                        todo += [lambda b=b: project(b)]
                    if b == 1 and u + 1 < len(units):
                        step()
                ln_squares(i + 1, 0)
                while todo:
                    step()

            def moe():
                ln_squares(1, 1)
                for b in range(B):
                    act.wait_ge(S("moe_logits"), b + 1)
                    nc.scalar.copy(htok[:, b * TB:(b + 1) * TB, :],
                                   PS[:, 4 + b, :].rearrange("p (t f) -> p t f", t=TB)).then_inc(S("moe_htok"), 1)
                act.wait_ge(S("moe_diff"), 1)
                A_(rt[:, 2, :], rt[:, 1, :], ACT.Exp).then_inc(S("moe_exp"), 1)
                context(1, "bk2", ACT.Identity, "bo2")
                context(2, "bk3", ACT.Tanh, "bo3")
                act.wait_ge(S("moe_slots"), 1)
                for k in range(2):
                    nc.scalar.copy(destb[:, k * 512:(k + 1) * 512], PS[:, 4 + k, :]).then_inc(S("moe_bcopied"), 1)
                act.wait_ge(S("moe_slots"), 2)
                for k in range(2):
                    nc.scalar.copy(gateb[:, k * 512:(k + 1) * 512], PS[:, 6 + k, :]).then_inc(S("moe_bcopied"), 1)
                for e in range(E):
                    act.wait_ge(S("moe_up"), e + 1)
                    if e >= 2:
                        act.wait_ge(S("moe_down"), e - 1)
                    A_(hid[:, e % 2, :], PS[:, 4 + e % 2, :], ACT.Gelu_apprx_tanh).then_inc(S("moe_gelu"), 1)

            def linear():
                layernorm(2)
                for b in range(B):
                    act.wait_ge(S("lin_num"), b + 1)
                    nc.scalar.copy(yb[:, b, :], PS[:, 2 * b, :]).then_inc(S("lin_numc"), 1)
                for b in range(B):
                    act.wait_ge(S("lin_proj"), b + 1)
                    act.wait_ge(S("lin_att"), b + 1)
                    A_(yb[:, b, :], PS[:, 6 + b, :], ACT.Identity, bias=V("bo1")).then_inc(S("lin_y"), 1)

            def rwkv():
                layernorm(3)
                for b in range(B):
                    act.wait_ge(S("mix_up"), 2 * b + 1)
                    A_(yb[:, b, :], PS[:, 4 + 2 * b, :], ACT.Sigmoid).then_inc(S("mix_act"), 1)
                    act.wait_ge(S("mix_up"), 2 * b + 2)
                    A_(PTB[:, b, :], PS[:, 5 + 2 * b, :], ACT.Relu).then_inc(S("mix_act"), 1)

            def experts():
                ln_squares(5, 1)
                act.wait_ge(S("ex_logits"), 1)
                A_(rt[:, 0, :], PS[:, 6, 0:64], ACT.Sigmoid).then_inc(S("ex_sig"), 1)
                for n in range(20):
                    act.wait_ge(S("ex_up"), 2 * n + 1)
                    if n >= 4:
                        act.wait_ge(S("ex_prod"), n - 3)
                    A_(PTB[:, 4 + n % 4, :], PS[:, 2 + n % 2, :],
                       ACT.Silu if n < 4 else ACT.Gelu).then_inc(S("ex_act"), 1)


            def final_layer():
                def pair(r, j):
                    act.wait_ge(S("d_pair"), 3 * r + j + 1)
                    if r >= 3:
                        act.wait_ge(S("d_scores"), 2 * TB * (r - 2))
                    for z in range(2):
                        nc.scalar.copy(QK[r % 3][0:64, 2 * j + z, :],
                                       PS[64 * z:64 * z + 64, pair_bank(r, j), :]).then_inc(S("d_raw"), 1)

                def router(b):
                    act.wait_ge(S("sp_router"), b + 1)
                    nc.scalar.copy(wk[32 * b:32 * b + 8, :], PS[0:8, 4 + b, :]).then_inc(S("sp_work"), 1)
                    act.wait_ge(S("sp_tokens"), b + 1)
                    nc.scalar.copy(htok[:, b * TB:(b + 1) * TB, :],
                                   PS[:, 6 + b, :].rearrange("p (t f) -> p t f", t=TB)).then_inc(S("sp_htok"), 1)

                def values(n):
                    act.wait_ge(S("d_values"), n + 1)
                    nc.scalar.copy(VD[n].rearrange("p (q c d) -> p q c d", q=4, c=3)[:, :, 0:3:2, :],
                                   PS[:, 6 + n % 2, :].rearrange("p (q c d) -> p q c d", q=4, c=2)
                                   ).then_inc(S("d_v_placed"), 1)

                def exps(u, *tiles):
                    for t in tiles:
                        act.wait_ge(S("d_max"), TB * u + ORDER.index(t) + 1)
                        A_(PQ[t], PS[:, t, (3 - t) * 128:512], ACT.Exp, scale=HP ** -0.5,
                           bias=mxd[:, u % 2, t:t + 1]).then_inc(S("d_exps"), 1)

                def sparse(b, s):
                    if s in ("gather", "v", "weights", "sums") or s and s[:4] == "turn":
                        out, p = {"gather": (xg, 128), "v": (spv[:, 0, :], 64), "weights": (spv[:, 1, :], 64),
                                  "sums": (spo, 64)}.get(s) or (GT[int(s[4:])], 128)
                        act.wait_ge(S("sp_product"), made(b, s))
                        nc.scalar.copy(out, PS[0:p, 7, :]).then_inc(S("sp_taken"), 1)
                    elif s == "qk":
                        act.wait_ge(S("sp_product"), made(b, s))
                        nc.scalar.copy(sqk[:, 0, :], PS[0:64, 7, :])
                        nc.scalar.copy(sqk[:, 1, :], PS[64:128, 7, :]).then_inc(S("sp_taken"), 1)
                    elif s == "swapped":
                        act.wait_ge(S("sp_product"), made(b, s))
                        A_(sps[:, 0, :], PS[64:128, 7, 0:8], ACT.Exp, scale=-1.0).then_inc(S("sp_gate"), 1)
                    elif s == "scores":
                        act.wait_ge(S("sp_diff"), b + 1)
                        A_(spp, sdiff, ACT.Exp, scale=HP ** -0.5).then_inc(S("sp_p"), 1)

                NU = B * NHD
                pair(0, 0)
                pair(0, 1)
                ln_squares(7, 1)
                act.wait_ge(S("sp_cleared"), 1)
                router(0)
                for n in range(TB):
                    values(n)
                router(1)
                pair(1, 0)
                pair(1, 1)
                for n in range(TB, NT):
                    values(n)
                exps(0, *ORDER)
                for u in range(NU):
                    r, z = divmod(u, 2)
                    act.wait_ge(S("d_groups"), 3 * u + 1)
                    nc.scalar.copy(PTB[:, 0:4, 384:512],
                                   PS[:, 4, :].rearrange("p (k q) -> p k q", k=4)).then_inc(S("d_turned"), 1)
                    act.wait_ge(S("d_groups"), 3 * u + 2)
                    nc.scalar.copy(PTB[:, 0:3, 256:384], PS[:, 5, 0:384].rearrange("p (k q) -> p k q", k=3))
                    nc.scalar.copy(PTB[:, 0, 0:128], PS[:, 5, 384:512]).then_inc(S("d_turned"), 1)
                    act.wait_ge(S("d_groups"), 3 * u + 3)
                    nc.scalar.copy(PTB[:, 0:2, 128:256],
                                   PS[:, 1, 0:256].rearrange("p (k q) -> p k q", k=2)).then_inc(S("d_turned"), 1)
                    if u + 1 < NU:
                        exps(u + 1, 3)
                    if z == 0 and r + 2 < NU // 2:
                        pair(r + 2, 0)
                    if u + 1 < NU:
                        exps(u + 1, 2, 0)
                    sparse(*slot(u, 0))
                    if z == 0 and r + 2 < NU // 2:
                        pair(r + 2, 1)
                    if u + 1 < NU:
                        exps(u + 1, 1)
                    sparse(*slot(u, 1))
                    act.wait_ge(S("d_weighed"), 4 * (u + 1))
                    if z == 0 and r >= 2:
                        act.wait_ge(S("d_dens"), r - 1)
                    nc.scalar.copy(dend[64 * z:64 * z + 64, r % 2, :],
                                   PS[64 - 64 * z:128 - 64 * z, 6, :]).then_inc(S("d_den"), 1)
                    sparse(*slot(u, 2))
            arrived(act, "cols")
            A_(tg[:], V("g"), ACT.Tanh).then_inc(S("gates"), 1)
            act.wait_ge(S("lam_dots"), 2)
            A_(small[:, 2:4], small[:, 0:2], ACT.Exp).then_inc(S("gates"), 1)
            attention(0, 0, None)
            moe()
            linear()
            rwkv()
            attention(1, 4, "bq2")
            experts()
            attention(2, 6, "bq3")
            final_layer()

        @block.vector
        def _(dve):
            link = Chain(dve, "dve_own")
            v = nc.vector

            def ln_eps(i, b):
                dve.wait_ge(S("ln_var"), 2 * i + b + 1)
                v.tensor_scalar(veps[:, b, :], PS[:, 2 * b + 1, 0:TB], EPS, None, ALU.add).then_inc(S("ln_veps"), 1)

            def ln_scale(i, b):
                k = 2 * i + b + 1
                dve.wait_ge(S("ln_bcast"), k)
                dve.wait_ge(S("ln_act"), 2 * k)
                v.tensor_tensor(h[b], xc[:, b, :], PS[:, 2 * b + 1, :], ALU.mult).then_inc(S("ln_h"), 1)

            def layernorm(i):
                for part in (ln_eps, ln_scale):
                    for b in range(B):
                        part(i, b)

            def widen(dst, src, width):
                n = src.shape[2]
                return v.tensor_copy(dst.rearrange("p (t n w) -> p t n w", t=TB, n=n),
                                     src.unsqueeze(3).to_broadcast([128, TB, n, width]))

            def residual(b, gate):
                v.scalar_tensor_tensor(xb[b], yb[:, b, :], tg[:, gate:gate + 1], xb[b], ALU.mult,
                                       ALU.add).then_inc(S("x_ready"), 1)

            def context(a):
                c = ATTN[a]
                nh, chunks = c["nh"], c["chunks"]
                s_ = lambda n: S("at_" + n)
                vm = C("vmask8" if nh == 8 else "vmask16").rearrange("p (c f) -> p c f", f=64)
                full = [j for j, (_, m) in enumerate(chunks) if m == 128]
                for b in range(B):
                    dve.wait_ge(s_("values"), before(a, "values") + b + 1)
                    for z in range(2):
                        n = len(full)
                        v.tensor_tensor(VA[a][:, b, z, 0:n, 0:64],
                                        PS[:, VBANK[a][b], 0:n * 128].rearrange("p (c f) -> p c f", f=128)[:, :, z * 64:z * 64 + 64],
                                        vm[:, 0:n, :], ALU.mult)
                        m = chunks[-1][1]
                        at = (n % 4) * 128 + z * 64
                        last = v.tensor_tensor(VA[a][0:m, b, z, n, 0:64], PS[0:m, VBANK[a][b] + n // 4, at:at + 64], vm[0:m, n, :],
                                               ALU.mult)
                    last.then_inc(s_("v_placed"), 1)

            def attention(a, i, layer):
                c = ATTN[a]
                nsub, nh, qd = c["nsub"], c["nh"], c["qd"]
                chunks = c["chunks"]
                s_ = lambda n: S("at_" + n)
                if a == 0:
                    context(0)
                layernorm(i)
                units = [(b, s) for b in range(B) for s in range(nsub)]

                def differences(u, t):
                    b, s = units[u]
                    n = TB * u + t
                    nb = c["rows"] // 308
                    view = lambda x: x.rearrange("p (j h k) -> p j h k", j=nb, k=SK)
                    tile = view(WQ[a][t][:, 0:c["rows"]])
                    src = PS[:, 2 * (n % 2):2 * (n % 2) + nb, 0:308].rearrange("p j (h k) -> p j h k", k=SK)
                    m = mx[:, n % 2, 0:nh]
                    dve.wait_ge(s_("scores"), before(a, "scores") + n + 1)
                    if a == 1:
                        for j in range(nb):
                            ins = v.tensor_tensor(tile[:, j], src[:, j], mbias[:, t, :].unsqueeze(1).to_broadcast([128, 4, SK]),
                                                  ALU.add)
                        ins.then_inc(s_("left"), 1)
                        dve.wait_ge(s_("left"), tile_done(a, "left", u, t))
                        src = tile
                        if n >= 2:
                            dve.wait_ge(s_("pool_diffs"), before(a, "pool_diffs") + n - 1)
                        link(v.tensor_reduce(m.rearrange("p (j h) -> p j h", j=nb), src, AX.X, ALU.max))
                        v.tensor_scalar(m, m, 0.5 * NEG, None, ALU.max).then_inc(s_("max_taken"), 1)
                    elif t in pool_tiles(c):
                        dve.wait_ge(s_("left"), tile_done(a, "left", u, t))
                        if u or t:
                            w_, t_ = divmod(n - 2, TB)
                            dve.wait_ge(s_("pool_diffs"), tile_done(a, "pool_diffs", w_, t_))
                        v.tensor_reduce(m.rearrange("p (j h) -> p j h", j=nb), tile, AX.X, ALU.max).then_inc(s_("max_taken"), 1)
                    else:
                        link(v.tensor_reduce(m.rearrange("p (j h) -> p j h", j=nb), src, AX.X, ALU.max))
                        mb = m.rearrange("p (j h) -> p j h", j=nb).unsqueeze(3).to_broadcast([128, nb, 4, SK])
                        v.tensor_tensor(tile, src, mb, ALU.subtract).then_inc(s_("diffs"), 1)

                def take(u):
                    b, s = units[u]
                    dve.wait_ge(s_("weighed"), before(a, "weighed") + u + 1)
                    z = s % 2
                    o = PS[:, 6, 0:TB * (64 + nh)].rearrange("p (t n) -> p t n", t=TB)
                    heads = lambda t: t.rearrange("p t (n f) -> p t n f", n=nh)
                    link(v.reciprocal(rec[:, b, :, 0:nh], o[:, :, 64:64 + nh]))
                    share = rec[:, b, :, 0:nh].unsqueeze(3).to_broadcast([128, TB, nh, 64 // nh])
                    dst = OT[:, b, 0, :].rearrange("p (t f) -> p t f", t=TB)[:, :, 64 * z:64 * z + 64]
                    if s < 2:
                        v.tensor_tensor(heads(dst), heads(o[:, :, 0:64]), share, ALU.mult).then_inc(s_("o_taken"), 1)
                    else:
                        second = OT[:, b, 1, 0:TB * 64].rearrange("p (t f) -> p t f", t=TB)
                        link(v.tensor_tensor(heads(second), heads(o[:, :, 0:64]), share, ALU.mult))
                        v.scalar_tensor_tensor(dst, second, small[:, 4:5], dst, ALU.mult, ALU.add).then_inc(s_("o_taken"), 1)

                def mean_squares(b):
                    dve.wait_ge(s_("o_taken"), nsub * (b + 1))
                    link(v.tensor_tensor(OT[:, b, 1, :], OT[:, b, 0, :], OT[:, b, 0, :], ALU.mult))
                    link(v.tensor_reduce(rms[:, b, :], OT[:, b, 1, :].rearrange("p (n f) -> p n f", f=8), AX.X, ALU.add))
                    link(v.tensor_scalar(rms[:, b, :], rms[:, b, :], 1.0 / 8.0, EPS, ALU.mult, ALU.add))
                    v.reciprocal(rms[:, b, :], rms[:, b, :]).then_inc(s_("rms_eps"), 1)

                def scale(b):
                    dve.wait_ge(s_("rms_r"), b + 1)
                    sums = OT[:, b, 0, :].rearrange("p (n f) -> p n f", f=8)
                    v.tensor_tensor(sums, sums, rmsr[:, b, :, :].rearrange("p t n -> p (t n)").unsqueeze(2)
                                    .to_broadcast([128, 64, 8]), ALU.mult).then_inc(s_("rms_done"), 1)

                def place(b):
                    dve.wait_ge(s_("turned"), before(a, "turned") + b + 1)
                    if a == 0:
                        ins = v.tensor_scalar(att[:, b, :], PS[:, 7, :], small[:, 5:6], None, ALU.mult)
                    else:
                        ins = v.tensor_copy(att[:, b, :], PS[:, 7, :])
                    ins.then_inc(s_("att_done"), 1)

                def add(b):
                    dve.wait_ge(s_("y_placed"), before(a, "y_placed") + b + 1)
                    if a == 2:
                        link(v.tensor_tensor(yb[:, b, :], yb[:, b, :], mask3f[:, b * T:(b + 1) * T], ALU.mult))
                    residual(b, layer)

                todo = []

                def step():
                    if todo:
                        todo.pop(0)()

                for t in range(TB):
                    differences(0, t)
                for u, (b, s) in enumerate(units):
                    for j in range(0, len(chunks), 2):
                        m = chunks[j][1]
                        g = u * len(chunks) + j
                        dve.wait_ge(s_("turned_keys"), before(a, "turned_keys") + g + 1)
                        v.tensor_copy(WK[a][j][0:m, :], PS[0:m, TURNED_BANK[j], :]).then_inc(s_("even"), 1)
                    for t in range(TB):
                        if u + 1 < len(units):
                            differences(u + 1, t)
                    step()
                    take(u)
                    if s == nsub - 1:
                        if a == 0:
                            if b == 0:
                                todo += [lambda: mean_squares(0), lambda: None]
                            else:
                                mean_squares(b)
                            todo += [lambda b=b: scale(b)]
                        todo += [lambda b=b: place(b), lambda b=b: add(b)]
                    if b == 1 and u + 1 < len(units):
                        step()
                if a > 0:
                    step()
                ln_eps(i + 1, 0)
                if a > 0:
                    step()
                ln_scale(i + 1, 0)
                while todo:
                    step()

            def first_max(vals, out_, tmp, m):
                v3 = lambda t: t.rearrange("p (t e) -> p t e", e=8)
                link(v.tensor_reduce(m, v3(vals), AX.X, ALU.max))
                link(v.tensor_tensor(v3(tmp), v3(vals), m.unsqueeze(2).to_broadcast([128, 8, 8]), ALU.is_equal))
                link(v.tensor_tensor(tmp, tmp, C("firstw"), ALU.mult))
                link(v.tensor_reduce(m, v3(tmp), AX.X, ALU.max))
                link(v.tensor_tensor(v3(out_), v3(tmp), m.unsqueeze(2).to_broadcast([128, 8, 8]), ALU.is_equal))

            v3 = lambda t: t.rearrange("p (t e) -> p t e", e=8)

            def moe():
                ln_eps(1, 1)
                ln_scale(1, 1)
                dve.wait_ge(S("moe_logits"), 2)
                link(v.tensor_copy(rt[:, 0, :], PS[:, 6, 0:64]))
                link(v.tensor_reduce(r8t[:, 0, :], v3(rt[:, 0, :]), AX.X, ALU.max))
                v.tensor_tensor(v3(rt[:, 1, :]), v3(rt[:, 0, :]), r8t[:, 0, :].unsqueeze(2).to_broadcast([128, 8, 8]),
                                ALU.subtract).then_inc(S("moe_diff"), 1)
                first_max(rt[:, 0, :], rt[:, 3, :], rt[:, 5, :], r8t[:, 1, :])
                link(v.memset(rt[:, 4, 0:8], 0.0))
                for t in range(1, NT):
                    ins = v.tensor_tensor(rt[:, 4, t * 8:t * 8 + 8], rt[:, 4, t * 8 - 8:t * 8], rt[:, 3, t * 8 - 8:t * 8],
                                          ALU.add)
                    if t < NT - 1:
                        link(ins)
                ins.then_inc(S("moe_prefix"), 1)
                dve.wait_ge(S("moe_exp"), 1)
                link(v.tensor_reduce(r8t[:, 7, :], v3(rt[:, 2, :]), AX.X, ALU.add))
                link(v.reciprocal(r8t[:, 6, :], r8t[:, 7, :]))
                dve.wait_ge(S("moe_cum"), 1)
                link(v.tensor_tensor(rt[:, 6, :], PS[:, 7, 0:64], rt[:, 3, :], ALU.mult))
                link(v.tensor_reduce(r8t[:, 2, :], v3(rt[:, 6, :]), AX.X, ALU.add))
                link(v.tensor_tensor(rt[:, 7, :], C("slot0"), rt[:, 3, :], ALU.mult))
                link(v.tensor_reduce(r8t[:, 3, :], v3(rt[:, 7, :]), AX.X, ALU.add))
                link(v.tensor_scalar(r8t[:, 4, :], r8t[:, 2, :], float(CAP), 4096.0, ALU.is_gt, ALU.mult))
                link(v.tensor_tensor(r8t[:, 4, :], r8t[:, 4, :], r8t[:, 3, :], ALU.add))
                link(v.scalar_tensor_tensor(r8t[:, 5, :], r8t[:, 2, :], -1.0, r8t[:, 4, :], ALU.add, ALU.add))
                dve.wait_ge(S("pool_set"), POOL_SET["iota"])
                for t in range(NT):
                    if t >= 2:
                        dve.wait_ge(S("moe_gathered"), t - 1)
                    if t == 2:
                        context(1)
                    v.tensor_scalar(G[:, t % 2, :], pool_iota[:], r8t[:, 5, t:t + 1], None,
                                    ALU.is_equal).then_inc(S("moe_G"), 1)
                dve.wait_ge(S("moe_gathered"), NT)
                for k in range(2):
                    v.tensor_copy(ein[:, k * 512:(k + 1) * 512], PS[:, k, :]).then_inc(S("moe_ein"), 1)
                context(2)
                dve.wait_ge(S("moe_bcopied"), 4)
                for e in range(E):
                    if e >= 2:
                        dve.wait_ge(S("moe_combined"), e - 1)
                    v.tensor_scalar(G[:, e % 2, :], destb[:], C("slotid")[:, e:e + 1], None,
                                    ALU.is_equal).then_inc(S("moe_GT"), 1)
                    dve.wait_ge(S("moe_down"), e + 1)
                    v.tensor_copy(eo[:, e % 2, :], PS[:, 6 + e % 2, 0:128]).then_inc(S("moe_eo"), 1)
                dve.wait_ge(S("moe_combined"), E)
                for b in range(B):
                    link(v.tensor_tensor(yb[:, b, :], gateb[:, b * T:(b + 1) * T], PS[:, 2 + b, :], ALU.mult))
                    residual(b, 4)

            def linear():
                dve.wait_ge(S("lin_kv"), 1)
                link(v.tensor_scalar(kf[:], PS[0:SK, 4, 0:256].rearrange("p (b f) -> p b f", b=B), 8 ** -0.5, 0.0,
                                     ALU.mult, ALU.max))
                link(v.tensor_scalar(kf[:], kf[:], 1e-6, None, ALU.add))
                v.tensor_copy(vs[:], PS[0:SK, 4, 256:512].rearrange("p (b f) -> p b f", b=B)).then_inc(S("lin_kf"), 1)
                layernorm(2)
                dve.wait_ge(S("lin_sum"), 1)
                v.tensor_tensor(kvm[:], PS[:, 5, 0:256].rearrange("p (b f) -> p b f", b=B),
                                C("block8").unsqueeze(1).to_broadcast([128, B, 128]), ALU.mult)
                v.tensor_tensor(ksh[:], PS[:, 5, 256:288].rearrange("p (b f) -> p b f", b=B),
                                C("head8").unsqueeze(1).to_broadcast([128, B, 16]), ALU.mult).then_inc(S("lin_kvm"), 1)
                for b in range(B):
                    dve.wait_ge(S("lin_q"), b + 1)
                    link(v.tensor_scalar(qf[:, b, :], PS[:, 6 + b, :], V("bq1"), 8 ** -0.5, ALU.add, ALU.mult))
                    v.tensor_scalar(qf[:, b, :], qf[:, b, :], 0.0, 1e-6, ALU.max, ALU.add).then_inc(S("lin_qf"), 1)
                for b in range(B):
                    dve.wait_ge(S("lin_num"), b + 1)
                    link(v.tensor_scalar(rms[:, b, :], PS[:, 4 + b, 0:64], 1e-8, None, ALU.add))
                    link(v.reciprocal(rmsr[:, b, :, :], rms[:, b, :].rearrange("p (t n) -> p t n", t=TB)))
                    widen(xc[:, b, :], rmsr[:, b, :, :], 8).then_inc(S("lin_rec"), 1)
                for b in range(B):
                    dve.wait_ge(S("lin_bcast"), b + 1)
                    dve.wait_ge(S("lin_numc"), b + 1)
                    v.tensor_tensor(att[:, b, :], yb[:, b, :], PS[:, 2 * b + 1, :], ALU.mult).then_inc(S("lin_att"), 1)
                for b in range(B):
                    dve.wait_ge(S("lin_y"), b + 1)
                    residual(b, 1)

            def rwkv():
                layernorm(3)
                for b in range(B):
                    dve.wait_ge(S("ln_h"), 2 * 3 + b + 1)
                    for mu, dst in ((0, xc), (1, sq)):
                        link(v.tensor_scalar(dst[:, b, :], hp[:, b, 0:T], small[:, 6 + mu:7 + mu], None, ALU.mult))
                        v.scalar_tensor_tensor(dst[:, b, :], h[b], V("mur" if mu == 0 else "muk"), dst[:, b, :],
                                               ALU.mult, ALU.add).then_inc(S("mix_in"), 1)
                for b in range(B):
                    dve.wait_ge(S("mix_act"), 2 * b + 2)
                    v.tensor_tensor(att[:, b, :], PTB[:, b, :], PTB[:, b, :], ALU.mult).then_inc(S("mix_k2"), 1)
                for b in range(B):
                    dve.wait_ge(S("mix_v"), b + 1)
                    link(v.tensor_tensor(yb[:, b, :], yb[:, b, :], PS[:, 2 * b, :], ALU.mult))
                    residual(b, 5)

            def experts():
                ln_eps(5, 1)
                ln_scale(5, 1)
                dve.wait_ge(S("ex_sig"), 1)

                def routing():
                    link(v.tensor_tensor(rt[:, 1, :], rt[:, 0, :], V("rbias"), ALU.add))
                    first_max(rt[:, 1, :], rt[:, 2, :], rt[:, 5, :], r8t[:, 0, :])
                    link(v.scalar_tensor_tensor(rt[:, 1, :], rt[:, 2, :], NEG, rt[:, 1, :], ALU.mult, ALU.add))
                    first_max(rt[:, 1, :], rt[:, 3, :], rt[:, 5, :], r8t[:, 0, :])
                    link(v.tensor_tensor(rt[:, 2, :], rt[:, 2, :], rt[:, 3, :], ALU.add))
                    link(v.tensor_tensor(rt[:, 4, :], rt[:, 2, :], rt[:, 0, :], ALU.mult))
                    link(v.tensor_reduce(r8t[:, 1, :], v3(rt[:, 4, :]), AX.X, ALU.add))
                    link(v.tensor_scalar(r8t[:, 2, :], r8t[:, 1, :], 1e-9, None, ALU.add))
                    link(v.reciprocal(r8t[:, 3, :], r8t[:, 2, :]))
                    link(v.tensor_scalar(r8t[:, 4, :], r8t[:, 1, :], 1e-9, None, ALU.is_gt))
                    link(v.tensor_tensor(r8t[:, 3, :], r8t[:, 3, :], r8t[:, 4, :], ALU.mult))
                    link(v.tensor_scalar(r8t[:, 4, :], r8t[:, 4, :], -0.5, 0.5, ALU.mult, ALU.add))
                    link(v.tensor_tensor(v3(rt[:, 4, :]), v3(rt[:, 4, :]),
                                         r8t[:, 3, :].unsqueeze(2).to_broadcast([128, 8, 8]), ALU.mult))
                    link(v.tensor_tensor(v3(rt[:, 2, :]), v3(rt[:, 2, :]),
                                         r8t[:, 4, :].unsqueeze(2).to_broadcast([128, 8, 8]), ALU.mult))
                    v.tensor_tensor(rt[:, 9, :], rt[:, 4, :], rt[:, 2, :], ALU.add).then_inc(S("ex_comb"), 1)

                routing()
                for n in range(20):
                    dve.wait_ge(S("ex_act"), n + 1)
                    dve.wait_ge(S("ex_up"), 2 * n + 2)
                    if n >= 4:
                        dve.wait_ge(S("ex_down"), n - 3)
                    v.tensor_tensor(PTB[:, n % 4, :], PTB[:, 4 + n % 4, :], PS[:, 4 + n % 2, :],
                                    ALU.mult).then_inc(S("ex_prod"), 1)
                for b in range(B):
                    dve.wait_ge(S("ex_down"), 19 + b)
                    v.scalar_tensor_tensor(xb[b], PS[:, b, :], tg[:, 6:7], xb[b], ALU.mult,
                                           ALU.add).then_inc(S("x_ready"), 1)


            def final_layer():
                v.memset(wk, 0.0).then_inc(S("sp_cleared"), 1)

                def swap(r):
                    dve.wait_ge(S("d_pair"), 3 * r + 3)
                    if r >= 1:
                        dve.wait_ge(S("d_roped"), 2 * r)
                    for j in range(4):
                        v.tensor_tensor(den4[:, j, :], PS[32 * j:32 * j + 32, pair_bank(r, 2), :], C3("ropes", 0, 32),
                                        ALU.mult).then_inc(S("d_swap"), 1)

                def maxima(u, *tiles):
                    for t in tiles:
                        dve.wait_ge(S("d_scores"), TB * u + ORDER.index(t) + 1)
                        link(v.tensor_tensor(PS[:, t, 384:512], PS[:, t, 384:512], C3("causal"), ALU.add))
                        m = mxd[:, u % 2, t:t + 1]
                        link(v.tensor_reduce(m, PS[:, t, (3 - t) * 128:512], AX.X, ALU.max))
                        v.tensor_scalar(m, m, -HP ** -0.5, None, ALU.mult).then_inc(S("d_max"), 1)

                def take(u):
                    b, hd = divmod(u, NHD)
                    mine = slice(64 * (hd % 2), 64 * (hd % 2) + 64)
                    dve.wait_ge(S("d_weighed"), 4 * (u + 1))
                    v.tensor_copy(AVT[mine, b, hd // 2, :], PS[mine, 6, :]).then_inc(S("d_taken"), 1)

                def recip(p):
                    dve.wait_ge(S("d_dens"), p + 1)
                    link(v.reciprocal(recd[:], PS[:, 4, 0:2 * TB].rearrange("p (t n) -> p t n", n=2)))
                    widen(wide, recd[:], 64).then_inc(S("d_wide"), 1)

                def norm(p):
                    b, q = divmod(p, 4)
                    dve.wait_ge(S("d_spread"), p + 1)
                    v.tensor_tensor(AVT[:, b, q, :], AVT[:, b, q, :], PS[:, 5, :], ALU.mult).then_inc(S("d_normed"), 1)

                def top(n):
                    if n == 0:
                        dve.wait_ge(S("sp_work"), 2)
                    link(v.max(m8[:], wk))
                    link(v.match_replace(wk, m8[:], wk, -BIG))

                def one_hots(b):
                    for t in range(TB):
                        at = t * 16 + b * 8
                        v.tensor_tensor(PT[:, t, :].rearrange("p (h s) -> p h s", h=8),
                                        C3("iota64").unsqueeze(1).to_broadcast([128, 8, 64]),
                                        selT[:, 2, at:at + 8].unsqueeze(2).to_broadcast([128, 8, 64]),
                                        ALU.is_equal).then_inc(S("sp_G"), 1)

                h64 = lambda t: t.rearrange("p (h s) -> p h s", h=8)

                def sparse(b, s):
                    def product():
                        dve.wait_ge(S("sp_product"), made(b, s))
                    if s == "columns":
                        product()
                        for c in range(B):
                            link(v.tensor_copy(selT[:, 0, :].rearrange("p (t n) -> p t n", t=TB)[:, :, 8 * c:8 * c + 8],
                                               PS[:, 7, 0:160].rearrange("p (t n) -> p t n", t=TB)[:, :, 32 * c:32 * c + 8]))
                        link(v.memset(selT[:, 1, 0:16], 0.0))
                        for t in range(1, TB):
                            ins = v.tensor_tensor(selT[:, 1, t * 16:t * 16 + 16], selT[:, 1, t * 16 - 16:t * 16],
                                                  selT[:, 0, t * 16 - 16:t * 16], ALU.add)
                            if t < TB - 1:
                                link(ins)
                        ins.then_inc(S("sp_taken"), 1)
                    elif s == "ranks":
                        product()
                        v.tensor_tensor(selT[:, 2, :], PS[:, 7, 0:64], selT[:, 0, :], ALU.mult).then_inc(S("sp_taken"), 1)
                        dve.wait_ge(S("sp_taken"), made(b, s))
                        link(v.tensor_scalar(selT[:, 2, :], selT[:, 2, :], -1.0, None, ALU.add))
                        one_hots(0)
                    elif s == "angles":
                        product()
                        v.tensor_copy(trig[:, 0, :], PS[0:32, 7, :])
                        v.tensor_copy(trig[:, 1, :], PS[32:64, 7, :]).then_inc(S("sp_taken"), 1)
                    elif s == "swapped":
                        product()
                        for j in range(2):
                            ins = v.tensor_tensor(trig[:, 2 + j, :], PS[32 * j:32 * j + 32, 7, :], trig[:, 1, :], ALU.mult)
                        ins.then_inc(S("sp_taken"), 1)
                    elif s == "qk":
                        dve.wait_ge(S("sp_taken"), made(b, s))
                        link(v.tensor_tensor(sqk[0:32, :, :], sqk[0:32, :, :],
                                             trig[:, 0, :].unsqueeze(1).to_broadcast([32, 2, T]), ALU.mult))
                        v.tensor_tensor(sqk[0:32, :, :], sqk[0:32, :, :], trig[:, 2:4, :],
                                        ALU.add).then_inc(S("sp_roped"), 1)
                    elif s == "scores":
                        product()
                        v.tensor_tensor(h64(sdiff), h64(PS[0:64, 7, :]),
                                        C3("causal", 0, 64)[:, 0:64].unsqueeze(1).to_broadcast([64, 8, 64]),
                                        ALU.add).then_inc(S("sp_taken"), 1)
                        dve.wait_ge(S("sp_taken"), made(b, s))
                        link(v.tensor_reduce(sps[:, 1, :], h64(sdiff), AX.X, ALU.max))
                        v.tensor_tensor(h64(sdiff), h64(sdiff), sps[:, 1, :].unsqueeze(2).to_broadcast([64, 8, 64]),
                                        ALU.subtract).then_inc(S("sp_diff"), 1)
                    elif s == "weights":
                        dve.wait_ge(S("sp_p"), b + 1)
                        link(v.tensor_reduce(sps[:, 2, :], h64(spp), AX.X, ALU.add))
                        dve.wait_ge(S("sp_gate"), b + 1)
                        link(v.scalar_tensor_tensor(sps[:, 3, :], sps[:, 0, :], 1.0, sps[:, 2, :], ALU.add, ALU.mult))
                        link(v.reciprocal(sps[:, 3, :], sps[:, 3, :]))
                    elif s == "turn3" and b == 0:
                        product()
                        one_hots(1)
                    elif s in ("out0", "out1"):
                        a = int(s[-1])
                        product()
                        for z in range(2):
                            ins = v.tensor_tensor(
                                spz[64 * z:64 * z + 64, 2 * a:2 * a + 2, :],
                                PS[0:64, 7, :].rearrange("p (c z d) -> p c z d", c=2, z=2)[:, :, z, :],
                                sps[:, 3, 4 * a:4 * a + 4].rearrange("p (c z) -> p c z", c=2)[:, :, z].unsqueeze(2)
                                .to_broadcast([64, 2, 128]), ALU.mult)
                        ins.then_inc(S("sp_taken"), 1)
                    elif s == "y":
                        dve.wait_ge(S("last_y"), b + 1)
                        v.scalar_tensor_tensor(xb[b], PS[:, 7, :], tg[:, 7:8], xb[b], ALU.mult,
                                               ALU.add).then_inc(S("x_ready"), 1)

                NU = B * NHD
                swap(0)
                ln_eps(7, 1)
                dve.wait_ge(S("d_swap"), 4)
                dve.wait_ge(S("d_raw"), 4)
                first = QK[0][0:32, 0:4:2, :]
                v.tensor_tensor(first, first, C3("ropec", 0, 32).unsqueeze(1).to_broadcast([32, 2, T]),
                                ALU.mult).then_inc(S("d_first"), 1)
                dve.wait_ge(S("d_first"), 1)
                v.tensor_tensor(first, first, den4[:, 0:4:2, :], ALU.add).then_inc(S("d_first"), 1)
                ln_scale(7, 1)
                for n in range(2):
                    top(n)
                swap(1)
                maxima(0, *ORDER)
                for u in range(NU):
                    r, z = divmod(u, 2)
                    if u + 1 < NU:
                        maxima(u + 1, 3, 2, 0)
                    sparse(*slot(u, 0))
                    if u + 1 < NU:
                        maxima(u + 1, 1)
                    if z == 0 and r + 2 < NU // 2:
                        swap(r + 2)
                    if z == 1 and r > 0:
                        recip(r - 1)
                    sparse(*slot(u, 1))
                    for n in ((2, 3), (4, 5), (6,), (7,))[u] if u < 4 else ():
                        top(n)
                    if 4 + u == SEL // 8 - 1:
                        v.tensor_scalar(wk, wk, -BIG, None, ALU.is_equal).then_inc(S("sp_selected"), 1)
                    take(u)
                    if z == 1 and r > 0:
                        norm(r - 1)
                    sparse(*slot(u, 2))
                recip(NU // 2 - 1)
                norm(NU // 2 - 1)
                sparse(1, "y")
            arrived(dve, "cols", "const")
            link(v.tensor_tensor(small[:, 8:12], V("lq1"), V("lk1"), ALU.mult))
            v.tensor_reduce(small[:, 0:1], small[:, 8:12], AX.X, ALU.add).then_inc(S("lam_dots"), 1)
            dve.wait_ge(S("lam_dots"), 1)
            link(v.tensor_tensor(small[:, 8:12], V("lq2"), V("lk2"), ALU.mult))
            v.tensor_reduce(small[:, 1:2], small[:, 8:12], AX.X, ALU.add).then_inc(S("lam_dots"), 1)
            dve.wait_ge(S("gates"), 2)
            link(v.tensor_tensor(small[:, 4:5], small[:, 3:4], small[:, 2:3], ALU.subtract))
            link(v.tensor_scalar(small[:, 4:5], small[:, 4:5], -LAMBDA_INIT, None, ALU.add))
            link(v.tensor_scalar(small[:, 5:6], V("subln"), 1.0 - LAMBDA_INIT, None, ALU.mult))
            link(v.tensor_scalar(small[:, 6:7], V("mur"), -1.0, 1.0, ALU.mult, ALU.add))
            link(v.tensor_scalar(small[:, 7:8], V("muk"), -1.0, 1.0, ALU.mult, ALU.add))
            dve.wait_ge(S("gates"), 2)
            attention(0, 0, 0)
            moe()
            linear()
            rwkv()
            dve.wait_ge(S("pool_set"), POOL_SET["mbias"])
            attention(1, 4, 2)
            experts()
            dve.wait_ge(S("pool_set"), POOL_SET["mask3"])
            attention(2, 6, 3)
            final_layer()

        @block.gpsimd
        def _(pool):
            g = nc.gpsimd

            def layernorm(i):
                for b in range(B):
                    pool.wait_ge(S("ln_veps"), 2 * i + b + 1)
                    g.tensor_tensor(rstd[:, b, :], veps[:, b, :], mhalf[:], ALU.pow).then_inc(S("ln_rstd"), 1)

            def zero_queries(a):
                c = ATTN[a]
                if a > 0:
                    pool.wait_ge(S("ln_rstd"), 8 if a == 1 else 12)
                g.memset(QA if a == 0 else QA[c["qd"]:128, :, 0:c["nsub"]], 0.0).then_inc(S("at_q_zeroed"), 1)
                pool.wait_ge(S("at_q_zeroed"), a + 1)

            def build(a, b):
                c = ATTN[a]
                qd = c["qd"]
                km = C({0: "kmask4", 1: "kmask8", 2: "kmask16"}[a], qd)
                if b == 0:
                    pool.wait_ge(S("at_k_placed"), before(a, "k_placed") + 1)
                for s in range(c["nsub"]):
                    g.tensor_tensor(KA[a][0:qd, b, s, :].rearrange("p (n k) -> p n k", k=SK),
                                    kT[0:qd, s, b * SK:(b + 1) * SK].unsqueeze(1).to_broadcast([qd, c["nh"], SK]),
                                    km.unsqueeze(2).to_broadcast([qd, c["nh"], SK]), ALU.mult).then_inc(S("at_k_built"), 1)

            def differences(a):
                c = ATTN[a]
                for u in range(B * c["nsub"]):
                    for t in pool_tiles(c):
                        tile = WQ[a][t][:, 0:c["rows"]].rearrange("p (n k) -> p n k", k=SK)
                        pool.wait_ge(S("at_max_taken"), tile_done(a, "max_taken", u, t))
                        g.tensor_tensor(tile, tile, mx[:, t % 2, 0:c["nh"]].unsqueeze(2).to_broadcast([128, c["nh"], SK]),
                                        ALU.subtract).then_inc(S("at_pool_diffs"), 1)

            def final_layer():
                layernorm(7)

                def rope(r):
                    qk, swapped = QK[r % 3][0:32], den4[:]
                    if r == 0:
                        qk, swapped = qk[:, 1:4:2, :], den4[:, 1:4:2, :]
                    pool.wait_ge(S("d_raw"), 4 * (r + 1))
                    g.tensor_tensor(qk, qk, C3("ropec", 0, 32).unsqueeze(1).to_broadcast([32, qk.shape[1], T]),
                                    ALU.mult).then_inc(S("d_roped"), 1)
                    pool.wait_ge(S("d_roped"), 2 * r + 1)
                    pool.wait_ge(S("d_swap"), 4 * (r + 1))
                    g.tensor_tensor(qk, qk, swapped, ALU.add).then_inc(S("d_roped"), 1)

                rope(0)
                pool.wait_ge(S("d_roped"), 2)
                for ones in (keys[:, 0:6 * 768], mask3f[:, 0:768], ctxf[:, 0:768]):
                    g.memset(ones.rearrange("p (n d) -> p n d", d=192)[:, :, 64:128], 1.0).then_inc(S("pool_set"), 1)
                pool.wait_ge(S("pool_set"), POOL_SET["last"])
                for r in range(1, B * NHD // 2):
                    rope(r)

            g.memset(keys[:, :], 0.0).then_inc(S("pool_set"), 1)
            g.memset(mhalf[:], -0.5).then_inc(S("pool_set"), 1)
            g.memset(hp[:, :, 0:1], 0.0).then_inc(S("pool_set"), 1)
            pool.wait_ge(S("pool_set"), 3)
            arrived(pool, "const")
            for a, one, nh in ((0, "vone8", 8), (2, "vone16", 4)):
                for b in range(B):
                    for z in range(2):
                        last = g.tensor_copy(VA[a][:, b, z, :, 64:64 + nh], C(one).rearrange("p (c n) -> p c n", n=nh))
                        last.then_inc(S("pool_set"), 1)
            zero_queries(0)
            build(0, 0)
            layernorm(0)
            build(0, 1)
            differences(0)
            g.iota(pool_iota[:], [[1, 1024]], base=0, channel_multiplier=0,
                   allow_small_or_imprecise_dtypes=True).then_inc(S("pool_set"), 1)
            layernorm(1)
            for a in (1, 2):
                for b in range(B):
                    build(a, b)
            arrived(pool, "maskq", "mask3")
            g.tensor_scalar(mbias[:], maskq[:], NEG, None, ALU.mult).then_inc(S("pool_set"), 1)
            g.tensor_copy(mask3f[:], mask3).then_inc(S("pool_set"), 1)
            layernorm(2)
            layernorm(3)
            pool.wait_ge(S("x_ready"), 2 * 4)
            zero_queries(1)
            layernorm(4)
            differences(1)
            layernorm(5)
            pool.wait_ge(S("x_ready"), 2 * 6)
            zero_queries(2)
            layernorm(6)
            differences(2)
            final_layer()


def layout(i):
    f = np.float32
    A = {}
    A["xT"] = i["x"].reshape(N, D).T
    c = i["ctx_1024"].transpose(2, 0, 1)
    A["ctx"] = np.tile(c, (1, 1, 8)).reshape(D, -1)

    def pack(*ws):
        return np.concatenate([w for w in ws], 1)

    for l, o in ((0, "Wp"), (1, "Wo"), (2, "Wo"), (3, "Wo")):
        A[f"wa{l}"] = pack(*(i[f"L{l}_xattn_{n}"].T for n in ("Wq", "Wk", "Wv", o)))
    A["wf1"] = pack(*(i[f"L1_ffn_{n}"].T for n in ("W_r", "W_k", "W_v")))
    A["rw0"] = pack(i["L0_ffn_router_w"], i["L2_ffn_router_w"].T, i["L3_ffn_mosa_router_w"])
    A["w1"] = i["L0_ffn_w1"].transpose(1, 0, 2).reshape(D, -1)
    A["w2"] = i["L0_ffn_w2"].reshape(E, 4, 128, D).transpose(2, 0, 1, 3).reshape(128, -1)
    A["sw13"] = pack(i["L2_ffn_sw1"], i["L2_ffn_sw3"])
    A["sw2"] = i["L2_ffn_sw2"].reshape(2, 128, D).transpose(1, 0, 2).reshape(128, -1)
    A["ew1"] = i["L2_ffn_ew1"].transpose(1, 0, 2).reshape(D, -1)
    A["ew2"] = i["L2_ffn_ew2"].transpose(1, 0, 2).reshape(128, -1)
    swapped = np.r_[ROT // 2:ROT, 0:ROT // 2]
    w = i["L3_ffn_dense_wqkv"]
    q, k, v = w[:, :, 0:HP], w[:, :, HP:2 * HP], w[:, :, 2 * HP:]
    parts = []
    for p in range(0, NHD, 2):
        parts += [q[:, p], q[:, p + 1], k[:, p], k[:, p + 1], q[:, p][:, swapped], q[:, p + 1][:, swapped],
                  k[:, p][:, swapped], k[:, p + 1][:, swapped]]
    A["wd"] = pack(*parts, v.reshape(D, -1))
    w = i["L3_ffn_mosa_wqkv"]
    q, k, v = w[:, :, 0:HP], w[:, :, HP:2 * HP], w[:, :, 2 * HP:]
    A["wm"] = pack(*(t for n in range(8) for t in (q[:, n], k[:, n], q[:, n][:, swapped], k[:, n][:, swapped], v[:, n])))
    A["wod"] = i["L3_ffn_dense_wo"].reshape(4, 128, D).transpose(1, 0, 2).reshape(128, -1)
    A["wom"] = i["L3_ffn_mosa_wo"].reshape(8, 64, D).transpose(1, 0, 2).reshape(64, -1)
    cols = np.zeros((128, COLS["_"]), f)

    def put(name, a):
        lo, hi = COLS[name]
        cols[:a.shape[0], lo:hi] = a

    put("g", np.tile(np.concatenate([i["g_xattn"], i["g_ffn"]])[None], (128, 1)))
    for n in ("lq1", "lk1", "lq2", "lk2"):
        put(n, np.tile(i["L0_xattn_" + n][None], (128, 1)))
    put("subln", np.tile(i["L0_xattn_subln_w"], 16)[:, None])
    for name, key in (("bp", "L0_xattn_bp"), ("bv2", "L2_xattn_bv"), ("bv3", "L3_xattn_bv"),
                      ("bo1", "L1_xattn_bo"), ("bo2", "L2_xattn_bo"), ("bo3", "L3_xattn_bo"),
                      ("bq1", "L1_xattn_bq"), ("mur", "L1_ffn_mu_r"), ("muk", "L1_ffn_mu_k")):
        put(name, i[key][:, None])
    for l in (2, 3):
        put(f"bq{l}", i[f"L{l}_xattn_bq"].reshape(2, 64).T)
        put(f"bk{l}", i[f"L{l}_xattn_bk"].reshape(2, 64).T)
    put("rbias", np.tile(i["L2_ffn_router_bias"][None], (128, 8)))
    A["cols"] = cols
    A["rows"] = np.concatenate([i["L1_xattn_bk"], i["L1_xattn_bv"]])[None]
    m = i["mask_1x1xSxS2_bk1"].reshape(T, SK)
    A["maskq"] = m.reshape(TB, 128, SK).transpose(1, 0, 2).reshape(128, -1)
    A["mask3"] = np.tile(i["mask_BxSx1_ik1"].reshape(1, N), (128, 1))
    A.update(constants())
    return {k_: np.ascontiguousarray(a) for k_, a in A.items()}


def kernel(**inputs):
    import concourse.bacc as _bacc
    from concourse.bass_utils import run_bass_kernel_spmd as _run

    arrays = layout({k: np.asarray(a) for k, a in inputs.items()})
    nc = _bacc.Bacc("TRN2", target_bir_lowering=False, num_devices=1)
    A = {k: nc.dram_tensor(k + "_dram", a.shape, mybir.dt.from_np(a.dtype), kind="ExternalInput").ap()
         for k, a in arrays.items()}
    out = nc.dram_tensor("out_dram", (D, N), F32, kind="ExternalOutput").ap()
    build(nc, A, out)
    r = _run(nc, [{k + "_dram": a for k, a in arrays.items()}], core_ids=[0])
    y = r.results[0]["out_dram"]
    return np.ascontiguousarray(y.T).reshape(B, T, D)
```
